# Optimizing a Trainium2 kernel written in Bass

```python
import numpy as np
import jax
import jax.numpy as jnp

def _softmax(x, axis=-1):
    return jax.nn.softmax(x, axis=axis)

def _gelu(x):
    return jax.nn.gelu(x, approximate=True)

def _silu(x):
    return jax.nn.silu(x)

def _sigmoid(x):
    return jax.nn.sigmoid(x)

def _layernorm(x, axis=-1, eps=1e-05):
    m = jnp.mean(x, axis=axis, keepdims=True)
    v = jnp.var(x, axis=axis, keepdims=True)
    return (x - m) / jnp.sqrt(v + eps)

def _scatter_add(tgt, idx, src, axis=0):
    return tgt.at[idx].add(src)

def _segment_sum(src, seg, n):
    return jax.ops.segment_sum(src, seg, n)
kernel_name = 'mk_seq_preln_d1_jaxref_r2_464dff'

def setup_inputs(seed: int=0):
    np.random.seed(seed)
    _w = jnp.asarray

    def _L0_attn_setup():
        import jax, jax.numpy as jnp
        import numpy as np
        NUM_HEAD = 16
        D_Q = 256
        D_KV = 256
        ROPE_BASE = 10000.0

        def _cos_sin(seq_len, dim):
            pos = jnp.arange(seq_len, dtype=jnp.float32)[:, None]
            ids = jnp.arange(dim // 2, dtype=jnp.float32)
            theta = ROPE_BASE ** (-2.0 * ids) / (dim // 2)
            r = pos * theta[None, :]
            return (jnp.cos(r), jnp.sin(r))

        def _rope(x, cos, sin):
            b, s, d = x.shape
            xv = x.reshape(b, s, d // 2, 2)
            x0, x1 = (xv[..., 0], xv[..., 1])
            out = jnp.stack([x0 * cos - x1 * sin, x1 * cos + x0 * sin], axis=-1)
            return out.reshape(b, s, d)
        key = jax.random.key(seed)
        ks = jax.random.split(key, 10)
        d_model, d_q, d_kv = (512, D_Q, D_KV)
        b, s = (2, 1024)
        w = lambda k, i, o: jax.random.normal(k, (i, o), dtype=jnp.float32) * 0.02
        return {'x': jax.random.normal(ks[0], (b, s, d_model), dtype=jnp.float32), 'Wd_q_w': w(ks[1], d_model, d_q), 'Wd_q_b': jnp.zeros((d_q,), jnp.float32), 'Wu_q_w': w(ks[2], d_q, d_model), 'Wu_q_b': jnp.zeros((d_model,), jnp.float32), 'Wq_r_w': w(ks[3], d_q, d_model), 'Wq_r_b': jnp.zeros((d_model,), jnp.float32), 'Wk_r_w': w(ks[4], d_model, d_model), 'Wk_r_b': jnp.zeros((d_model,), jnp.float32), 'Wd_kv_w': w(ks[5], d_model, d_kv), 'Wd_kv_b': jnp.zeros((d_kv,), jnp.float32), 'Wu_k_w': w(ks[6], d_kv, d_model), 'Wu_k_b': jnp.zeros((d_model,), jnp.float32), 'Wu_v_w': w(ks[7], d_kv, d_model), 'Wu_v_b': jnp.zeros((d_model,), jnp.float32), 'Wo_w': w(ks[8], d_model, d_model), 'Wo_b': jnp.zeros((d_model,), jnp.float32)}
    _L0_attn_in = _L0_attn_setup()

    def _L0_ffn_setup():
        import jax, jax.numpy as jnp
        import numpy as np
        DIM = 512

        def _reference_tuple_inner(x, W_r, W_k, W_v, mu_r, mu_k):
            B, T, C = x.shape
            x_prev = jnp.concatenate([jnp.zeros((B, 1, C), x.dtype), x[:, :-1, :]], axis=1)
            xr = mu_r * x + (1.0 - mu_r) * x_prev
            xk = mu_k * x + (1.0 - mu_k) * x_prev
            r = jax.nn.sigmoid(jnp.einsum('btc,dc->btd', xr, W_r))
            k = jnp.einsum('btc,dc->btd', xk, W_k)
            k_act = jnp.square(jax.nn.relu(k))
            out = r * jnp.einsum('btc,dc->btd', k_act, W_v)
            new_state = x[:, -1, :]
            return (out, new_state)
        key = jax.random.key(seed)
        ks = jax.random.split(key, 6)
        B, T, C = (8, 1024, DIM)
        x = jax.random.normal(ks[0], (B, T, C), dtype=jnp.float32)
        s = 1.0 / np.sqrt(C)
        W_r = jax.random.uniform(ks[1], (C, C), jnp.float32, -s, s)
        W_k = jax.random.uniform(ks[2], (C, C), jnp.float32, -s, s)
        W_v = jax.random.uniform(ks[3], (C, C), jnp.float32, -s, s)
        mu_r = jax.random.uniform(ks[4], (C,), jnp.float32)
        mu_k = jax.random.uniform(ks[5], (C,), jnp.float32)
        return {'x': x, 'W_r': W_r, 'W_k': W_k, 'W_v': W_v, 'mu_r': mu_r, 'mu_k': mu_k}
    _L0_ffn_in = _L0_ffn_setup()
    _d = {'L0_attn_x': _L0_attn_in['x'], 'L0_attn_Wd_q_w': _L0_attn_in['Wd_q_w'], 'L0_attn_Wd_q_b': _L0_attn_in['Wd_q_b'], 'L0_attn_Wu_q_w': _L0_attn_in['Wu_q_w'], 'L0_attn_Wu_q_b': _L0_attn_in['Wu_q_b'], 'L0_attn_Wq_r_w': _L0_attn_in['Wq_r_w'], 'L0_attn_Wq_r_b': _L0_attn_in['Wq_r_b'], 'L0_attn_Wk_r_w': _L0_attn_in['Wk_r_w'], 'L0_attn_Wk_r_b': _L0_attn_in['Wk_r_b'], 'L0_attn_Wd_kv_w': _L0_attn_in['Wd_kv_w'], 'L0_attn_Wd_kv_b': _L0_attn_in['Wd_kv_b'], 'L0_attn_Wu_k_w': _L0_attn_in['Wu_k_w'], 'L0_attn_Wu_k_b': _L0_attn_in['Wu_k_b'], 'L0_attn_Wu_v_w': _L0_attn_in['Wu_v_w'], 'L0_attn_Wu_v_b': _L0_attn_in['Wu_v_b'], 'L0_attn_Wo_w': _L0_attn_in['Wo_w'], 'L0_attn_Wo_b': _L0_attn_in['Wo_b'], 'L0_ffn_W_r': _L0_ffn_in['W_r'], 'L0_ffn_W_k': _L0_ffn_in['W_k'], 'L0_ffn_W_v': _L0_ffn_in['W_v'], 'L0_ffn_mu_r': _L0_ffn_in['mu_r'], 'L0_ffn_mu_k': _L0_ffn_in['mu_k']}
    _x0 = _d['L0_attn_x']
    _d['L0_attn_x'] = jax.random.normal(jax.random.fold_in(jax.random.key(seed), 1), (8, 1024, 512), dtype=_x0.dtype)
    del _x0
    return _d

def reference(L0_attn_x, L0_attn_Wd_q_w, L0_attn_Wd_q_b, L0_attn_Wu_q_w, L0_attn_Wu_q_b, L0_attn_Wq_r_w, L0_attn_Wq_r_b, L0_attn_Wk_r_w, L0_attn_Wk_r_b, L0_attn_Wd_kv_w, L0_attn_Wd_kv_b, L0_attn_Wu_k_w, L0_attn_Wu_k_b, L0_attn_Wu_v_w, L0_attn_Wu_v_b, L0_attn_Wo_w, L0_attn_Wo_b, L0_ffn_W_r, L0_ffn_W_k, L0_ffn_W_v, L0_ffn_mu_r, L0_ffn_mu_k):

    def _L0_attn_ref(x, Wd_q_w, Wd_q_b, Wu_q_w, Wu_q_b, Wq_r_w, Wq_r_b, Wk_r_w, Wk_r_b, Wd_kv_w, Wd_kv_b, Wu_k_w, Wu_k_b, Wu_v_w, Wu_v_b, Wo_w, Wo_b):
        import jax, jax.numpy as jnp
        import numpy as np
        NUM_HEAD = 16
        D_Q = 256
        D_KV = 256
        ROPE_BASE = 10000.0

        def _cos_sin(seq_len, dim):
            pos = jnp.arange(seq_len, dtype=jnp.float32)[:, None]
            ids = jnp.arange(dim // 2, dtype=jnp.float32)
            theta = ROPE_BASE ** (-2.0 * ids) / (dim // 2)
            r = pos * theta[None, :]
            return (jnp.cos(r), jnp.sin(r))

        def _rope(x, cos, sin):
            b, s, d = x.shape
            xv = x.reshape(b, s, d // 2, 2)
            x0, x1 = (xv[..., 0], xv[..., 1])
            out = jnp.stack([x0 * cos - x1 * sin, x1 * cos + x0 * sin], axis=-1)
            return out.reshape(b, s, d)
        b, s, d_model = x.shape
        h = NUM_HEAD
        hd = d_model // h
        scale = jnp.sqrt(jnp.float32(h + D_KV + D_Q))

        def heads(t):
            return t.reshape(b, s, h, hd).transpose(0, 2, 1, 3)
        cos, sin = _cos_sin(s, d_model)
        ct_q = x @ Wd_q_w + Wd_q_b
        qt_c = heads(ct_q @ Wu_q_w + Wu_q_b)
        qt_r = heads(_rope(ct_q @ Wq_r_w + Wq_r_b, cos, sin))
        query = qt_c + qt_r
        ct_kv = x @ Wd_kv_w + Wd_kv_b
        kt_c = heads(ct_kv @ Wu_k_w + Wu_k_b)
        kt_r = heads(_rope(x @ Wk_r_w + Wk_r_b, cos, sin))
        key = kt_c + kt_r
        value = heads(ct_kv @ Wu_v_w + Wu_v_b)
        attn = jnp.einsum('bhqd,bhkd->bhqk', query, key) / scale
        attn = jax.nn.softmax(attn, axis=-1)
        out = jnp.einsum('bhqk,bhkd->bhqd', attn, value)
        out = out.transpose(0, 2, 1, 3).reshape(b, s, d_model)
        return out @ Wo_w + Wo_b

    def _L0_ffn_ref(x, W_r, W_k, W_v, mu_r, mu_k):
        import jax, jax.numpy as jnp
        import numpy as np
        DIM = 512

        def _reference_tuple_inner(x, W_r, W_k, W_v, mu_r, mu_k):
            B, T, C = x.shape
            x_prev = jnp.concatenate([jnp.zeros((B, 1, C), x.dtype), x[:, :-1, :]], axis=1)
            xr = mu_r * x + (1.0 - mu_r) * x_prev
            xk = mu_k * x + (1.0 - mu_k) * x_prev
            r = jax.nn.sigmoid(jnp.einsum('btc,dc->btd', xr, W_r))
            k = jnp.einsum('btc,dc->btd', xk, W_k)
            k_act = jnp.square(jax.nn.relu(k))
            out = r * jnp.einsum('btc,dc->btd', k_act, W_v)
            new_state = x[:, -1, :]
            return (out, new_state)
        return _reference_tuple_inner(x, W_r, W_k, W_v, mu_r, mu_k)[0]
    x = L0_attn_x
    x = x + _L0_attn_ref(_layernorm(x, axis=-1), L0_attn_Wd_q_w, L0_attn_Wd_q_b, L0_attn_Wu_q_w, L0_attn_Wu_q_b, L0_attn_Wq_r_w, L0_attn_Wq_r_b, L0_attn_Wk_r_w, L0_attn_Wk_r_b, L0_attn_Wd_kv_w, L0_attn_Wd_kv_b, L0_attn_Wu_k_w, L0_attn_Wu_k_b, L0_attn_Wu_v_w, L0_attn_Wu_v_b, L0_attn_Wo_w, L0_attn_Wo_b)
    x = x + _L0_ffn_ref(_layernorm(x, axis=-1), L0_ffn_W_r, L0_ffn_W_k, L0_ffn_W_v, L0_ffn_mu_r, L0_ffn_mu_k)
    return x

_drawn_inputs = setup_inputs


def setup_inputs(seed=0):
    import zlib

    import numpy as np

    out = dict(_drawn_inputs(seed))
    spreads = {'L0_attn_Wd_q_b': (0.0, 0.8),
     'L0_attn_Wu_q_b': (0.0, 0.8),
     'L0_attn_Wq_r_b': (0.0, 0.8),
     'L0_attn_Wk_r_b': (0.0, 2.0),
     'L0_attn_Wd_kv_b': (0.0, 0.519),
     'L0_attn_Wu_k_b': (0.0, 2.0),
     'L0_attn_Wu_v_b': (0.0, 0.396),
     'L0_attn_Wo_b': (0.0, 0.1)}
    factors = {'L0_attn_Wd_q_w': 8.0,
     'L0_attn_Wu_q_w': 8.0,
     'L0_attn_Wq_r_w': 8.0,
     'L0_attn_Wk_r_w': 8.0,
     'L0_attn_Wd_kv_w': 8.0,
     'L0_attn_Wu_k_w': 8.0,
     'L0_attn_Wu_v_w': 3.708,
     'L0_ffn_W_r': 3.147,
     'L0_ffn_mu_r': 6.487}
    for name, (base, spread) in spreads.items():
        noise = np.random.default_rng([zlib.crc32(name.encode()), seed]).standard_normal(out[name].shape)
        drawn = base * np.exp(spread * noise) if base else spread * noise
        out[name] = jnp.asarray(drawn.astype(out[name].dtype))
    for name, factor in factors.items():
        out[name] = (out[name] * factor).astype(out[name].dtype)
    return out
```

```python
from contextlib import ExitStack

import concourse.bass as bass
from concourse import mybir

F32 = mybir.dt.float32
F32R = mybir.dt.float32r
ALU = mybir.AluOpType
ACT = mybir.ActivationFunctionType
AX = mybir.AxisListType.X

B, S, D, H = 8, 1024, 512, 16
DL = 256
HD = D // H
P = 128
FC = D // P
LC = DL // P
HG = P // HD
NG = B * FC
CH = 512
TPC = CH // P
CPB = S // CH
KT = S // P
EPS = 1e-5
SCALE = float(H + DL + DL) ** -0.5
SWAP = [i ^ 1 for i in range(32)]


def is_first(c):
    return type(c) is int and c == 0


def fold_block(nc, sem, t, w, drams):
    (wdq_d, wdkv_d, wuq_d, wqr_d, wuk_d, wuv_d, wkr_d, bdq_d, bdkv_d, buq_d, bqr_d, buk_d, bkr_d, buv_d,
     cos_d, sin_d, ident_d) = drams
    with ExitStack() as ctx:
        def sb(name, shape, dt=F32):
            return ctx.enter_context(nc.sbuf_tensor(name, shape, dt))

        wdqT = sb("wdqT", [P, LC, D])
        wdkvT = sb("wdkvT", [P, LC, D])
        wuq = sb("wuq", [P, LC, D])
        wqr = sb("wqr", [P, LC, D])
        wuk = sb("wuk", [P, LC, D])
        wuv = sb("wuv", [P, LC, D])
        wkr = sb("wkr", [P, FC, D])
        bdq = sb("bdq", [P, LC])
        bdkv = sb("bdkv", [P, LC])
        buq = sb("buq", [P, FC])
        bqr = sb("bqr", [P, FC])
        buk = sb("buk", [P, FC])
        bkr = sb("bkr", [P, FC])
        buv = sb("buv", [P, D])
        bd_cols = sb("bd_cols", [P, LC, P])
        k_full = sb("k_full", [P, 2, D + P])
        ps_a = [ctx.enter_context(nc.psum_tensor(f"fold_a{i}", [P, D], F32)) for i in range(2)]
        ps_y = [ctx.enter_context(nc.psum_tensor(f"fold_y{i}", [P, D], F32)) for i in range(2)]
        ps_b = ctx.enter_context(nc.psum_tensor("fold_bias", [P, D], F32))
        ps_v = ctx.enter_context(nc.psum_tensor("fold_vbias", [P, D], F32))

        loaded = sem("fold_loaded")
        product = sem("fold_product")
        hi_done = sem("fold_hi")
        lo_done = sem("fold_lo")
        k_sum = sem("fold_k_sum")
        bcols = sem("fold_bcols")
        bias_ps = sem("fold_bias_ps")
        bias_sb = sem("fold_bias_sb")
        block = ctx.enter_context(nc.Block())
        loads = [(wdqT, wdq_d.rearrange("(j p) n -> p j n", p=P)), (wuq, wuq_d.rearrange("(j p) n -> p j n", p=P)),
                 (wqr, wqr_d.rearrange("(j p) n -> p j n", p=P)), (wdkvT, wdkv_d.rearrange("(j p) n -> p j n", p=P)),
                 (wuk, wuk_d.rearrange("(j p) n -> p j n", p=P)), (wuv, wuv_d.rearrange("(j p) n -> p j n", p=P)),
                 (wkr, wkr_d.rearrange("(j p) n -> p j n", p=P)),
                 (t["cos"], cos_d), (t["sin"], sin_d), (t["ident"], ident_d),
                 (bdq, bdq_d), (bdkv, bdkv_d),
                 (buq, buq_d), (bqr, bqr_d),
                 (buk, buk_d), (bkr, bkr_d),
                 (buv, buv_d.rearrange("(a n) -> a n", a=1).broadcast_to([P, D]))]
        n_loads = 16 * len(loads)

        @block.sync
        def _(sp):
            for dst, src in loads:
                sp.dma_start(dst[:], src).then_inc(loaded, 16)

        @block.tensor
        def _(pe):
            pe.wait_ge(loaded, n_loads)
            for i in range(3 * FC):
                kind, c = divmod(i, FC)
                if i >= 2:
                    pe.wait_ge(lo_done, i - 1)
                a, y, cs = ps_a[i % 2], ps_y[i % 2], slice(c * P, (c + 1) * P)
                if kind == 0:
                    for j in range(LC):
                        nc.tensor.matmul(a[:, 0:P], wdqT[:, j, cs], wuq[:, j, 0:P], start=j == 0, stop=j == LC - 1)
                    for j in range(LC):
                        nc.tensor.matmul(y[:, 0:P], wdqT[:, j, cs], wqr[:, j, 0:P], start=j == 0, stop=j == LC - 1)
                    for j in range(LC):
                        nc.tensor.matmul(a[:, P:D], wdqT[:, j, cs], wuq[:, j, P:D], start=j == 0, stop=False)
                        last = nc.tensor.matmul(a[:, P:D], wdqT[:, j, cs], wqr[:, j, P:D], start=False, stop=j == LC - 1)
                else:
                    up = wuk if kind == 1 else wuv
                    for j in range(LC):
                        last = nc.tensor.matmul(a[:, :], wdkvT[:, j, cs], up[:, j, :], start=j == 0, stop=j == LC - 1)
                last.then_inc(product, 1)
            for g in range(FC):
                fs = slice(g * P, (g + 1) * P)
                for j in range(LC):
                    nc.tensor.matmul(ps_b[:, g:g + 1], wuq[:, j, fs], bdq[:, j:j + 1], start=j == 0, stop=g == 0 and j == LC - 1)
                for j in range(LC if g else 0):
                    nc.tensor.matmul(ps_b[:, g:g + 1], wqr[:, j, fs], bdq[:, j:j + 1], start=False, stop=j == LC - 1)
            for j in range(LC):
                nc.tensor.matmul(ps_b[:, FC:FC + 1], wqr[:, j, 0:P], bdq[:, j:j + 1], start=j == 0, stop=j == LC - 1)
            for g in range(FC):
                for j in range(LC):
                    nc.tensor.matmul(ps_b[:, FC + 1 + g:FC + 2 + g], wuk[:, j, g * P:(g + 1) * P], bdkv[:, j:j + 1],
                                     start=j == 0, stop=j == LC - 1)
            pe.wait_ge(bcols, LC)
            for j in range(LC):
                last = nc.tensor.matmul(ps_v[:, :], bd_cols[:, j, :], wuv[:, j, :], start=j == 0, stop=j == LC - 1)
            last.then_inc(bias_ps, 1)

        @block.scalar
        def _(act):
            for i in range(3 * FC):
                kind, c = divmod(i, FC)
                act.wait_ge(product, i + 1)
                if kind == 0:
                    nc.scalar.copy(w["q_hi"][:, c, 0:D], ps_a[i % 2][:, :])
                    nc.scalar.copy(w["q_hi"][:, c, D:D + P], ps_y[i % 2][:, 0:P]).then_inc(hi_done, 1)
                elif kind == 1:
                    act.wait_ge(k_sum, c + 1)
                    nc.scalar.copy(w["k_hi"][:, c, :], k_full[:, c % 2, :]).then_inc(hi_done, 1)
                else:
                    nc.scalar.copy(w["v_hi"][:, c, :], ps_a[i % 2][:, :]).then_inc(hi_done, 1)

        @block.vector
        def _(dve):
            dve.wait_ge(loaded, n_loads)
            nc.vector.memset(bd_cols[:], 1.0).then_inc(bias_sb, 1)
            dve.wait_ge(bias_sb, 1)
            for j in range(LC):
                nc.vector.tensor_scalar(bd_cols[:, j, :], bd_cols[:, j, :], bdkv[:, j:j + 1], None, ALU.mult).then_inc(bcols, 1)
            for i in range(3 * FC):
                kind, c = divmod(i, FC)
                a, y = ps_a[i % 2], ps_y[i % 2]
                dve.wait_ge(product, i + 1)
                if kind == 0:
                    dve.wait_ge(hi_done, i + 1)
                    nc.vector.tensor_tensor(w["q_lo"][:, c, 0:D], a[:, :], w["q_hi"][:, c, 0:D], ALU.subtract)
                    nc.vector.tensor_tensor(w["q_lo"][:, c, D:D + P], y[:, 0:P], w["q_hi"][:, c, D:D + P],
                                            ALU.subtract).then_inc(lo_done, 1)
                elif kind == 1:
                    kf = k_full[:, c % 2, :]
                    nc.vector.tensor_copy(kf[:, 0:P], a[:, 0:P])
                    nc.vector.tensor_tensor(kf[:, P:D], a[:, P:D], wkr[:, c, P:D], ALU.add)
                    nc.vector.tensor_copy(kf[:, D:D + P], wkr[:, c, 0:P]).then_inc(k_sum, 1)
                    dve.wait_ge(k_sum, c + 1)
                    dve.wait_ge(hi_done, i + 1)
                    nc.vector.tensor_tensor(w["k_lo"][:, c, :], kf, w["k_hi"][:, c, :], ALU.subtract).then_inc(lo_done, 1)
                else:
                    dve.wait_ge(hi_done, i + 1)
                    nc.vector.tensor_tensor(w["v_lo"][:, c, :], a[:, :], w["v_hi"][:, c, :], ALU.subtract).then_inc(lo_done, 1)
            dve.wait_ge(bias_ps, 1)
            nc.vector.tensor_tensor(t["bq"][:, 0:FC], ps_b[:, 0:FC], buq[:, :], ALU.add)
            nc.vector.tensor_tensor(t["bq"][:, FC:FC + 1], ps_b[:, FC:FC + 1], bqr[:, 0:1], ALU.add)
            nc.vector.tensor_tensor(t["bk"][:, 0:FC], ps_b[:, FC + 1:2 * FC + 1], buk[:, :], ALU.add)
            nc.vector.tensor_copy(t["bk"][:, FC:FC + 1], bkr[:, 0:1])
            nc.vector.tensor_tensor(t["bv"][:, :], ps_v[:, :], buv[:, :], ALU.add).then_inc(bias_sb, 1)
            dve.wait_ge(bias_sb, 2)
            nc.vector.tensor_tensor(t["bq"][:, 1:FC], t["bq"][:, 1:FC], bqr[:, 1:FC], ALU.add)
            nc.vector.tensor_tensor(t["bk"][:, 1:FC], t["bk"][:, 1:FC], bkr[:, 1:FC], ALU.add)


def project_block(nc, sem, held, t, w, x_d, scratch):
    qh_d, ql_d, kh_d, kl_d, v_d = scratch
    ITEMS = [("rot", "q"), ("rot", "k"), ("q", 1), ("q", 2), ("q", 3), ("k", 1), ("k", 2), ("k", 3),
             ("sum", "q"), ("sum", "k")] + [("v", s) for s in range(TPC)]
    NI = len(ITEMS)
    BEFORE_T = 6
    RING = 4
    STORED = 2 * FC
    with ExitStack() as ctx:
        def sb(name, shape, dt=F32):
            return ctx.enter_context(nc.sbuf_tensor(name, shape, dt))

        x_in = [sb(f"x_in{i}", [P, TPC, D]) for i in range(2)]
        xT_hi = [sb(f"xT_hi{i}", [P, FC, CH], F32R) for i in range(2)]
        xT_lo = [sb(f"xT_lo{i}", [P, FC, CH], F32R) for i in range(2)]
        stats = sb("ln_stats", [P, TPC, 6])
        mv = sb("ln_mv", [P, TPC, 2])
        rstd = sb("ln_rstd", [P, TPC])
        minus_half = sb("ln_minus_half", [P, TPC])
        y_rot = sb("y_rot", [P, 2, CH])
        y_swap = sb("y_swap", [P, 2, CH])
        y_sum = sb("y_sum", [P, 2, CH])
        g0 = sb("group0", [P, 2, CH])
        st_hi = sb("st_hi", [P, RING, CH], F32R)
        st_lo = sb("st_lo", [P, RING, CH], F32R)
        st_v = sb("st_v", [P, TPC, D])
        ps_t = [ctx.enter_context(nc.psum_tensor(f"ps_t{i}", [P, CH], F32)) for i in range(FC)]
        ps_p = [ctx.enter_context(nc.psum_tensor(f"ps_p{i}", [P, CH], F32)) for i in range(RING)]

        x_loaded = [sem(f"x_loaded{i}") for i in range(2)]
        ln_step = sem("ln_step")
        rstd_done = sem("rstd_done")
        normed = sem("normed")
        transposed = sem("transposed")
        xhi_done = sem("xhi_done")
        xlo_done = sem("xlo_done")
        proj = sem("proj")
        half_set = sem("half_set")
        rot_y = sem("rot_y")
        rot_swap = sem("rot_swap")
        rot_mul = sem("rot_mul")
        rot_sum = sem("rot_sum")
        g0_done = sem("g0_done")
        hi_done = sem("hi_done")
        lo_done = sem("lo_done")
        v_done = sem("v_done")
        stored = [sem(f"stored{i}") for i in range(RING)]
        v_stored = [sem(f"v_stored{i}") for i in range(TPC)]
        block = ctx.enter_context(nc.Block())
        x_v = x_d.rearrange("b (h s p) d -> b h p s d", h=CPB, p=P)
        last_i = B - 1

        @block.sync
        def _(sp):
            for par in range(CPB):
                sp.dma_start(x_in[par][:], x_v[0, par]).then_inc(x_loaded[par], 16)

            def body(i, last):
                for par in range(CPB):
                    c = i * CPB + par
                    if not last:
                        sp.wait_ge(transposed, c * FC + FC)
                        sp.sem_inc(held, 1)
                        sp.dma_start(x_in[par][:], x_v[i + 1, par]).then_inc(x_loaded[par], 16)
                    cs = slice(par * CH, (par + 1) * CH)
                    for n in range(STORED):
                        sp.wait_ge(lo_done, c * STORED + n + 1)
                        sp.sem_inc(held, 1)
                        g = n % 3 + 1 if n < 6 else 0
                        is_q = n < 3 or n == 6
                        dh, dl = (qh_d, ql_d) if is_q else (kh_d, kl_d)
                        sp.dma_start(dh[i, g, :, cs], st_hi[:, n % RING, :].bitcast(F32)).then_inc(stored[n % RING], 16)
                        sp.dma_start(dl[i, g, :, cs], st_lo[:, n % RING, :].bitcast(F32)).then_inc(stored[n % RING], 16)
                    for s in range(TPC):
                        sp.wait_ge(v_done, c * TPC + s + 1)
                        sp.sem_inc(held, 1)
                        sp.dma_start(v_d[i, :, :, par * TPC + s, :].rearrange("g p d -> p g d"),
                                     st_v[:, s, :].rearrange("p (g d) -> p g d", g=FC)).then_inc(v_stored[s], 16)

            body(0, False)
            with sp.Fori(1, last_i) as i:
                body(i, False)
            body(last_i, True)
            for s in stored:
                sp.wait_ge(s, 32 * B * CPB * STORED // RING)
            for s in v_stored:
                sp.wait_ge(s, 16 * B * CPB)

        @block.tensor
        def _(pe):
            def transposes(c, par):
                pe.wait_ge(normed, c + 1)
                for f in range(FC):
                    if not is_first(c):
                        pe.wait_ge(xlo_done, (c - 1) * FC + f + 1)
                    for s in range(TPC):
                        m = nc.tensor.transpose(ps_t[f][:, s * P:(s + 1) * P], x_in[par][:, s, f * P:(f + 1) * P], t["ident"][:])
                    m.then_inc(transposed, 1)

            def item(c, par, n):
                kind, g = ITEMS[n]
                slot = (par * NI + n) % RING
                if n < RING:
                    if not is_first(c):
                        pe.wait_ge(v_done, (c - 1) * TPC + n + 1)
                elif n < RING + 2:
                    pe.wait_ge(rot_y, c * 2 + n - RING + 1)
                elif n < RING + 8:
                    pe.wait_ge(lo_done, c * STORED + n - RING - 1)
                else:
                    pe.wait_ge(g0_done, c * 2 + n - RING - 7)
                out = ps_p[slot][:, :]
                hi, lo = xT_hi[par], xT_lo[par]
                if kind == "v":
                    ts_ = slice(g * P, (g + 1) * P)
                    for f in range(FC):
                        nc.tensor.matmul(out, hi[:, f, ts_], w["v_hi"][:, f, :], start=f == 0, stop=False)
                        nc.tensor.matmul(out, hi[:, f, ts_], w["v_lo"][:, f, :], start=False, stop=False)
                        m = nc.tensor.matmul(out, lo[:, f, ts_], w["v_hi"][:, f, :], start=False, stop=f == FC - 1)
                else:
                    k = g if kind in ("rot", "sum") else kind
                    blk = {"rot": FC, "sum": 0}.get(kind, g)
                    ws = slice(blk * P, (blk + 1) * P)
                    wh, wl = w[k + "_hi"], w[k + "_lo"]
                    for f in range(FC):
                        nc.tensor.matmul(out, wh[:, f, ws], hi[:, f, :], start=f == 0, stop=False)
                        nc.tensor.matmul(out, wh[:, f, ws], lo[:, f, :], start=False, stop=False)
                        m = nc.tensor.matmul(out, wl[:, f, ws], hi[:, f, :], start=False, stop=f == FC - 1)
                m.then_inc(proj, 1)

            def body(i, last):
                for par in range(CPB):
                    c = i * CPB + par
                    pe.wait_ge(xlo_done, c * FC + FC)
                    for n in range(BEFORE_T):
                        item(c, par, n)
                    if not (last and par == CPB - 1):
                        transposes(c + 1, 1 - par)
                    for n in range(BEFORE_T, NI):
                        item(c, par, n)

            transposes(0, 0)
            body(0, False)
            with pe.Fori(1, last_i) as i:
                body(i, False)
            body(last_i, True)

        @block.scalar
        def _(act):
            def x_hi(c, par):
                for f in range(FC):
                    act.wait_ge(transposed, c * FC + f + 1)
                    if f == 0 and not (type(c) is int and c < CPB):
                        act.wait_ge(proj, (c - CPB) * NI + NI)
                    nc.scalar.copy(xT_hi[par][:, f, :], ps_t[f][:, :]).then_inc(xhi_done, 1)

            def rot(c, par, n):
                act.wait_ge(proj, c * NI + n + 1)
                if not is_first(c):
                    act.wait_ge(rot_mul, (c - 1) * 2 + n + 1)
                bias = t["bq"] if n == 0 else t["bk"]
                nc.scalar.activation(y_rot[:, n, :], ps_p[(par * NI + n) % RING][:, :], ACT.Identity,
                                     bias=bias[:, FC:FC + 1]).then_inc(rot_y, 1)

            def plain(c, par, n):
                kind, g = ITEMS[n]
                act.wait_ge(proj, c * NI + n + 1)
                if n - 2 >= RING or not is_first(c):
                    act.wait_ge(stored[(n - 2) % RING], 32 * (c * (STORED // RING) + (n - 2) // RING))
                bias = t["bq"] if kind == "q" else t["bk"]
                nc.scalar.activation(st_hi[:, (n - 2) % RING, :], ps_p[(par * NI + n) % RING][:, :], ACT.Identity,
                                     bias=bias[:, g:g + 1]).then_inc(hi_done, 1)

            def body(i, last):
                for par in range(CPB):
                    c = i * CPB + par
                    rot(c, par, 0)
                    rot(c, par, 1)
                    for n in range(2, BEFORE_T):
                        plain(c, par, n)
                    if not (last and par == CPB - 1):
                        x_hi(c + 1, 1 - par)
                    for n in range(BEFORE_T, 8):
                        plain(c, par, n)
                    for k in range(2):
                        n = 6 + k
                        act.wait_ge(g0_done, c * 2 + k + 1)
                        act.wait_ge(stored[n % RING], 32 * (c * (STORED // RING) + n // RING))
                        nc.scalar.copy(st_hi[:, n % RING, :], g0[:, k, :]).then_inc(hi_done, 1)

            x_hi(0, 0)
            body(0, False)
            with act.Fori(1, last_i) as i:
                body(i, False)
            body(last_i, True)

        @block.gpsimd
        def _(pool):
            nc.gpsimd.memset(minus_half[:], -0.5).then_inc(half_set, 1)
            pool.wait_ge(half_set, 1)

            def inv_std(c):
                pool.wait_ge(ln_step, c * 3 + 3)
                nc.gpsimd.tensor_tensor(rstd[:, :], rstd[:, :], minus_half[:, :], ALU.pow).then_inc(rstd_done, 1)

            def body(i, last):
                for par in range(CPB):
                    c = i * CPB + par
                    cs = slice(par * CH, (par + 1) * CH)
                    for k in range(2):
                        pool.wait_ge(rot_swap, c * 2 + k + 1)
                        if not is_first(c):
                            pool.wait_ge(g0_done, (c - 1) * 2 + k + 1)
                        nc.gpsimd.tensor_tensor(y_sum[:, k, :], y_rot[:, k, :], t["cos"][:, cs], ALU.mult)
                        nc.gpsimd.tensor_tensor(y_swap[:, k, :], y_swap[:, k, :], t["sin"][:, cs], ALU.mult).then_inc(rot_mul, 1)
                        pool.wait_ge(rot_mul, c * 2 + k + 1)
                        nc.gpsimd.tensor_tensor(y_sum[:, k, :], y_sum[:, k, :], y_swap[:, k, :], ALU.add).then_inc(rot_sum, 1)
                    if not (last and par == CPB - 1):
                        inv_std(c + 1)

            inv_std(0)
            body(0, False)
            with pool.Fori(1, last_i) as i:
                body(i, False)
            body(last_i, True)

        @block.vector
        def _(dve):
            def norm(c, par, loads):
                dve.wait_ge(x_loaded[par], 16 * loads)
                x = x_in[par]
                for s in range(TPC):
                    v = nc.vector.bn_stats(stats[:, s, :], x[:, s, :])
                v.then_inc(ln_step, 1)
                dve.wait_ge(ln_step, c * 3 + 1)
                dve.sem_inc(held, 1)
                for s in range(TPC):
                    v = nc.vector.bn_aggr(mv[:, s, :], stats[:, s, :])
                v.then_inc(ln_step, 1)
                dve.wait_ge(ln_step, c * 3 + 2)
                nc.vector.tensor_scalar(rstd[:, :], mv[:, :, 1], EPS, None, ALU.add).then_inc(ln_step, 1)
                dve.wait_ge(rstd_done, c + 1)
                for s in range(TPC):
                    v = nc.vector.tensor_scalar(x[:, s, :], x[:, s, :], mv[:, s, 0:1], rstd[:, s:s + 1],
                                                ALU.subtract, ALU.mult)
                v.then_inc(normed, 1)

            def x_lo(c, par):
                for f in range(FC):
                    dve.wait_ge(xhi_done, c * FC + f + 1)
                    nc.vector.tensor_tensor(xT_lo[par][:, f, :], ps_t[f][:, :], xT_hi[par][:, f, :],
                                            ALU.subtract).then_inc(xlo_done, 1)

            def low(c, par, n):
                kind, g = ITEMS[n]
                bias = t["bq"] if kind == "q" else t["bk"]
                slot = (n - 2) % RING
                dve.wait_ge(hi_done, c * STORED + n - 1)
                v = nc.vector.scalar_tensor_tensor(st_lo[:, slot, :], ps_p[(par * NI + n) % RING][:, :], bias[:, g:g + 1],
                                                   st_hi[:, slot, :], ALU.add, ALU.subtract)
                v.then_inc(lo_done, 1)

            def body(i, last):
                for par in range(CPB):
                    c = i * CPB + par
                    more = not (last and par == CPB - 1)
                    for k in range(2):
                        dve.wait_ge(rot_y, c * 2 + k + 1)
                        if not is_first(c):
                            dve.wait_ge(rot_sum, (c - 1) * 2 + k + 1)
                        dve.sem_inc(held, 1)
                        nc.vector.stream_shuffle(y_swap[:, k, :], y_rot[:, k, :], SWAP).then_inc(rot_swap, 1)
                    low(c, par, 2)
                    low(c, par, 3)
                    if more:
                        norm(c + 1, 1 - par, i + 1 if par == 0 else i + 2)
                    low(c, par, 4)
                    low(c, par, 5)
                    if more:
                        x_lo(c + 1, 1 - par)
                    low(c, par, 6)
                    low(c, par, 7)
                    for k in range(2):
                        n = 8 + k
                        bias = t["bq"] if k == 0 else t["bk"]
                        dve.wait_ge(proj, c * NI + n + 1)
                        dve.wait_ge(rot_sum, c * 2 + k + 1)
                        if not is_first(c):
                            dve.wait_ge(lo_done, (c - 1) * STORED + 7 + k)
                        nc.vector.scalar_tensor_tensor(g0[:, k, :], ps_p[(par * NI + n) % RING][:, :], bias[:, 0:1],
                                                       y_sum[:, k, :], ALU.add, ALU.add).then_inc(g0_done, 1)
                    for k in range(2):
                        n = 6 + k
                        dve.wait_ge(hi_done, c * STORED + n + 1)
                        nc.vector.tensor_tensor(st_lo[:, n % RING, :], g0[:, k, :], st_hi[:, n % RING, :],
                                                ALU.subtract).then_inc(lo_done, 1)
                    for s in range(TPC):
                        n = 10 + s
                        dve.wait_ge(proj, c * NI + n + 1)
                        if not is_first(c):
                            dve.wait_ge(v_stored[s], 16 * c)
                        nc.vector.tensor_tensor(st_v[:, s, :], ps_p[(par * NI + n) % RING][:, :], t["bv"][:, :],
                                                ALU.add).then_inc(v_done, 1)

            norm(0, 0, 1)
            x_lo(0, 0)
            body(0, False)
            with dve.Fori(1, last_i) as i:
                body(i, False)
            body(last_i, True)


def attend_block(nc, sem, held, t, scratch, o_d):
    qh_d, ql_d, kh_d, kl_d, v_d = scratch
    R3 = 3
    NQ = S // CH
    UNITS = NQ * KT
    TILES = 2 * UNITS
    PR = 4
    QT = CH // P
    MAXH = 2 * HG * QT
    USES = 2 * (MAXH + 1)
    ROWS = 3 * HD
    with ExitStack() as ctx:
        def sb(name, shape, dt=F32):
            return ctx.enter_context(nc.sbuf_tensor(name, shape, dt))

        qs = [sb(f"q_stack{r}", [ROWS + 1, NQ, HG, CH], F32R) for r in range(R3)]
        ks = [sb(f"k_stack{r}", [ROWS + 1, HG, S], F32R) for r in range(R3)]
        vt = [sb(f"v_tiles{r}", [P, KT, P]) for r in range(R3)]
        probs = sb("probs", [P, PR, HG, CH])
        ones = sb("ones", [P, HD])
        part_max = sb("part_max", [P, 2, 2, HG * QT])
        row_max = sb("row_max", [P, 2, HG * QT])
        neg_max = sb("neg_max", [HG * QT, 2, P], F32R)
        recip = sb("recip", [P, CH])
        o_sb = sb("o_sb", [P, NQ, CH])
        ps_s = [ctx.enter_context(nc.psum_tensor(f"ps_s{i}", [P, 2, CH], F32)) for i in range(2)]
        ps_m = [ctx.enter_context(nc.psum_tensor(f"ps_m{i}", [P, CH], F32)) for i in range(2)]
        ps_o = ctx.enter_context(nc.psum_tensor("ps_o", [P, CH], F32))
        ps_l = ctx.enter_context(nc.psum_tensor("ps_l", [P, CH], F32))

        loaded = [sem(f"stack_loaded{r}") for r in range(R3)]
        v_loaded = [sem(f"vt_loaded{r}") for r in range(R3)]
        ones_done = sem("ones_done")
        m_scored = sem("m_scored")
        m_read = sem("m_read")
        m_rows = sem("m_rows")
        m_stacked = [sem(f"m_stacked{h}") for h in range(2)]
        scored = sem("scored")
        exped = sem("exped")
        pv_done = sem("pv_done")
        recips = sem("recips")
        o_done = sem("o_done")
        o_stored = [sem(f"o_stored{q}") for q in range(NQ)]
        block = ctx.enter_context(nc.Block())

        q_parts = [(0, qh_d), (1, ql_d), (2, qh_d)]
        k_parts = [(0, kh_d), (1, kh_d), (2, kl_d)]
        STEPS = NG // R3
        REST = NG - STEPS * R3

        def rounds(eng, step):
            for r in range(R3):
                step(0, r, r)
            with eng.Fori(1, STEPS) as i:
                for r in range(R3):
                    step(i, r, i * R3 + r)
            for r in range(REST):
                step(STEPS, r, STEPS * R3 + r)

        def is_last(n):
            return type(n) is int and n == NG - 1

        @block.sync
        def _(sp):
            def load(n, r):
                for a, (part, src) in enumerate(q_parts):
                    for qc in range(NQ):
                        sp.dma_start(qs[r][part * HD:(part + 1) * HD, qc, :, :].bitcast(F32),
                                     src[n, :, qc * CH:(qc + 1) * CH].rearrange("(a p) t -> p a t", p=HD)).then_inc(loaded[r], 16)
                for a, (part, src) in enumerate(k_parts):
                    sp.dma_start(ks[r][part * HD:(part + 1) * HD, :, :].bitcast(F32),
                                 src[n].rearrange("(a p) t -> p a t", p=HD)).then_inc(loaded[r], 16)
                sp.dma_start(vt[r][:], v_d[n]).then_inc(v_loaded[r], 16)

            def stack_max(n, r, half):
                sp.wait_ge(m_read, n * USES + (half + 1) * (MAXH + 1))
                sp.sem_inc(held, 1)
                sp.dma_start(qs[r][ROWS:ROWS + 1, half, :, :].bitcast(F32).rearrange("o a t -> o (a t)"),
                             neg_max[:, half, :].bitcast(F32)).then_inc(m_stacked[half], 16)

            def step(i, r, n):
                if not (type(n) is int and n + 2 >= NG):
                    if not is_first(n):
                        sp.wait_ge(pv_done, n * UNITS)
                        sp.sem_inc(held, 1)
                    load(n + 2, (r + 2) % R3)
                if not is_last(n):
                    stack_max(n + 1, (r + 1) % R3, 0)
                sp.wait_ge(o_done, n * NQ + 1)
                sp.sem_inc(held, 1)
                sp.dma_start(o_d[n, :, 0:CH], o_sb[:, 0, :]).then_inc(o_stored[0], 16)
                if not is_last(n):
                    stack_max(n + 1, (r + 1) % R3, 1)
                sp.wait_ge(o_done, n * NQ + 2)
                sp.sem_inc(held, 1)
                sp.dma_start(o_d[n, :, CH:S], o_sb[:, 1, :]).then_inc(o_stored[1], 16)

            load(0, 0)
            load(1, 1)
            stack_max(0, 0, 0)
            stack_max(0, 0, 1)
            rounds(sp, step)
            for s in o_stored:
                sp.wait_ge(s, 16 * NG)

        LOADS = 9

        @block.tensor
        def _(pe):
            def max_use(m, i, r, u):
                half, j = divmod(u, MAXH + 1)
                if u >= 2:
                    pe.wait_ge(m_read, m * USES + u - 1)
                elif not is_first(m):
                    pe.wait_ge(m_read, m * USES + u - 1)
                if j == MAXH:
                    pe.wait_ge(m_rows, m * 2 + half + 1)
                    nc.tensor.transpose(ps_m[u % 2][0:HG * QT, 0:P], row_max[:, half, :], t["ident"][:]).then_inc(m_scored, 1)
                    return
                if u == 0:
                    pe.wait_ge(loaded[r], 16 * LOADS * (i + 1))
                a, q, kc = j // (2 * QT), j // 2 % QT, j % 2
                nc.tensor.matmul(ps_m[u % 2][:, :], qs[r][0:ROWS, half, a, q * P:(q + 1) * P],
                                 ks[r][0:ROWS, a, kc * CH:(kc + 1) * CH], start=True, stop=True).then_inc(m_scored, 1)

            def scores(n, r, u):
                qc, kt = divmod(u, KT)
                if kt == 0:
                    pe.wait_ge(m_stacked[qc], 16 * (n + 1))
                for hp in range(2):
                    e = 2 * u + hp
                    if e >= 2:
                        pe.wait_ge(exped, n * TILES + e - 1)
                    elif not is_first(n):
                        pe.wait_ge(exped, n * TILES + e - 1)
                    for a in range(2):
                        m = nc.tensor.matmul(ps_s[hp][:, a, :], ks[r][:, 2 * hp + a, kt * P:(kt + 1) * P],
                                             qs[r][:, qc, 2 * hp + a, :], start=True, stop=True)
                    m.then_inc(scored, 1)

            def pv(n, i, r, u):
                qc, kt = divmod(u, KT)
                if u == 0:
                    pe.wait_ge(v_loaded[r], 16 * (i + 1))
                if kt == 0 and not (is_first(n) and qc == 0):
                    pe.wait_ge(o_done, n * NQ + qc)
                pe.wait_ge(exped, n * TILES + 2 * u + 2)
                for a in range(HG):
                    nc.tensor.matmul(ps_o[a * HD:(a + 1) * HD, :], vt[r][:, kt, a * HD:(a + 1) * HD],
                                     probs[:, u % PR, a, :], start=kt == 0, stop=kt == KT - 1)
                for a in range(HG):
                    m = nc.tensor.matmul(ps_l[a * HD:(a + 1) * HD, :], ones[:, :], probs[:, u % PR, a, :],
                                         start=kt == 0, stop=kt == KT - 1)
                m.then_inc(pv_done, 1)

            def step(i, r, n):
                r1 = (r + 1) % R3
                i1 = i + 1 if r1 == 0 else i
                todo = [] if is_last(n) else list(range(USES))
                for u in range(UNITS):
                    scores(n, r, u)
                    for _ in range(5 if u == UNITS // 2 else 4):
                        if todo:
                            max_use(n + 1, i1, r1, todo.pop(0))
                    if u >= 1:
                        pv(n, i, r, u - 1)
                if todo:
                    max_use(n + 1, i1, r1, todo.pop(0))
                pv(n, i, r, UNITS - 1)

            pe.wait_ge(ones_done, 1)
            for u in range(USES):
                max_use(0, 0, 0, u)
            rounds(pe, step)

        @block.scalar
        def _(act):
            def step(i, r, n):
                for e in range(TILES):
                    u, hp = divmod(e, 2)
                    if hp == 0 and (u >= PR or not is_first(n)):
                        act.wait_ge(pv_done, n * UNITS + u - PR + 1)
                    act.wait_ge(scored, n * TILES + e + 1)
                    nc.scalar.activation(probs[:, u % PR, 2 * hp:2 * hp + 2, :], ps_s[hp][:, :, :], ACT.Exp,
                                         scale=SCALE).then_inc(exped, 1)

            rounds(act, step)

        @block.vector
        def _(dve):
            for r in range(R3):
                nc.vector.memset(ks[r][ROWS:ROWS + 1, :, :].bitcast(F32), 1.0)
            nc.vector.memset(ones[:], 1.0).then_inc(ones_done, 1)

            def max_use(m, u):
                half, j = divmod(u, MAXH + 1)
                dve.wait_ge(m_scored, m * USES + u + 1)
                if j == MAXH:
                    if not is_first(m):
                        dve.wait_ge(m_stacked[half], 16 * m)
                    nc.vector.tensor_scalar(neg_max[:, half, :], ps_m[u % 2][0:HG * QT, 0:P], -1.0, None,
                                            ALU.mult).then_inc(m_read, 1)
                    return
                aq, kc = divmod(j, 2)
                nc.vector.reduce_max(part_max[:, half, kc, aq:aq + 1], ps_m[u % 2][:, :], AX).then_inc(m_read, 1)
                if j == MAXH - 1:
                    dve.wait_ge(m_read, m * USES + u + 1)
                    nc.vector.tensor_tensor(row_max[:, half, :], part_max[:, half, 0, :], part_max[:, half, 1, :],
                                            ALU.max).then_inc(m_rows, 1)

            def output(n, qc):
                dve.wait_ge(pv_done, n * UNITS + (qc + 1) * KT)
                nc.vector.reciprocal(recip[:, :], ps_l[:, :]).then_inc(recips, 1)
                dve.wait_ge(recips, n * NQ + qc + 1)
                if not is_first(n):
                    dve.wait_ge(o_stored[qc], 16 * n)
                nc.vector.tensor_tensor(o_sb[:, qc, :], ps_o[:, :], recip[:, :], ALU.mult).then_inc(o_done, 1)

            def step(i, r, n):
                todo = [] if is_last(n) else list(range(USES))
                for u in range(UNITS):
                    for _ in range(5 if u == UNITS // 2 else 4):
                        if todo:
                            max_use(n + 1, todo.pop(0))
                    if u == UNITS // 2:
                        output(n, 0)
                if todo:
                    max_use(n + 1, todo.pop(0))
                output(n, 1)

            for u in range(USES):
                max_use(0, u)
            rounds(dve, step)


def mix_block(nc, sem, held, t, x_d, o_d, wo_d, wr_d, wk_d, wv_d, bo_d, mur_d, muk_d, out_d):
    RELU = 2
    with ExitStack() as ctx:
        def sb(name, shape, dt=F32):
            return ctx.enter_context(nc.sbuf_tensor(name, shape, dt))

        w_hi = {k: sb(f"mix_w_{k}_hi", [P, FC, D], F32R) for k in "okrv"}
        w_lo = {k: sb(f"mix_w_{k}_lo", [P, FC, D], F32R) for k in "okrv"}
        bo = sb("bo", [P, D])
        mu_r = sb("mu_r", [P, FC])
        mu_k = sb("mu_k", [P, FC])
        xs = [sb(f"xs{i}", [P, TPC, D]) for i in range(2)]
        o_in = sb("o_in", [P, FC, CH])
        o_hi = sb("o_hi", [P, FC, CH], F32R)
        o_lo = sb("o_lo", [P, FC, CH], F32R)
        xn = sb("xn", [P, TPC, D])
        xT = [sb(f"xT{i}", [P, FC, CH + 1]) for i in range(2)]
        diff = sb("diff", [P, FC, CH])
        mixed = sb("mixed", [P, FC, CH])
        xk_hi = sb("xk_hi", [P, FC, CH], F32R)
        xk_lo = sb("xk_lo", [P, FC, CH], F32R)
        xr_hi = sb("xr_hi", [P, FC, CH], F32R)
        xr_lo = sb("xr_lo", [P, FC, CH], F32R)
        relu = sb("relu", [P, RELU, CH])
        ka_hi = sb("ka_hi", [P, FC, CH], F32R)
        ka_lo = sb("ka_lo", [P, FC, CH], F32R)
        gate = sb("gate", [P, TPC, D])
        stats = sb("mix_stats", [P, TPC, 6])
        mv = sb("mix_mv", [P, TPC, 2])
        rstd = sb("mix_rstd", [P, TPC])
        minus_half = sb("mix_minus_half", [P, TPC])
        ps_t = [ctx.enter_context(nc.psum_tensor(f"mix_t{i}", [P, CH], F32)) for i in range(FC)]
        ps_p = [ctx.enter_context(nc.psum_tensor(f"mix_p{i}", [P, CH], F32)) for i in range(TPC)]

        w_loaded = sem("w_loaded")
        w_split_hi = sem("w_split_hi")
        w_split_lo = sem("w_split_lo")
        x_loaded = [sem(f"mix_x_loaded{i}") for i in range(2)]
        o_loaded = sem("mix_o_loaded")
        oh_done = sem("oh_done")
        ol_done = sem("ol_done")
        xb_done = sem("xb_done")
        wo_done = sem("wo_done")
        x1_done = sem("x1_done")
        ln_step = sem("mix_ln_step")
        rstd_done = sem("mix_rstd_done")
        normed = sem("mix_normed")
        transposed = sem("mix_transposed")
        xT_done = sem("xT_done")
        half_set = sem("mix_half_set")
        zero_done = sem("zero_done")
        edge_done = sem("edge_done")
        diff_done = sem("diff_done")
        xk_done = sem("xk_done")
        xkh_done = sem("xkh_done")
        xkl_done = sem("xkl_done")
        xr_done = sem("xr_done")
        xrh_done = sem("xrh_done")
        xrl_done = sem("xrl_done")
        k_done = sem("k_done")
        relu_done = sem("relu_done")
        sq_done = sem("sq_done")
        kah_done = sem("kah_done")
        kal_done = sem("kal_done")
        r_done = sem("r_done")
        gate_done = sem("gate_done")
        v_done = sem("mix_v_done")
        gated = sem("gated")
        out_done = sem("out_done")
        out_stored = [sem(f"out_stored{i}") for i in range(2)]
        block = ctx.enter_context(nc.Block())
        x_v = x_d.rearrange("b (h s p) d -> b h p s d", h=CPB, p=P)
        out_v = out_d.rearrange("b (h s p) d -> b h p s d", h=CPB, p=P)
        o_v = o_d.rearrange("(b g) p t -> b p g t", g=FC)
        ORDER = "okrv"
        staging = {"o": xs[0], "k": xs[1], "r": diff, "v": mixed}
        last_i = B - 1

        def chunks(eng, body):
            body(0, False)
            with eng.Fori(1, last_i) as i:
                body(i, False)
            body(last_i, True)

        @block.sync
        def _(sp):
            for k, src in zip(ORDER, (wo_d, wk_d, wr_d, wv_d)):
                sp.dma_start(staging[k][:], src.rearrange("(c p) n -> p c n", p=P)).then_inc(w_loaded, 16)
            sp.dma_start(bo[:], bo_d.rearrange("(a n) -> a n", a=1).broadcast_to([P, D])).then_inc(w_loaded, 16)
            sp.dma_start(mu_r[:], mur_d).then_inc(w_loaded, 16)
            sp.dma_start(mu_k[:], muk_d).then_inc(w_loaded, 16)
            sp.dma_start(o_in[:], o_v[0, :, :, 0:CH]).then_inc(o_loaded, 16)
            sp.wait_ge(w_split_lo, 4)
            sp.sem_inc(held, 1)
            sp.dma_start(xs[0][:], x_v[0, 0]).then_inc(x_loaded[0], 16)
            sp.wait_ge(ol_done, 1)
            sp.sem_inc(held, 1)
            sp.dma_start(o_in[:], o_v[0, :, :, CH:S]).then_inc(o_loaded, 16)
            sp.dma_start(xs[1][:], x_v[0, 1]).then_inc(x_loaded[1], 16)

            def body(i, last):
                for par in range(CPB):
                    c = i * CPB + par
                    if not last:
                        sp.wait_ge(ol_done, c + 2)
                        sp.sem_inc(held, 1)
                        sp.dma_start(o_in[:], o_v[i + 1, :, :, par * CH:(par + 1) * CH]).then_inc(o_loaded, 16)
                    sp.wait_ge(out_done, c + 1)
                    sp.sem_inc(held, 1)
                    sp.dma_start(out_v[i, par], xs[par][:]).then_inc(out_stored[par], 16)
                    if not last:
                        sp.wait_ge(out_stored[par], 16 * (i + 1))
                        sp.sem_inc(held, 1)
                        sp.dma_start(xs[par][:], x_v[i + 1, par]).then_inc(x_loaded[par], 16)

            chunks(sp, body)
            for s in out_stored:
                sp.wait_ge(s, 16 * B)

        @block.tensor
        def _(pe):
            def product(out, stat_hi, stat_lo, mov_hi, mov_lo):
                for f in range(FC):
                    nc.tensor.matmul(out, stat_hi(f), mov_hi(f), start=f == 0, stop=False)
                    nc.tensor.matmul(out, stat_hi(f), mov_lo(f), start=False, stop=False)
                    m = nc.tensor.matmul(out, stat_lo(f), mov_hi(f), start=False, stop=f == FC - 1)
                return m

            def by_token(s, hi, lo, k):
                ts_ = slice(s * P, (s + 1) * P)
                return product(ps_p[s][:, :], lambda f: hi[:, f, ts_], lambda f: lo[:, f, ts_],
                               lambda f: w_hi[k][:, f, :], lambda f: w_lo[k][:, f, :])

            def project(c):
                pe.wait_ge(ol_done, c + 1)
                for s in range(TPC):
                    if type(c) is not int or c >= 2:
                        pe.wait_ge(gated, (c - 2) * TPC + s + 1)
                    by_token(s, o_hi, o_lo, "o").then_inc(wo_done, 1)

            def transposes(c):
                pe.wait_ge(normed, c + 1)
                for f in range(FC):
                    if not is_first(c):
                        pe.wait_ge(xT_done, (c - 1) * FC + f + 1)
                    for s in range(TPC):
                        m = nc.tensor.transpose(ps_t[f][:, s * P:(s + 1) * P], xn[:, s, f * P:(f + 1) * P], t["ident"][:])
                    m.then_inc(transposed, 1)

            def body(i, last):
                for par in range(CPB):
                    c = i * CPB + par
                    more = not (last and par == CPB - 1)
                    if more:
                        project(c + 1)
                    pe.wait_ge(xkl_done, c + 1)
                    for g in range(FC):
                        if more:
                            pe.wait_ge(x1_done, (c + 1) * TPC + g + 1)
                        else:
                            pe.wait_ge(gated, (c - 1) * TPC + g + 1)
                        gs = slice(g * P, (g + 1) * P)
                        product(ps_p[g][:, :], lambda f: w_hi["k"][:, f, gs], lambda f: w_lo["k"][:, f, gs],
                                lambda f: xk_hi[:, f, :], lambda f: xk_lo[:, f, :]).then_inc(k_done, 1)
                    pe.wait_ge(xrl_done, c + 1)
                    for s in range(TPC):
                        pe.wait_ge(relu_done, c * TPC + s + 1)
                        by_token(s, xr_hi, xr_lo, "r").then_inc(r_done, 1)
                    if more:
                        transposes(c + 1)
                    pe.wait_ge(kal_done, c * FC + FC)
                    for s in range(TPC):
                        pe.wait_ge(gate_done, c * TPC + s + 1)
                        by_token(s, ka_hi, ka_lo, "v").then_inc(v_done, 1)

            pe.wait_ge(w_split_lo, 4)
            project(0)
            transposes(0)
            chunks(pe, body)

        @block.scalar
        def _(act):
            for n, k in enumerate(ORDER):
                act.wait_ge(w_loaded, 16 * (len(ORDER) + 3))
                nc.scalar.copy(w_hi[k][:], staging[k][:]).then_inc(w_split_hi, 1)

            def o_high(c):
                act.wait_ge(o_loaded, 16 * (c + 1))
                if not is_first(c):
                    act.wait_ge(wo_done, c * TPC)
                nc.scalar.copy(o_hi[:], o_in[:]).then_inc(oh_done, 1)

            def x_T(c, par, batch):
                for f in range(FC):
                    act.wait_ge(transposed, c * FC + f + 1)
                    if f == 0 and (type(c) is not int or c >= 2):
                        act.wait_ge(xr_done, c - 1)
                        if par == 0:
                            act.wait_ge(edge_done, batch)
                    nc.scalar.copy(xT[par][:, f, 1:CH + 1], ps_t[f][:, :]).then_inc(xT_done, 1)

            def highs(c):
                act.wait_ge(xk_done, c + 1)
                if not is_first(c):
                    act.wait_ge(k_done, c * FC)
                nc.scalar.copy(xk_hi[:], mixed[:]).then_inc(xkh_done, 1)
                act.wait_ge(xr_done, c + 1)
                if not is_first(c):
                    act.wait_ge(r_done, c * TPC)
                nc.scalar.copy(xr_hi[:], diff[:]).then_inc(xrh_done, 1)

            def body(i, last):
                for par in range(CPB):
                    c = i * CPB + par
                    more = not (last and par == CPB - 1)

                    def square_hi(g):
                        act.wait_ge(sq_done, c * FC + g + 1)
                        if g == 0 and not is_first(c):
                            act.wait_ge(v_done, c * TPC)
                        nc.scalar.copy(ka_hi[:, g, :], relu[:, g % RELU, :]).then_inc(kah_done, 1)

                    for g in range(FC):
                        act.wait_ge(k_done, c * FC + g + 1)
                        if g >= RELU or not is_first(c):
                            act.wait_ge(kal_done, c * FC + g + 1 - RELU)
                        nc.scalar.activation(relu[:, g % RELU, :], ps_p[g][:, :], ACT.Relu).then_inc(relu_done, 1)
                        if g >= 1:
                            square_hi(g - 1)
                    square_hi(FC - 1)
                    for s in range(TPC):
                        act.wait_ge(r_done, c * TPC + s + 1)
                        if s == 0 and not is_first(c):
                            act.wait_ge(out_done, c)
                        nc.scalar.activation(gate[:, s, :], ps_p[s][:, :], ACT.Sigmoid).then_inc(gate_done, 1)
                    if more:
                        x_T(c + 1, 1 - par, i + par)
                        if not (last and par == CPB - 2):
                            o_high(c + 2)
                        highs(c + 1)

            o_high(0)
            x_T(0, 0, 0)
            o_high(1)
            highs(0)
            chunks(act, body)

        @block.gpsimd
        def _(pool):
            nc.gpsimd.memset(xT[0][:, :, 0:1], 0.0).then_inc(zero_done, 1)
            nc.gpsimd.memset(minus_half[:], -0.5).then_inc(half_set, 1)
            pool.wait_ge(half_set, 1)
            pool.wait_ge(w_loaded, 16 * (len(ORDER) + 3))

            def inv_std(c):
                pool.wait_ge(ln_step, c * 3 + 3)
                nc.gpsimd.tensor_tensor(rstd[:, :], rstd[:, :], minus_half[:, :], ALU.pow).then_inc(rstd_done, 1)

            def o_low(c, par):
                pool.wait_ge(oh_done, c + 1)
                nc.gpsimd.tensor_tensor(o_lo[:], o_in[:], o_hi[:], ALU.subtract).then_inc(ol_done, 1)

            def add_bias(i, par):
                pool.wait_ge(x_loaded[par], 16 * (i + 1))
                for s in range(TPC):
                    p_ = nc.gpsimd.tensor_tensor(xs[par][:, s, :], xs[par][:, s, :], bo[:, :], ALU.add)
                p_.then_inc(xb_done, 1)

            def edge(c):
                pool.wait_ge(xT_done, c * FC + FC)
                if not is_first(c):
                    pool.wait_ge(xr_done, c)
                pool.sem_inc(held, 1)
                nc.gpsimd.tensor_copy(xT[1][:, :, 0:1], xT[0][:, :, CH:CH + 1]).then_inc(edge_done, 1)

            def body(i, last):
                for par in range(CPB):
                    c = i * CPB + par
                    more = not (last and par == CPB - 1)
                    if more:
                        inv_std(c + 1)
                    for g in range(FC):
                        pool.wait_ge(relu_done, c * FC + g + 1)
                        nc.gpsimd.tensor_tensor(relu[:, g % RELU, :], relu[:, g % RELU, :], relu[:, g % RELU, :],
                                                ALU.mult).then_inc(sq_done, 1)
                    if more and not (last and par == CPB - 2):
                        o_low(c + 2, par)
                    if more and par == 1:
                        edge(c + 1)
                    pool.wait_ge(gated, c * TPC + TPC)
                    for s in range(TPC):
                        p_ = nc.gpsimd.tensor_tensor(xs[par][:, s, :], gate[:, s, :], xs[par][:, s, :], ALU.add)
                    p_.then_inc(out_done, 1)
                    if more and not (last and par == CPB - 2):
                        add_bias(i + 1, par)

            o_low(0, 0)
            add_bias(0, 0)
            inv_std(0)
            o_low(1, 1)
            add_bias(0, 1)
            edge(0)
            chunks(pool, body)

        @block.vector
        def _(dve):
            for n, k in enumerate(ORDER):
                dve.wait_ge(w_split_hi, n + 1)
                nc.vector.tensor_tensor(w_lo[k][:], staging[k][:], w_hi[k][:], ALU.subtract).then_inc(w_split_lo, 1)

            def norm(c, par):
                dve.wait_ge(xb_done, c + 1)
                x = xs[par]
                for s in range(TPC):
                    dve.wait_ge(wo_done, c * TPC + s + 1)
                    nc.vector.tensor_tensor(x[:, s, :], ps_p[s][:, :], x[:, s, :], ALU.add).then_inc(x1_done, 1)
                for s in range(TPC):
                    dve.wait_ge(x1_done, c * TPC + s + 1)
                    v = nc.vector.bn_stats(stats[:, s, :], x[:, s, :])
                v.then_inc(ln_step, 1)
                dve.wait_ge(ln_step, c * 3 + 1)
                dve.sem_inc(held, 1)
                for s in range(TPC):
                    v = nc.vector.bn_aggr(mv[:, s, :], stats[:, s, :])
                v.then_inc(ln_step, 1)
                dve.wait_ge(ln_step, c * 3 + 2)
                nc.vector.tensor_scalar(rstd[:, :], mv[:, :, 1], EPS, None, ALU.add).then_inc(ln_step, 1)
                dve.wait_ge(rstd_done, c + 1)
                if not is_first(c):
                    dve.wait_ge(transposed, c * FC)
                for s in range(TPC):
                    v = nc.vector.tensor_scalar(xn[:, s, :], x[:, s, :], mv[:, s, 0:1], rstd[:, s:s + 1],
                                                ALU.subtract, ALU.mult)
                v.then_inc(normed, 1)

            def shift(c, par, batch):
                dve.wait_ge(xT_done, c * FC + FC)
                if par == 0:
                    dve.wait_ge(zero_done, 1)
                else:
                    dve.wait_ge(edge_done, batch + 1)
                cur, prev = xT[par][:, :, 1:CH + 1], xT[par][:, :, 0:CH]
                nc.vector.tensor_tensor(diff[:], cur, prev, ALU.subtract).then_inc(diff_done, 1)
                dve.wait_ge(diff_done, c + 1)
                for f in range(FC):
                    v = nc.vector.scalar_tensor_tensor(mixed[:, f, :], diff[:, f, :], mu_k[:, f:f + 1], prev[:, f, :],
                                                       ALU.mult, ALU.add)
                v.then_inc(xk_done, 1)
                for f in range(FC):
                    v = nc.vector.scalar_tensor_tensor(diff[:, f, :], diff[:, f, :], mu_r[:, f:f + 1], prev[:, f, :],
                                                       ALU.mult, ALU.add)
                v.then_inc(xr_done, 1)
                dve.wait_ge(xkh_done, c + 1)
                nc.vector.tensor_tensor(xk_lo[:], mixed[:], xk_hi[:], ALU.subtract).then_inc(xkl_done, 1)
                dve.wait_ge(xrh_done, c + 1)
                nc.vector.tensor_tensor(xr_lo[:], diff[:], xr_hi[:], ALU.subtract).then_inc(xrl_done, 1)

            def body(i, last):
                for par in range(CPB):
                    c = i * CPB + par
                    more = not (last and par == CPB - 1)

                    def square_lo(g):
                        dve.wait_ge(kah_done, c * FC + g + 1)
                        nc.vector.tensor_tensor(ka_lo[:, g, :], relu[:, g % RELU, :], ka_hi[:, g, :],
                                                ALU.subtract).then_inc(kal_done, 1)

                    if more:
                        norm(c + 1, 1 - par)
                    for g in range(FC):
                        square_lo(g)
                    if more:
                        shift(c + 1, 1 - par, i if par == 0 else i + 1)
                    for s in range(TPC):
                        dve.wait_ge(v_done, c * TPC + s + 1)
                        nc.vector.tensor_tensor(gate[:, s, :], ps_p[s][:, :], gate[:, s, :], ALU.mult).then_inc(gated, 1)

            norm(0, 0)
            shift(0, 0, 0)
            chunks(dve, body)


def block_program(nc, x, wdqT, bdq, wuq, buq, wqr, bqr, wkr, bkr, wdkvT, bdkv, wuk, buk, wuv, buv, wo, bo,
                  wrT, wkT, wvT, mu_r, mu_k, cos, sin, ident, out):
    def scratch(name, shape, dt):
        return nc.dram_tensor(name, shape, dt, kind="Internal").ap()

    qk = [scratch(n, (B, FC, P, S), F32) for n in ("q_hi_scratch", "q_lo_scratch", "k_hi_scratch", "k_lo_scratch")]
    v_s = scratch("v_scratch", (B, FC, P, KT, P), F32)
    o_s = scratch("o_scratch", (NG, P, S), F32)
    with ExitStack() as ctx:
        def sem(name):
            return ctx.enter_context(nc.semaphore(name))

        held = sem("held")
        t = {"ident": ctx.enter_context(nc.sbuf_tensor("ident", [P, P], F32))}
        with ExitStack() as early:
            def sb(name, shape, dt=F32):
                return early.enter_context(nc.sbuf_tensor(name, shape, dt))

            t["cos"] = sb("cos", [P, S])
            t["sin"] = sb("sin", [P, S])
            t["bq"] = sb("bq", [P, FC + 1])
            t["bk"] = sb("bk", [P, FC + 1])
            t["bv"] = sb("bv", [P, D])
            w = {k: sb("w_" + k, [P, FC, D if k[0] == "v" else D + P], F32R)
                 for k in ("q_hi", "q_lo", "k_hi", "k_lo", "v_hi", "v_lo")}
            fold_block(nc, sem, t, w, (wdqT, wdkvT, wuq, wqr, wuk, wuv, wkr, bdq, bdkv, buq, bqr, buk, bkr, buv,
                                       cos, sin, ident))
            project_block(nc, sem, held, t, w, x, (*qk, v_s))
        grouped = [a.rearrange("b g p t -> (b g) p t") for a in qk] + [v_s.rearrange("b g p k d -> (b g) p k d")]
        attend_block(nc, sem, held, t, grouped, o_s)
        mix_block(nc, sem, held, t, x, o_s, wo, wrT, wkT, wvT, bo, mu_r, mu_k, out)


def kernel(**inputs):
    import numpy as np
    import concourse.bacc as bacc
    from concourse.bass_utils import run_bass_kernel_spmd

    def given(name):
        return np.ascontiguousarray(inputs[name])

    def turned(name):
        return np.ascontiguousarray(np.asarray(inputs[name]).T)

    def columns(name):
        return np.ascontiguousarray(np.asarray(inputs[name]).reshape(-1, P).T)

    tiny = np.finfo(np.float32).tiny
    theta = np.power(np.float32(10000.0), np.float32(-2.0) * np.arange(D // 2, dtype=np.float32)) / np.float32(D // 2)
    theta[theta < tiny] = 0.0
    assert not theta[P // 2:].any()
    angle = np.arange(S, dtype=np.float32)[None, :] * theta[:P // 2, None]
    cos = np.repeat(np.cos(angle.astype(np.float64)), 2, axis=0).astype(np.float32)
    sin = np.repeat(np.sin(angle.astype(np.float64)), 2, axis=0).astype(np.float32)
    sin[0::2] *= -1.0

    a, f = "L0_attn_", "L0_ffn_"
    arrays = {
        "x": given(a + "x"), "wdqT": turned(a + "Wd_q_w"), "bdq": columns(a + "Wd_q_b"),
        "wuq": given(a + "Wu_q_w"), "buq": columns(a + "Wu_q_b"), "wqr": given(a + "Wq_r_w"), "bqr": columns(a + "Wq_r_b"),
        "wkr": given(a + "Wk_r_w"), "bkr": columns(a + "Wk_r_b"), "wdkvT": turned(a + "Wd_kv_w"),
        "bdkv": columns(a + "Wd_kv_b"), "wuk": given(a + "Wu_k_w"), "buk": columns(a + "Wu_k_b"),
        "wuv": given(a + "Wu_v_w"), "buv": given(a + "Wu_v_b"), "wo": given(a + "Wo_w"), "bo": given(a + "Wo_b"),
        "wrT": turned(f + "W_r"), "wkT": turned(f + "W_k"), "wvT": turned(f + "W_v"),
        "mu_r": columns(f + "mu_r"), "mu_k": columns(f + "mu_k"),
        "cos": cos, "sin": sin, "ident": np.eye(P, dtype=np.float32),
    }
    nc = bacc.Bacc("TRN2", target_bir_lowering=False, num_devices=1)
    args = [nc.dram_tensor(f"in_{k}", v.shape, mybir.dt.from_np(v.dtype), kind="ExternalInput").ap()
            for k, v in arrays.items()]
    out = nc.dram_tensor("out", (B, S, D), F32, kind="ExternalOutput").ap()
    block_program(nc, *args, out)
    got = run_bass_kernel_spmd(nc, [{f"in_{k}": v for k, v in arrays.items()}], core_ids=[0])
    return got.results[0]["out"]
```

```python
from contextlib import ExitStack

import concourse.bass as bass
from concourse import mybir

F32 = mybir.dt.float32
F32R = mybir.dt.float32r
ALU = mybir.AluOpType
ACT = mybir.ActivationFunctionType
AX = mybir.AxisListType.X

B, S, D, H = 8, 1024, 512, 16
DL = 256
HD = D // H
P = 128
FC = D // P
LC = DL // P
HG = P // HD
NG = B * FC
CH = 512
TPC = CH // P
CPB = S // CH
KT = S // P
EPS = 1e-5
SCALE = float(H + DL + DL) ** -0.5
SWAP = [i ^ 1 for i in range(32)]


def is_first(c):
    return type(c) is int and c == 0


def fold_block(nc, sem, t, w, drams):
    (wdq_d, wdkv_d, wuq_d, wqr_d, wuk_d, wuv_d, wkr_d, bdq_d, bdkv_d, buq_d, bqr_d, buk_d, bkr_d, buv_d,
     cos_d, sin_d, ident_d) = drams
    with ExitStack() as ctx:
        def sb(name, shape, dt=F32):
            return ctx.enter_context(nc.sbuf_tensor(name, shape, dt))

        wdqT = sb("wdqT", [P, LC, D])
        wdkvT = sb("wdkvT", [P, LC, D])
        wuq = sb("wuq", [P, LC, D])
        wqr = sb("wqr", [P, LC, D])
        wuk = sb("wuk", [P, LC, D])
        wuv = sb("wuv", [P, LC, D])
        wkr = sb("wkr", [P, FC, D])
        bdq = sb("bdq", [P, LC])
        bdkv = sb("bdkv", [P, LC])
        buq = sb("buq", [P, FC])
        bqr = sb("bqr", [P, FC])
        buk = sb("buk", [P, FC])
        bkr = sb("bkr", [P, FC])
        buv = sb("buv", [P, D])
        bd_cols = sb("bd_cols", [P, LC, P])
        k_full = sb("k_full", [P, 2, D + P])
        ps_a = [ctx.enter_context(nc.psum_tensor(f"fold_a{i}", [P, D], F32)) for i in range(2)]
        ps_y = [ctx.enter_context(nc.psum_tensor(f"fold_y{i}", [P, D], F32)) for i in range(2)]
        ps_b = ctx.enter_context(nc.psum_tensor("fold_bias", [P, D], F32))
        ps_v = ctx.enter_context(nc.psum_tensor("fold_vbias", [P, D], F32))

        loaded = sem("fold_loaded")
        product = sem("fold_product")
        hi_done = sem("fold_hi")
        lo_done = sem("fold_lo")
        k_sum = sem("fold_k_sum")
        bcols = sem("fold_bcols")
        bias_ps = sem("fold_bias_ps")
        bias_sb = sem("fold_bias_sb")
        block = ctx.enter_context(nc.Block())
        loads = [(wdqT, wdq_d.rearrange("(j p) n -> p j n", p=P)), (wuq, wuq_d.rearrange("(j p) n -> p j n", p=P)),
                 (wqr, wqr_d.rearrange("(j p) n -> p j n", p=P)), (wdkvT, wdkv_d.rearrange("(j p) n -> p j n", p=P)),
                 (wuk, wuk_d.rearrange("(j p) n -> p j n", p=P)), (wuv, wuv_d.rearrange("(j p) n -> p j n", p=P)),
                 (wkr, wkr_d.rearrange("(j p) n -> p j n", p=P)),
                 (t["cos"], cos_d), (t["sin"], sin_d), (t["ident"], ident_d),
                 (bdq, bdq_d), (bdkv, bdkv_d),
                 (buq, buq_d), (bqr, bqr_d),
                 (buk, buk_d), (bkr, bkr_d),
                 (buv, buv_d.rearrange("(a n) -> a n", a=1).broadcast_to([P, D]))]
        n_loads = 16 * len(loads)

        @block.sync
        def _(sp):
            for dst, src in loads:
                sp.dma_start(dst[:], src).then_inc(loaded, 16)

        @block.tensor
        def _(pe):
            pe.wait_ge(loaded, n_loads)
            for i in range(3 * FC):
                kind, c = divmod(i, FC)
                if i >= 2:
                    pe.wait_ge(lo_done, i - 1)
                a, y, cs = ps_a[i % 2], ps_y[i % 2], slice(c * P, (c + 1) * P)
                if kind == 0:
                    for j in range(LC):
                        nc.tensor.matmul(a[:, 0:P], wdqT[:, j, cs], wuq[:, j, 0:P], start=j == 0, stop=j == LC - 1)
                    for j in range(LC):
                        nc.tensor.matmul(y[:, 0:P], wdqT[:, j, cs], wqr[:, j, 0:P], start=j == 0, stop=j == LC - 1)
                    for j in range(LC):
                        nc.tensor.matmul(a[:, P:D], wdqT[:, j, cs], wuq[:, j, P:D], start=j == 0, stop=False)
                        last = nc.tensor.matmul(a[:, P:D], wdqT[:, j, cs], wqr[:, j, P:D], start=False, stop=j == LC - 1)
                else:
                    up = wuk if kind == 1 else wuv
                    for j in range(LC):
                        last = nc.tensor.matmul(a[:, :], wdkvT[:, j, cs], up[:, j, :], start=j == 0, stop=j == LC - 1)
                last.then_inc(product, 1)
            for g in range(FC):
                fs = slice(g * P, (g + 1) * P)
                for j in range(LC):
                    nc.tensor.matmul(ps_b[:, g:g + 1], wuq[:, j, fs], bdq[:, j:j + 1], start=j == 0, stop=g == 0 and j == LC - 1)
                for j in range(LC if g else 0):
                    nc.tensor.matmul(ps_b[:, g:g + 1], wqr[:, j, fs], bdq[:, j:j + 1], start=False, stop=j == LC - 1)
            for j in range(LC):
                nc.tensor.matmul(ps_b[:, FC:FC + 1], wqr[:, j, 0:P], bdq[:, j:j + 1], start=j == 0, stop=j == LC - 1)
            for g in range(FC):
                for j in range(LC):
                    nc.tensor.matmul(ps_b[:, FC + 1 + g:FC + 2 + g], wuk[:, j, g * P:(g + 1) * P], bdkv[:, j:j + 1],
                                     start=j == 0, stop=j == LC - 1)
            pe.wait_ge(bcols, LC)
            for j in range(LC):
                last = nc.tensor.matmul(ps_v[:, :], bd_cols[:, j, :], wuv[:, j, :], start=j == 0, stop=j == LC - 1)
            last.then_inc(bias_ps, 1)

        @block.scalar
        def _(act):
            for i in range(3 * FC):
                kind, c = divmod(i, FC)
                act.wait_ge(product, i + 1)
                if kind == 0:
                    nc.scalar.copy(w["q_hi"][:, c, 0:D], ps_a[i % 2][:, :])
                    nc.scalar.copy(w["q_hi"][:, c, D:D + P], ps_y[i % 2][:, 0:P]).then_inc(hi_done, 1)
                elif kind == 1:
                    act.wait_ge(k_sum, c + 1)
                    nc.scalar.copy(w["k_hi"][:, c, :], k_full[:, c % 2, :]).then_inc(hi_done, 1)
                else:
                    nc.scalar.copy(w["v_hi"][:, c, :], ps_a[i % 2][:, :]).then_inc(hi_done, 1)

        @block.vector
        def _(dve):
            dve.wait_ge(loaded, n_loads)
            nc.vector.memset(bd_cols[:], 1.0).then_inc(bias_sb, 1)
            dve.wait_ge(bias_sb, 1)
            for j in range(LC):
                nc.vector.tensor_scalar(bd_cols[:, j, :], bd_cols[:, j, :], bdkv[:, j:j + 1], None, ALU.mult).then_inc(bcols, 1)
            for i in range(3 * FC):
                kind, c = divmod(i, FC)
                a, y = ps_a[i % 2], ps_y[i % 2]
                dve.wait_ge(product, i + 1)
                if kind == 0:
                    dve.wait_ge(hi_done, i + 1)
                    nc.vector.tensor_tensor(w["q_lo"][:, c, 0:D], a[:, :], w["q_hi"][:, c, 0:D], ALU.subtract)
                    nc.vector.tensor_tensor(w["q_lo"][:, c, D:D + P], y[:, 0:P], w["q_hi"][:, c, D:D + P],
                                            ALU.subtract).then_inc(lo_done, 1)
                elif kind == 1:
                    kf = k_full[:, c % 2, :]
                    nc.vector.tensor_copy(kf[:, 0:P], a[:, 0:P])
                    nc.vector.tensor_tensor(kf[:, P:D], a[:, P:D], wkr[:, c, P:D], ALU.add)
                    nc.vector.tensor_copy(kf[:, D:D + P], wkr[:, c, 0:P]).then_inc(k_sum, 1)
                    dve.wait_ge(k_sum, c + 1)
                    dve.wait_ge(hi_done, i + 1)
                    nc.vector.tensor_tensor(w["k_lo"][:, c, :], kf, w["k_hi"][:, c, :], ALU.subtract).then_inc(lo_done, 1)
                else:
                    dve.wait_ge(hi_done, i + 1)
                    nc.vector.tensor_tensor(w["v_lo"][:, c, :], a[:, :], w["v_hi"][:, c, :], ALU.subtract).then_inc(lo_done, 1)
            dve.wait_ge(bias_ps, 1)
            nc.vector.tensor_tensor(t["bq"][:, 0:FC], ps_b[:, 0:FC], buq[:, :], ALU.add)
            nc.vector.tensor_tensor(t["bq"][:, FC:FC + 1], ps_b[:, FC:FC + 1], bqr[:, 0:1], ALU.add)
            nc.vector.tensor_tensor(t["bk"][:, 0:FC], ps_b[:, FC + 1:2 * FC + 1], buk[:, :], ALU.add)
            nc.vector.tensor_copy(t["bk"][:, FC:FC + 1], bkr[:, 0:1])
            nc.vector.tensor_tensor(t["bv"][:, :], ps_v[:, :], buv[:, :], ALU.add).then_inc(bias_sb, 1)
            dve.wait_ge(bias_sb, 2)
            nc.vector.tensor_tensor(t["bq"][:, 1:FC], t["bq"][:, 1:FC], bqr[:, 1:FC], ALU.add)
            nc.vector.tensor_tensor(t["bk"][:, 1:FC], t["bk"][:, 1:FC], bkr[:, 1:FC], ALU.add)


def project_block(nc, sem, held, t, w, x_d, scratch):
    qh_d, ql_d, kh_d, kl_d, v_d = scratch
    ITEMS = [("rot", "q"), ("rot", "k"), ("q", 1), ("q", 2), ("q", 3), ("k", 1), ("k", 2), ("k", 3),
             ("sum", "q"), ("sum", "k")] + [("v", s) for s in range(TPC)]
    NI = len(ITEMS)
    BEFORE_T = 6
    RING = 4
    STORED = 2 * FC
    with ExitStack() as ctx:
        def sb(name, shape, dt=F32):
            return ctx.enter_context(nc.sbuf_tensor(name, shape, dt))

        x_in = [sb(f"x_in{i}", [P, TPC, D]) for i in range(2)]
        xT_hi = [sb(f"xT_hi{i}", [P, FC, CH], F32R) for i in range(2)]
        xT_lo = [sb(f"xT_lo{i}", [P, FC, CH], F32R) for i in range(2)]
        stats = sb("ln_stats", [P, TPC, 6])
        mv = sb("ln_mv", [P, TPC, 2])
        rstd = sb("ln_rstd", [P, TPC])
        minus_half = sb("ln_minus_half", [P, TPC])
        y_rot = sb("y_rot", [P, 2, CH])
        y_swap = sb("y_swap", [P, 2, CH])
        y_sum = sb("y_sum", [P, 2, CH])
        g0 = sb("group0", [P, 2, CH])
        st_hi = sb("st_hi", [P, RING, CH], F32R)
        st_lo = sb("st_lo", [P, RING, CH], F32R)
        st_v = sb("st_v", [P, TPC, D])
        ps_t = [ctx.enter_context(nc.psum_tensor(f"ps_t{i}", [P, CH], F32)) for i in range(FC)]
        ps_p = [ctx.enter_context(nc.psum_tensor(f"ps_p{i}", [P, CH], F32)) for i in range(RING)]

        x_loaded = [sem(f"x_loaded{i}") for i in range(2)]
        ln_step = sem("ln_step")
        rstd_done = sem("rstd_done")
        normed = sem("normed")
        transposed = sem("transposed")
        xhi_done = sem("xhi_done")
        xlo_done = sem("xlo_done")
        proj = sem("proj")
        half_set = sem("half_set")
        rot_y = sem("rot_y")
        rot_swap = sem("rot_swap")
        rot_mul = sem("rot_mul")
        rot_sum = sem("rot_sum")
        g0_done = sem("g0_done")
        hi_done = sem("hi_done")
        lo_done = sem("lo_done")
        v_done = sem("v_done")
        stored = [sem(f"stored{i}") for i in range(RING)]
        v_stored = [sem(f"v_stored{i}") for i in range(TPC)]
        block = ctx.enter_context(nc.Block())
        x_v = x_d.rearrange("b (h s p) d -> b h p s d", h=CPB, p=P)
        last_i = B - 1

        @block.sync
        def _(sp):
            for par in range(CPB):
                sp.dma_start(x_in[par][:], x_v[0, par]).then_inc(x_loaded[par], 16)

            def body(i, last):
                for par in range(CPB):
                    c = i * CPB + par
                    if not last:
                        sp.wait_ge(transposed, c * FC + FC)
                        sp.sem_inc(held, 1)
                        sp.dma_start(x_in[par][:], x_v[i + 1, par]).then_inc(x_loaded[par], 16)
                    cs = slice(par * CH, (par + 1) * CH)
                    for n in range(STORED):
                        sp.wait_ge(lo_done, c * STORED + n + 1)
                        sp.sem_inc(held, 1)
                        g = n % 3 + 1 if n < 6 else 0
                        is_q = n < 3 or n == 6
                        dh, dl = (qh_d, ql_d) if is_q else (kh_d, kl_d)
                        sp.dma_start(dh[i, g, :, cs], st_hi[:, n % RING, :].bitcast(F32)).then_inc(stored[n % RING], 16)
                        sp.dma_start(dl[i, g, :, cs], st_lo[:, n % RING, :].bitcast(F32)).then_inc(stored[n % RING], 16)
                    for s in range(TPC):
                        sp.wait_ge(v_done, c * TPC + s + 1)
                        sp.sem_inc(held, 1)
                        sp.dma_start(v_d[i, :, :, par * TPC + s, :].rearrange("g p d -> p g d"),
                                     st_v[:, s, :].rearrange("p (g d) -> p g d", g=FC)).then_inc(v_stored[s], 16)

            body(0, False)
            with sp.Fori(1, last_i) as i:
                body(i, False)
            body(last_i, True)
            for s in stored:
                sp.wait_ge(s, 32 * B * CPB * STORED // RING)
            for s in v_stored:
                sp.wait_ge(s, 16 * B * CPB)

        @block.tensor
        def _(pe):
            def transposes(c, par):
                pe.wait_ge(normed, c + 1)
                for f in range(FC):
                    if not is_first(c):
                        pe.wait_ge(xlo_done, (c - 1) * FC + f + 1)
                    for s in range(TPC):
                        m = nc.tensor.transpose(ps_t[f][:, s * P:(s + 1) * P], x_in[par][:, s, f * P:(f + 1) * P], t["ident"][:])
                    m.then_inc(transposed, 1)

            def item(c, par, n):
                kind, g = ITEMS[n]
                slot = (par * NI + n) % RING
                if n < RING:
                    if not is_first(c):
                        pe.wait_ge(v_done, (c - 1) * TPC + n + 1)
                elif n < RING + 2:
                    pe.wait_ge(rot_y, c * 2 + n - RING + 1)
                elif n < RING + 8:
                    pe.wait_ge(lo_done, c * STORED + n - RING - 1)
                else:
                    pe.wait_ge(g0_done, c * 2 + n - RING - 7)
                out = ps_p[slot][:, :]
                hi, lo = xT_hi[par], xT_lo[par]
                if kind == "v":
                    ts_ = slice(g * P, (g + 1) * P)
                    for f in range(FC):
                        nc.tensor.matmul(out, hi[:, f, ts_], w["v_hi"][:, f, :], start=f == 0, stop=False)
                        nc.tensor.matmul(out, hi[:, f, ts_], w["v_lo"][:, f, :], start=False, stop=False)
                        m = nc.tensor.matmul(out, lo[:, f, ts_], w["v_hi"][:, f, :], start=False, stop=f == FC - 1)
                else:
                    k = g if kind in ("rot", "sum") else kind
                    blk = {"rot": FC, "sum": 0}.get(kind, g)
                    ws = slice(blk * P, (blk + 1) * P)
                    wh, wl = w[k + "_hi"], w[k + "_lo"]
                    for f in range(FC):
                        nc.tensor.matmul(out, wh[:, f, ws], hi[:, f, :], start=f == 0, stop=False)
                        nc.tensor.matmul(out, wh[:, f, ws], lo[:, f, :], start=False, stop=False)
                        m = nc.tensor.matmul(out, wl[:, f, ws], hi[:, f, :], start=False, stop=f == FC - 1)
                m.then_inc(proj, 1)

            def body(i, last):
                for par in range(CPB):
                    c = i * CPB + par
                    pe.wait_ge(xlo_done, c * FC + FC)
                    for n in range(BEFORE_T):
                        item(c, par, n)
                    if not (last and par == CPB - 1):
                        transposes(c + 1, 1 - par)
                    for n in range(BEFORE_T, NI):
                        item(c, par, n)

            transposes(0, 0)
            body(0, False)
            with pe.Fori(1, last_i) as i:
                body(i, False)
            body(last_i, True)

        @block.scalar
        def _(act):
            def x_hi(c, par):
                for f in range(FC):
                    act.wait_ge(transposed, c * FC + f + 1)
                    if f == 0 and not (type(c) is int and c < CPB):
                        act.wait_ge(proj, (c - CPB) * NI + NI)
                    nc.scalar.copy(xT_hi[par][:, f, :], ps_t[f][:, :]).then_inc(xhi_done, 1)

            def rot(c, par, n):
                act.wait_ge(proj, c * NI + n + 1)
                if not is_first(c):
                    act.wait_ge(rot_mul, (c - 1) * 2 + n + 1)
                bias = t["bq"] if n == 0 else t["bk"]
                nc.scalar.activation(y_rot[:, n, :], ps_p[(par * NI + n) % RING][:, :], ACT.Identity,
                                     bias=bias[:, FC:FC + 1]).then_inc(rot_y, 1)

            def plain(c, par, n):
                kind, g = ITEMS[n]
                act.wait_ge(proj, c * NI + n + 1)
                if n - 2 >= RING or not is_first(c):
                    act.wait_ge(stored[(n - 2) % RING], 32 * (c * (STORED // RING) + (n - 2) // RING))
                bias = t["bq"] if kind == "q" else t["bk"]
                nc.scalar.activation(st_hi[:, (n - 2) % RING, :], ps_p[(par * NI + n) % RING][:, :], ACT.Identity,
                                     bias=bias[:, g:g + 1]).then_inc(hi_done, 1)

            def body(i, last):
                for par in range(CPB):
                    c = i * CPB + par
                    rot(c, par, 0)
                    rot(c, par, 1)
                    for n in range(2, BEFORE_T):
                        plain(c, par, n)
                    if not (last and par == CPB - 1):
                        x_hi(c + 1, 1 - par)
                    for n in range(BEFORE_T, 8):
                        plain(c, par, n)
                    for k in range(2):
                        n = 6 + k
                        act.wait_ge(g0_done, c * 2 + k + 1)
                        act.wait_ge(stored[n % RING], 32 * (c * (STORED // RING) + n // RING))
                        nc.scalar.copy(st_hi[:, n % RING, :], g0[:, k, :]).then_inc(hi_done, 1)

            x_hi(0, 0)
            body(0, False)
            with act.Fori(1, last_i) as i:
                body(i, False)
            body(last_i, True)

        @block.gpsimd
        def _(pool):
            nc.gpsimd.memset(minus_half[:], -0.5).then_inc(half_set, 1)
            pool.wait_ge(half_set, 1)

            def inv_std(c):
                pool.wait_ge(ln_step, c * 3 + 3)
                nc.gpsimd.tensor_tensor(rstd[:, :], rstd[:, :], minus_half[:, :], ALU.pow).then_inc(rstd_done, 1)

            def body(i, last):
                for par in range(CPB):
                    c = i * CPB + par
                    cs = slice(par * CH, (par + 1) * CH)
                    for k in range(2):
                        pool.wait_ge(rot_swap, c * 2 + k + 1)
                        if not is_first(c):
                            pool.wait_ge(g0_done, (c - 1) * 2 + k + 1)
                        nc.gpsimd.tensor_tensor(y_sum[:, k, :], y_rot[:, k, :], t["cos"][:, cs], ALU.mult)
                        nc.gpsimd.tensor_tensor(y_swap[:, k, :], y_swap[:, k, :], t["sin"][:, cs], ALU.mult).then_inc(rot_mul, 1)
                        pool.wait_ge(rot_mul, c * 2 + k + 1)
                        nc.gpsimd.tensor_tensor(y_sum[:, k, :], y_sum[:, k, :], y_swap[:, k, :], ALU.add).then_inc(rot_sum, 1)
                    if not (last and par == CPB - 1):
                        inv_std(c + 1)

            inv_std(0)
            body(0, False)
            with pool.Fori(1, last_i) as i:
                body(i, False)
            body(last_i, True)

        @block.vector
        def _(dve):
            def norm(c, par, loads):
                dve.wait_ge(x_loaded[par], 16 * loads)
                x = x_in[par]
                for s in range(TPC):
                    v = nc.vector.bn_stats(stats[:, s, :], x[:, s, :])
                v.then_inc(ln_step, 1)
                dve.wait_ge(ln_step, c * 3 + 1)
                dve.sem_inc(held, 1)
                for s in range(TPC):
                    v = nc.vector.bn_aggr(mv[:, s, :], stats[:, s, :])
                v.then_inc(ln_step, 1)
                dve.wait_ge(ln_step, c * 3 + 2)
                nc.vector.tensor_scalar(rstd[:, :], mv[:, :, 1], EPS, None, ALU.add).then_inc(ln_step, 1)
                dve.wait_ge(rstd_done, c + 1)
                for s in range(TPC):
                    v = nc.vector.tensor_scalar(x[:, s, :], x[:, s, :], mv[:, s, 0:1], rstd[:, s:s + 1],
                                                ALU.subtract, ALU.mult)
                v.then_inc(normed, 1)

            def x_lo(c, par):
                for f in range(FC):
                    dve.wait_ge(xhi_done, c * FC + f + 1)
                    nc.vector.tensor_tensor(xT_lo[par][:, f, :], ps_t[f][:, :], xT_hi[par][:, f, :],
                                            ALU.subtract).then_inc(xlo_done, 1)

            def low(c, par, n):
                kind, g = ITEMS[n]
                bias = t["bq"] if kind == "q" else t["bk"]
                slot = (n - 2) % RING
                dve.wait_ge(hi_done, c * STORED + n - 1)
                v = nc.vector.scalar_tensor_tensor(st_lo[:, slot, :], ps_p[(par * NI + n) % RING][:, :], bias[:, g:g + 1],
                                                   st_hi[:, slot, :], ALU.add, ALU.subtract)
                v.then_inc(lo_done, 1)

            def body(i, last):
                for par in range(CPB):
                    c = i * CPB + par
                    more = not (last and par == CPB - 1)
                    for k in range(2):
                        dve.wait_ge(rot_y, c * 2 + k + 1)
                        if not is_first(c):
                            dve.wait_ge(rot_sum, (c - 1) * 2 + k + 1)
                        dve.sem_inc(held, 1)
                        nc.vector.stream_shuffle(y_swap[:, k, :], y_rot[:, k, :], SWAP).then_inc(rot_swap, 1)
                    low(c, par, 2)
                    low(c, par, 3)
                    if more:
                        norm(c + 1, 1 - par, i + 1 if par == 0 else i + 2)
                    low(c, par, 4)
                    low(c, par, 5)
                    if more:
                        x_lo(c + 1, 1 - par)
                    low(c, par, 6)
                    low(c, par, 7)
                    for k in range(2):
                        n = 8 + k
                        bias = t["bq"] if k == 0 else t["bk"]
                        dve.wait_ge(proj, c * NI + n + 1)
                        dve.wait_ge(rot_sum, c * 2 + k + 1)
                        if not is_first(c):
                            dve.wait_ge(lo_done, (c - 1) * STORED + 7 + k)
                        nc.vector.scalar_tensor_tensor(g0[:, k, :], ps_p[(par * NI + n) % RING][:, :], bias[:, 0:1],
                                                       y_sum[:, k, :], ALU.add, ALU.add).then_inc(g0_done, 1)
                    for k in range(2):
                        n = 6 + k
                        dve.wait_ge(hi_done, c * STORED + n + 1)
                        nc.vector.tensor_tensor(st_lo[:, n % RING, :], g0[:, k, :], st_hi[:, n % RING, :],
                                                ALU.subtract).then_inc(lo_done, 1)
                    for s in range(TPC):
                        n = 10 + s
                        dve.wait_ge(proj, c * NI + n + 1)
                        if not is_first(c):
                            dve.wait_ge(v_stored[s], 16 * c)
                        nc.vector.tensor_tensor(st_v[:, s, :], ps_p[(par * NI + n) % RING][:, :], t["bv"][:, :],
                                                ALU.add).then_inc(v_done, 1)

            norm(0, 0, 1)
            x_lo(0, 0)
            body(0, False)
            with dve.Fori(1, last_i) as i:
                body(i, False)
            body(last_i, True)


def attend_block(nc, sem, held, t, scratch, o_d, l_d):
    qh_d, ql_d, kh_d, kl_d, v_d = scratch
    R3 = 3
    NQ = S // CH
    UNITS = NQ * KT
    TILES = 2 * UNITS
    PR = 4
    PAIRS = UNITS // 2
    PAIR_LAG = 4
    QT = CH // P
    MAXH = 2 * HG * QT
    USES = 2 * (MAXH + 1)
    ROWS = 3 * HD
    with ExitStack() as ctx:
        def sb(name, shape, dt=F32):
            return ctx.enter_context(nc.sbuf_tensor(name, shape, dt))

        qs = [sb(f"q_stack{r}", [ROWS + 1, NQ, HG, CH], F32R) for r in range(R3)]
        ks = [sb(f"k_stack{r}", [ROWS + 1, HG, S], F32R) for r in range(R3)]
        vt = [sb(f"v_tiles{r}", [P, KT, P]) for r in range(R3)]
        probs = sb("probs", [P, PR, HG, CH])
        ones = sb("ones", [P, HD])
        part_max = sb("part_max", [P, 2, 2, HG * QT])
        row_max = sb("row_max", [P, 2, HG * QT])
        neg_max = sb("neg_max", [HG * QT, 2, P], F32R)
        pairs = sb("pairs", [P, 2, HG, CH])
        o_sb = sb("o_sb", [P, NQ, CH])
        l_sb = sb("l_sb", [P, NQ, CH])
        ps_s = [ctx.enter_context(nc.psum_tensor(f"ps_s{i}", [P, 2, CH], F32)) for i in range(2)]
        ps_m = [ctx.enter_context(nc.psum_tensor(f"ps_m{i}", [P, CH], F32)) for i in range(2)]
        ps_o = ctx.enter_context(nc.psum_tensor("ps_o", [P, CH], F32))
        ps_l = ctx.enter_context(nc.psum_tensor("ps_l", [P, CH], F32))

        loaded = [sem(f"stack_loaded{r}") for r in range(R3)]
        v_loaded = [sem(f"vt_loaded{r}") for r in range(R3)]
        ones_done = sem("ones_done")
        m_scored = sem("m_scored")
        m_read = sem("m_read")
        m_rows = sem("m_rows")
        m_stacked = [sem(f"m_stacked{h}") for h in range(2)]
        scored = sem("scored")
        exped = sem("exped")
        pv_done = sem("pv_done")
        pair_done = sem("pair_done")
        sum_done = sem("sum_done")
        o_out = sem("o_out")
        l_out = sem("l_out")
        o_stored = [sem(f"o_stored{q}") for q in range(NQ)]
        l_stored = [sem(f"l_stored{q}") for q in range(NQ)]
        block = ctx.enter_context(nc.Block())

        q_parts = [(0, qh_d), (1, ql_d), (2, qh_d)]
        k_parts = [(0, kh_d), (1, kh_d), (2, kl_d)]
        STEPS = NG // R3
        REST = NG - STEPS * R3

        def rounds(eng, step):
            for r in range(R3):
                step(0, r, r)
            with eng.Fori(1, STEPS) as i:
                for r in range(R3):
                    step(i, r, i * R3 + r)
            for r in range(REST):
                step(STEPS, r, STEPS * R3 + r)

        def is_last(n):
            return type(n) is int and n == NG - 1

        @block.sync
        def _(sp):
            def load(n, r):
                for a, (part, src) in enumerate(q_parts):
                    for qc in range(NQ):
                        sp.dma_start(qs[r][part * HD:(part + 1) * HD, qc, :, :].bitcast(F32),
                                     src[n, :, qc * CH:(qc + 1) * CH].rearrange("(a p) t -> p a t", p=HD)).then_inc(loaded[r], 16)
                for a, (part, src) in enumerate(k_parts):
                    sp.dma_start(ks[r][part * HD:(part + 1) * HD, :, :].bitcast(F32),
                                 src[n].rearrange("(a p) t -> p a t", p=HD)).then_inc(loaded[r], 16)
                sp.dma_start(vt[r][:], v_d[n]).then_inc(v_loaded[r], 16)

            def stack_max(n, r, half):
                sp.wait_ge(m_read, n * USES + (half + 1) * (MAXH + 1))
                sp.sem_inc(held, 1)
                sp.dma_start(qs[r][ROWS:ROWS + 1, half, :, :].bitcast(F32).rearrange("o a t -> o (a t)"),
                             neg_max[:, half, :].bitcast(F32)).then_inc(m_stacked[half], 16)

            def store_o(n, qc):
                sp.wait_ge(o_out, n * NQ + qc + 1)
                sp.sem_inc(held, 1)
                sp.dma_start(o_d[n, :, qc * CH:(qc + 1) * CH], o_sb[:, qc, :]).then_inc(o_stored[qc], 16)

            def store_l(n, qc):
                sp.wait_ge(l_out, n * NQ + qc + 1)
                sp.sem_inc(held, 1)
                sp.dma_start(l_d[n, :, qc * CH:(qc + 1) * CH], l_sb[0:P - HD + 1:HD, qc, :]).then_inc(l_stored[qc], 16)

            def step(i, r, n):
                if not (type(n) is int and n + 2 >= NG):
                    if not is_first(n):
                        sp.wait_ge(pv_done, n * UNITS)
                        sp.sem_inc(held, 1)
                    load(n + 2, (r + 2) % R3)
                if not is_first(n):
                    store_o(n - 1, 1)
                    store_l(n - 1, 1)
                if not is_last(n):
                    stack_max(n + 1, (r + 1) % R3, 0)
                store_o(n, 0)
                store_l(n, 0)
                if not is_last(n):
                    stack_max(n + 1, (r + 1) % R3, 1)

            load(0, 0)
            load(1, 1)
            stack_max(0, 0, 0)
            stack_max(0, 0, 1)
            rounds(sp, step)
            store_o(NG - 1, 1)
            store_l(NG - 1, 1)
            for s in o_stored + l_stored:
                sp.wait_ge(s, 16 * NG)

        LOADS = 9

        @block.tensor
        def _(pe):
            def max_use(m, i, r, u):
                half, j = divmod(u, MAXH + 1)
                if u >= 2:
                    pe.wait_ge(m_read, m * USES + u - 1)
                elif not is_first(m):
                    pe.wait_ge(m_read, m * USES + u - 1)
                if j == MAXH:
                    pe.wait_ge(m_rows, m * 2 + half + 1)
                    nc.tensor.transpose(ps_m[u % 2][0:HG * QT, 0:P], row_max[:, half, :], t["ident"][:]).then_inc(m_scored, 1)
                    return
                if u == 0:
                    pe.wait_ge(loaded[r], 16 * LOADS * (i + 1))
                a, q, kc = j // (2 * QT), j // 2 % QT, j % 2
                nc.tensor.matmul(ps_m[u % 2][:, :], qs[r][0:ROWS, half, a, q * P:(q + 1) * P],
                                 ks[r][0:ROWS, a, kc * CH:(kc + 1) * CH], start=True, stop=True).then_inc(m_scored, 1)

            def scores(n, r, u, hp):
                qc, kt = divmod(u, KT)
                e = 2 * u + hp
                if kt == 0 and hp == 0:
                    pe.wait_ge(m_stacked[qc], 16 * (n + 1))
                if e >= 2 or not is_first(n):
                    pe.wait_ge(exped, n * TILES + e - 1)
                for a in range(2):
                    m = nc.tensor.matmul(ps_s[hp][:, a, :], ks[r][:, 2 * hp + a, kt * P:(kt + 1) * P],
                                         qs[r][:, qc, 2 * hp + a, :], start=True, stop=True)
                m.then_inc(scored, 1)

            def pv(n, i, r, u):
                qc, kt = divmod(u, KT)
                if u == 0:
                    pe.wait_ge(v_loaded[r], 16 * (i + 1))
                if kt == 0 and not (is_first(n) and qc == 0):
                    pe.wait_ge(o_out, n * NQ + qc)
                pe.wait_ge(exped, n * TILES + 2 * u + 2)
                for a in range(HG):
                    m = nc.tensor.matmul(ps_o[a * HD:(a + 1) * HD, :], vt[r][:, kt, a * HD:(a + 1) * HD],
                                         probs[:, u % PR, a, :], start=kt == 0, stop=kt == KT - 1)
                m.then_inc(pv_done, 1)

            def sums(n, w):
                qc, kp = divmod(w, KT // 2)
                if kp == 0 and not (is_first(n) and qc == 0):
                    pe.wait_ge(l_out, n * NQ + qc)
                pe.wait_ge(pair_done, n * PAIRS + w + 1)
                for a in range(HG):
                    m = nc.tensor.matmul(ps_l[a * HD:(a + 1) * HD, :], ones[:, :], pairs[:, w % 2, a, :],
                                         start=kp == 0, stop=kp == KT // 2 - 1)
                m.then_inc(sum_done, 1)

            def late(n, i, r, u):
                before = (n - 1, i if r else i - 1, (r - 1) % R3)
                if u >= 1:
                    pv(n, i, r, u - 1)
                elif not is_first(n):
                    pv(*before, UNITS - 1)

            def late_sums(n, u):
                if u % 2 == 0:
                    w = (u - PAIR_LAG) // 2
                    if w >= 0:
                        sums(n, w)
                    elif not is_first(n):
                        sums(n - 1, PAIRS + w)

            def step(i, r, n):
                r1 = (r + 1) % R3
                i1 = i + 1 if r1 == 0 else i
                todo = [] if is_last(n) else list(range(USES))

                def maxima(count):
                    for _ in range(count if todo else 0):
                        max_use(n + 1, i1, r1, todo.pop(0))

                for u in range(UNITS):
                    spread = (1, 2, 1, 1) if u % (UNITS // 2) == 0 else (1, 2, 0, 1) if u == UNITS - 1 else (1, 1, 1, 1)
                    scores(n, r, u, 0)
                    maxima(spread[0])
                    scores(n, r, u, 1)
                    maxima(spread[1])
                    late(n, i, r, u)
                    maxima(spread[2])
                    late_sums(n, u)
                    maxima(spread[3])
                if is_last(n):
                    pv(n, i, r, UNITS - 1)
                    sums(n, PAIRS - 2)
                    sums(n, PAIRS - 1)

            pe.wait_ge(ones_done, 1)
            for u in range(USES):
                max_use(0, 0, 0, u)
            rounds(pe, step)

        @block.scalar
        def _(act):
            def take(n, qc, src, dst, ready, count, stored, out):
                act.wait_ge(ready, count)
                if not is_first(n):
                    act.wait_ge(stored[qc], 16 * n)
                nc.scalar.copy(dst[:, qc, :], src[:, :]).then_inc(out, 1)

            def take_o(n, qc):
                take(n, qc, ps_o, o_sb, pv_done, n * UNITS + (qc + 1) * KT, o_stored, o_out)

            def take_l(n, qc):
                take(n, qc, ps_l, l_sb, sum_done, n * PAIRS + (qc + 1) * KT // 2, l_stored, l_out)

            def step(i, r, n):
                for u in range(UNITS):
                    for hp in range(2):
                        if hp == 0 and (u >= PR or not is_first(n)):
                            act.wait_ge(pv_done, n * UNITS + u - PR + 1)
                            if u % 2 == 0:
                                act.wait_ge(pair_done, n * PAIRS + (u - PR) // 2 + 1)
                        act.wait_ge(scored, n * TILES + 2 * u + hp + 1)
                        nc.scalar.activation(probs[:, u % PR, 2 * hp:2 * hp + 2, :], ps_s[hp][:, :, :], ACT.Exp,
                                             scale=SCALE).then_inc(exped, 1)
                        if hp == 0:
                            if u == KT + 1:
                                take_o(n, 0)
                            if u == KT + PAIR_LAG - 1:
                                take_l(n, 0)
                            if u == 1 and not is_first(n):
                                take_o(n - 1, 1)
                            if u == PAIR_LAG - 1 and not is_first(n):
                                take_l(n - 1, 1)
                if is_last(n):
                    take_o(n, 1)
                    take_l(n, 1)

            rounds(act, step)

        @block.gpsimd
        def _(pool):
            def step(i, r, n):
                for w in range(PAIRS):
                    if w >= 2 or not is_first(n):
                        pool.wait_ge(sum_done, n * PAIRS + w - 1)
                    pool.wait_ge(exped, n * TILES + 4 * w + 4)
                    nc.gpsimd.tensor_tensor(pairs[:, w % 2, :, :], probs[:, 2 * w % PR, :, :],
                                            probs[:, (2 * w + 1) % PR, :, :], ALU.add).then_inc(pair_done, 1)

            rounds(pool, step)

        @block.vector
        def _(dve):
            for r in range(R3):
                nc.vector.memset(ks[r][ROWS:ROWS + 1, :, :].bitcast(F32), 1.0)
            nc.vector.memset(ones[:], 1.0).then_inc(ones_done, 1)

            def max_use(m, u):
                half, j = divmod(u, MAXH + 1)
                dve.wait_ge(m_scored, m * USES + u + 1)
                if j == MAXH:
                    if not is_first(m):
                        dve.wait_ge(m_stacked[half], 16 * m)
                    nc.vector.tensor_scalar(neg_max[:, half, :], ps_m[u % 2][0:HG * QT, 0:P], -1.0, None,
                                            ALU.mult).then_inc(m_read, 1)
                    return
                aq, kc = divmod(j, 2)
                nc.vector.reduce_max(part_max[:, half, kc, aq:aq + 1], ps_m[u % 2][:, :], AX).then_inc(m_read, 1)
                if j == MAXH - 1:
                    dve.wait_ge(m_read, m * USES + u + 1)
                    nc.vector.tensor_tensor(row_max[:, half, :], part_max[:, half, 0, :], part_max[:, half, 1, :],
                                            ALU.max).then_inc(m_rows, 1)

            def step(i, r, n):
                for u in range(0 if is_last(n) else USES):
                    max_use(n + 1, u)

            for u in range(USES):
                max_use(0, u)
            rounds(dve, step)


def mix_block(nc, sem, held, t, x_d, o_d, l_d, inv_d, wo_d, wr_d, wk_d, wv_d, bo_d, mur_d, muk_d, out_d):
    RELU = 2
    with ExitStack() as ctx:
        def sb(name, shape, dt=F32):
            return ctx.enter_context(nc.sbuf_tensor(name, shape, dt))

        w_hi = {k: sb(f"mix_w_{k}_hi", [P, FC, D], F32R) for k in "okrv"}
        w_lo = {k: sb(f"mix_w_{k}_lo", [P, FC, D], F32R) for k in "okrv"}
        bo = sb("bo", [P, D])
        mu_r = sb("mu_r", [P, FC])
        mu_k = sb("mu_k", [P, FC])
        x_in = sb("mix_x_in", [P, TPC, D])
        xs = [sb(f"xs{i}", [P, TPC, D]) for i in range(2)]
        o_in = sb("o_in", [P, FC, CH])
        o_hi = sb("o_hi", [P, FC, CH], F32R)
        o_lo = sb("o_lo", [P, FC, CH], F32R)
        xT = [sb(f"xT{i}", [P, FC, CH + 1]) for i in range(2)]
        diff = sb("diff", [P, FC, CH])
        mixed = sb("mixed", [P, FC, CH])
        xn = mixed[:].rearrange("p f t -> p (f t)").rearrange("p (s d) -> p s d", s=TPC)
        xk_hi = sb("xk_hi", [P, FC, CH], F32R)
        xk_lo = sb("xk_lo", [P, FC, CH], F32R)
        xr_hi = sb("xr_hi", [P, FC, CH], F32R)
        xr_lo = sb("xr_lo", [P, FC, CH], F32R)
        relu = sb("relu", [P, RELU, CH])
        ka_hi = sb("ka_hi", [P, FC, CH], F32R)
        ka_lo = sb("ka_lo", [P, FC, CH], F32R)
        gate = sb("gate", [P, TPC, D])
        stats = sb("mix_stats", [P, TPC, 6])
        mv = sb("mix_mv", [P, TPC, 2])
        rstd = sb("mix_rstd", [P, TPC])
        minus_half = sb("mix_minus_half", [P, TPC])
        ps_t = [ctx.enter_context(nc.psum_tensor(f"mix_t{i}", [P, CH], F32)) for i in range(FC)]
        ps_p = [ctx.enter_context(nc.psum_tensor(f"mix_p{i}", [P, CH], F32)) for i in range(TPC)]

        w_loaded = {k: sem(f"w_loaded_{k}") for k in "okrv"}
        small_loaded = sem("small_loaded")
        w_split_hi = sem("w_split_hi")
        w_split_lo = sem("w_split_lo")
        l_loaded = sem("l_loaded")
        inv_done = sem("inv_done")
        inv_stored = sem("inv_stored")
        x_loaded = sem("mix_x_loaded")
        o_loaded = sem("mix_o_loaded")
        inv_loaded = sem("inv_loaded")
        o_div = sem("o_div")
        oh_done = sem("oh_done")
        ol_done = sem("ol_done")
        xb_done = sem("xb_done")
        wo_done = sem("wo_done")
        x1_done = sem("x1_done")
        ln_step = sem("mix_ln_step")
        rstd_done = sem("mix_rstd_done")
        normed = sem("mix_normed")
        transposed = sem("mix_transposed")
        xT_done = sem("xT_done")
        half_set = sem("mix_half_set")
        zero_done = sem("zero_done")
        edge_done = sem("edge_done")
        diff_done = sem("diff_done")
        xk_done = sem("xk_done")
        xkh_done = sem("xkh_done")
        xkl_done = sem("xkl_done")
        xr_done = sem("xr_done")
        xrh_done = sem("xrh_done")
        xrl_done = sem("xrl_done")
        k_done = sem("k_done")
        relu_done = sem("relu_done")
        sq_done = sem("sq_done")
        kah_done = sem("kah_done")
        kal_done = sem("kal_done")
        r_done = sem("r_done")
        gate_done = sem("gate_done")
        v_done = sem("mix_v_done")
        gated = sem("gated")
        out_done = sem("out_done")
        out_stored = sem("out_stored")
        block = ctx.enter_context(nc.Block())
        x_v = x_d.rearrange("b (h s p) d -> b h p s d", h=CPB, p=P)
        out_v = out_d.rearrange("b (h s p) d -> b h p s d", h=CPB, p=P)
        o_v = o_d.rearrange("(b g) p t -> b p g t", g=FC)
        ORDER = "okrv"
        staging = {"o": x_in, "k": xs[1], "r": diff, "v": mixed}
        sums = gate[:].rearrange("p s d -> p (s d)")[:, 0:S]
        inv = xs[0][:].rearrange("p s d -> p (s d)")[:, 0:S]
        inv_v = inv_d.rearrange("(b g a) t -> b g a t", g=FC, a=HG)
        last_i = B - 1

        def chunks(eng, body):
            body(0, False)
            with eng.Fori(1, last_i) as i:
                body(i, False)
            body(last_i, True)

        @block.sync
        def _(sp):
            def load_o(b, par):
                cs = slice(par * CH, (par + 1) * CH)
                sp.dma_start(o_in[:], o_v[b, :, :, cs]).then_inc(o_loaded, 16)
                for a in range(HG):
                    sp.dma_start(o_lo[a * HD:(a + 1) * HD, :, :].bitcast(F32),
                                 inv_v[b, :, a, cs].rearrange("(o g) t -> o g t", o=1).broadcast_to([HD, FC, CH])
                                 ).then_inc(inv_loaded, 16)

            sp.dma_start(sums, l_d).then_inc(l_loaded, 16)
            for k, src in zip(ORDER, (wo_d, wk_d, wr_d, wv_d)):
                sp.dma_start(staging[k][:], src.rearrange("(c p) n -> p c n", p=P)).then_inc(w_loaded[k], 16)
                if k == "o":
                    sp.dma_start(bo[:], bo_d.rearrange("(a n) -> a n", a=1).broadcast_to([P, D])).then_inc(small_loaded, 16)
                    sp.dma_start(mu_r[:], mur_d).then_inc(small_loaded, 16)
                    sp.dma_start(mu_k[:], muk_d).then_inc(small_loaded, 16)
                    sp.wait_ge(inv_done, 1)
                    sp.dma_start(inv_d, inv).then_inc(inv_stored, 16)
                    sp.wait_ge(inv_stored, 16)
                    load_o(0, 0)
                    sp.wait_ge(w_split_lo, 1)
                    sp.dma_start(x_in[:], x_v[0, 0]).then_inc(x_loaded, 16)
            sp.wait_ge(wo_done, TPC)
            load_o(0, 1)
            sp.wait_ge(xb_done, TPC)
            sp.dma_start(x_in[:], x_v[0, 1]).then_inc(x_loaded, 16)

            def body(i, last):
                for par in range(CPB):
                    c = i * CPB + par
                    if not last:
                        sp.wait_ge(wo_done, c * TPC + 2 * TPC)
                        sp.sem_inc(held, 1)
                        load_o(i + 1, par)
                        sp.wait_ge(xb_done, c * TPC + 2 * TPC)
                        sp.sem_inc(held, 1)
                        sp.dma_start(x_in[:], x_v[i + 1, par]).then_inc(x_loaded, 16)
                    sp.wait_ge(out_done, c * TPC + TPC)
                    sp.sem_inc(held, 1)
                    sp.dma_start(out_v[i, par], gate[:]).then_inc(out_stored, 16)

            chunks(sp, body)
            sp.wait_ge(out_stored, 16 * B * CPB)

        @block.tensor
        def _(pe):
            def product(out, stat_hi, stat_lo, mov_hi, mov_lo):
                for f in range(FC):
                    nc.tensor.matmul(out, stat_hi(f), mov_hi(f), start=f == 0, stop=False)
                    nc.tensor.matmul(out, stat_hi(f), mov_lo(f), start=False, stop=False)
                    m = nc.tensor.matmul(out, stat_lo(f), mov_hi(f), start=False, stop=f == FC - 1)
                return m

            def by_token(s, hi, lo, k):
                ts_ = slice(s * P, (s + 1) * P)
                return product(ps_p[s][:, :], lambda f: hi[:, f, ts_], lambda f: lo[:, f, ts_],
                               lambda f: w_hi[k][:, f, :], lambda f: w_lo[k][:, f, :])

            def project(c):
                pe.wait_ge(ol_done, c + 1)
                for s in range(TPC):
                    if type(c) is not int or c >= 2:
                        pe.wait_ge(gated, (c - 2) * TPC + s + 1)
                    by_token(s, o_hi, o_lo, "o").then_inc(wo_done, 1)

            def transposes(c):
                pe.wait_ge(normed, c + 1)
                for f in range(FC):
                    if not is_first(c):
                        pe.wait_ge(xT_done, (c - 1) * FC + f + 1)
                    for s in range(TPC):
                        m = nc.tensor.transpose(ps_t[f][:, s * P:(s + 1) * P], xn[:, s, f * P:(f + 1) * P], t["ident"][:])
                    m.then_inc(transposed, 1)

            def body(i, last):
                for par in range(CPB):
                    c = i * CPB + par
                    more = not (last and par == CPB - 1)
                    if more:
                        project(c + 1)
                    pe.wait_ge(xkl_done, c + 1)
                    for g in range(FC):
                        if more:
                            pe.wait_ge(x1_done, (c + 1) * TPC + g + 1)
                        else:
                            pe.wait_ge(gated, (c - 1) * TPC + g + 1)
                        gs = slice(g * P, (g + 1) * P)
                        product(ps_p[g][:, :], lambda f: w_hi["k"][:, f, gs], lambda f: w_lo["k"][:, f, gs],
                                lambda f: xk_hi[:, f, :], lambda f: xk_lo[:, f, :]).then_inc(k_done, 1)
                    pe.wait_ge(xrl_done, c + 1)
                    for s in range(TPC):
                        pe.wait_ge(relu_done, c * TPC + s + 1)
                        by_token(s, xr_hi, xr_lo, "r").then_inc(r_done, 1)
                    if more:
                        transposes(c + 1)
                    pe.wait_ge(kal_done, c * FC + FC)
                    for s in range(TPC):
                        pe.wait_ge(gate_done, c * TPC + s + 1)
                        by_token(s, ka_hi, ka_lo, "v").then_inc(v_done, 1)

            pe.wait_ge(w_split_lo, 1)
            project(0)
            transposes(0)
            pe.wait_ge(w_split_lo, len(ORDER))
            chunks(pe, body)

        @block.scalar
        def _(act):
            def weights_high(k):
                act.wait_ge(w_loaded[k], 16)
                nc.scalar.copy(w_hi[k][:], staging[k][:]).then_inc(w_split_hi, 1)

            def o_high(c):
                act.wait_ge(o_div, c + 1)
                if not is_first(c):
                    act.wait_ge(wo_done, c * TPC)
                nc.scalar.copy(o_hi[:], o_in[:]).then_inc(oh_done, 1)

            def x_T(c, par, batch):
                for f in range(FC):
                    act.wait_ge(transposed, c * FC + f + 1)
                    if f == 0 and (type(c) is not int or c >= 2):
                        act.wait_ge(xr_done, c - 1)
                        if par == 0:
                            act.wait_ge(edge_done, batch)
                    nc.scalar.copy(xT[par][:, f, 1:CH + 1], ps_t[f][:, :]).then_inc(xT_done, 1)

            def highs(c):
                act.wait_ge(xk_done, c + 1)
                if not is_first(c):
                    act.wait_ge(k_done, c * FC)
                nc.scalar.copy(xk_hi[:], mixed[:]).then_inc(xkh_done, 1)
                act.wait_ge(xr_done, c + 1)
                if not is_first(c):
                    act.wait_ge(r_done, c * TPC)
                nc.scalar.copy(xr_hi[:], diff[:]).then_inc(xrh_done, 1)

            def body(i, last):
                for par in range(CPB):
                    c = i * CPB + par
                    more = not (last and par == CPB - 1)

                    def square_hi(g):
                        act.wait_ge(sq_done, c * FC + g + 1)
                        if g == 0 and not is_first(c):
                            act.wait_ge(v_done, c * TPC)
                        nc.scalar.copy(ka_hi[:, g, :], relu[:, g % RELU, :]).then_inc(kah_done, 1)

                    for g in range(FC):
                        act.wait_ge(k_done, c * FC + g + 1)
                        if g >= RELU or not is_first(c):
                            act.wait_ge(kal_done, c * FC + g + 1 - RELU)
                        nc.scalar.activation(relu[:, g % RELU, :], ps_p[g][:, :], ACT.Relu).then_inc(relu_done, 1)
                        if g >= 1:
                            square_hi(g - 1)
                    square_hi(FC - 1)
                    for s in range(TPC):
                        act.wait_ge(r_done, c * TPC + s + 1)
                        if s == 0 and not is_first(c):
                            act.wait_ge(out_stored, 16 * c)
                        nc.scalar.activation(gate[:, s, :], ps_p[s][:, :], ACT.Sigmoid).then_inc(gate_done, 1)
                    if more:
                        x_T(c + 1, 1 - par, i + par)
                        if not (last and par == CPB - 2):
                            o_high(c + 2)
                        highs(c + 1)

            weights_high("o")
            o_high(0)
            for k in ORDER[1:]:
                weights_high(k)
            x_T(0, 0, 0)
            o_high(1)
            highs(0)
            chunks(act, body)

        @block.gpsimd
        def _(pool):
            nc.gpsimd.memset(xT[0][:, :, 0:1], 0.0).then_inc(zero_done, 1)
            nc.gpsimd.memset(minus_half[:], -0.5).then_inc(half_set, 1)
            pool.wait_ge(half_set, 1)
            pool.wait_ge(small_loaded, 16 * 3)

            def inv_std(c):
                pool.wait_ge(ln_step, c * 3 + 3)
                nc.gpsimd.tensor_tensor(rstd[:, :], rstd[:, :], minus_half[:, :], ALU.pow).then_inc(rstd_done, 1)

            def divide(c):
                pool.wait_ge(o_loaded, 16 * (c + 1))
                pool.wait_ge(inv_loaded, 16 * HG * (c + 1))
                nc.gpsimd.tensor_tensor(o_in[:], o_in[:], o_lo[:].bitcast(F32), ALU.mult).then_inc(o_div, 1)

            def o_low(c):
                pool.wait_ge(oh_done, c + 1)
                nc.gpsimd.tensor_tensor(o_lo[:], o_in[:], o_hi[:], ALU.subtract).then_inc(ol_done, 1)

            def add_bias(c, par, s):
                if s == 0:
                    pool.wait_ge(x_loaded, 16 * (c + 1))
                nc.gpsimd.tensor_tensor(xs[par][:, s, :], x_in[:, s, :], bo[:, :], ALU.add).then_inc(xb_done, 1)

            def edge(c):
                pool.wait_ge(xT_done, c * FC + FC)
                if not is_first(c):
                    pool.wait_ge(xr_done, c)
                pool.sem_inc(held, 1)
                nc.gpsimd.tensor_copy(xT[1][:, :, 0:1], xT[0][:, :, CH:CH + 1]).then_inc(edge_done, 1)

            def body(i, last):
                for par in range(CPB):
                    c = i * CPB + par
                    more = not (last and par == CPB - 1)
                    if more:
                        inv_std(c + 1)
                    for g in range(FC):
                        pool.wait_ge(relu_done, c * FC + g + 1)
                        nc.gpsimd.tensor_tensor(relu[:, g % RELU, :], relu[:, g % RELU, :], relu[:, g % RELU, :],
                                                ALU.mult).then_inc(sq_done, 1)
                    two_more = not last
                    if two_more:
                        divide(c + 2)
                    if more and par == 1:
                        edge(c + 1)
                    if two_more:
                        o_low(c + 2)
                    for s in range(TPC):
                        pool.wait_ge(gated, c * TPC + s + 1)
                        nc.gpsimd.tensor_tensor(gate[:, s, :], gate[:, s, :], xs[par][:, s, :], ALU.add).then_inc(out_done, 1)
                        if two_more:
                            pool.wait_ge(out_done, c * TPC + s + 1)
                            add_bias(c + 2, par, s)

            divide(0)
            o_low(0)
            for s in range(TPC):
                add_bias(0, 0, s)
            inv_std(0)
            edge(0)
            divide(1)
            o_low(1)
            for s in range(TPC):
                add_bias(1, 1, s)
            chunks(pool, body)

        @block.vector
        def _(dve):
            def weights_low(n):
                k = ORDER[n]
                dve.wait_ge(w_split_hi, n + 1)
                nc.vector.tensor_tensor(w_lo[k][:], staging[k][:], w_hi[k][:], ALU.subtract).then_inc(w_split_lo, 1)

            def norm(c, par):
                x = xs[par]
                for s in range(TPC):
                    dve.wait_ge(xb_done, c * TPC + s + 1)
                    dve.wait_ge(wo_done, c * TPC + s + 1)
                    nc.vector.tensor_tensor(x[:, s, :], ps_p[s][:, :], x[:, s, :], ALU.add).then_inc(x1_done, 1)
                for s in range(TPC):
                    dve.wait_ge(x1_done, c * TPC + s + 1)
                    v = nc.vector.bn_stats(stats[:, s, :], x[:, s, :])
                v.then_inc(ln_step, 1)
                dve.wait_ge(ln_step, c * 3 + 1)
                dve.sem_inc(held, 1)
                for s in range(TPC):
                    v = nc.vector.bn_aggr(mv[:, s, :], stats[:, s, :])
                v.then_inc(ln_step, 1)
                dve.wait_ge(ln_step, c * 3 + 2)
                nc.vector.tensor_scalar(rstd[:, :], mv[:, :, 1], EPS, None, ALU.add).then_inc(ln_step, 1)
                dve.wait_ge(rstd_done, c + 1)
                if not is_first(c):
                    dve.wait_ge(transposed, c * FC)
                for s in range(TPC):
                    v = nc.vector.tensor_scalar(xn[:, s, :], x[:, s, :], mv[:, s, 0:1], rstd[:, s:s + 1],
                                                ALU.subtract, ALU.mult)
                v.then_inc(normed, 1)

            def shift(c, par, batch):
                dve.wait_ge(xT_done, c * FC + FC)
                if par == 0:
                    dve.wait_ge(zero_done, 1)
                else:
                    dve.wait_ge(edge_done, batch + 1)
                cur, prev = xT[par][:, :, 1:CH + 1], xT[par][:, :, 0:CH]
                nc.vector.tensor_tensor(diff[:], cur, prev, ALU.subtract).then_inc(diff_done, 1)
                dve.wait_ge(diff_done, c + 1)
                for f in range(FC):
                    v = nc.vector.scalar_tensor_tensor(mixed[:, f, :], diff[:, f, :], mu_k[:, f:f + 1], prev[:, f, :],
                                                       ALU.mult, ALU.add)
                v.then_inc(xk_done, 1)
                for f in range(FC):
                    v = nc.vector.scalar_tensor_tensor(diff[:, f, :], diff[:, f, :], mu_r[:, f:f + 1], prev[:, f, :],
                                                       ALU.mult, ALU.add)
                v.then_inc(xr_done, 1)
                dve.wait_ge(xkh_done, c + 1)
                nc.vector.tensor_tensor(xk_lo[:], mixed[:], xk_hi[:], ALU.subtract).then_inc(xkl_done, 1)
                dve.wait_ge(xrh_done, c + 1)
                nc.vector.tensor_tensor(xr_lo[:], diff[:], xr_hi[:], ALU.subtract).then_inc(xrl_done, 1)

            def body(i, last):
                for par in range(CPB):
                    c = i * CPB + par
                    more = not (last and par == CPB - 1)

                    def square_lo(g):
                        dve.wait_ge(kah_done, c * FC + g + 1)
                        nc.vector.tensor_tensor(ka_lo[:, g, :], relu[:, g % RELU, :], ka_hi[:, g, :],
                                                ALU.subtract).then_inc(kal_done, 1)

                    if more:
                        norm(c + 1, 1 - par)
                    for g in range(FC):
                        square_lo(g)
                    if more:
                        shift(c + 1, 1 - par, i if par == 0 else i + 1)
                    for s in range(TPC):
                        dve.wait_ge(v_done, c * TPC + s + 1)
                        nc.vector.tensor_tensor(gate[:, s, :], ps_p[s][:, :], gate[:, s, :], ALU.mult).then_inc(gated, 1)

            dve.wait_ge(l_loaded, 16)
            nc.vector.reciprocal(inv, sums).then_inc(inv_done, 1)
            dve.wait_ge(small_loaded, 16 * 3)
            dve.sem_inc(held, 1)
            for n in range(len(ORDER)):
                weights_low(n)
            norm(0, 0)
            shift(0, 0, 0)
            chunks(dve, body)


def block_program(nc, x, wdqT, bdq, wuq, buq, wqr, bqr, wkr, bkr, wdkvT, bdkv, wuk, buk, wuv, buv, wo, bo,
                  wrT, wkT, wvT, mu_r, mu_k, cos, sin, ident, out):
    def scratch(name, shape, dt):
        return nc.dram_tensor(name, shape, dt, kind="Internal").ap()

    qk = [scratch(n, (B, FC, P, S), F32) for n in ("q_hi_scratch", "q_lo_scratch", "k_hi_scratch", "k_lo_scratch")]
    v_s = scratch("v_scratch", (B, FC, P, KT, P), F32)
    o_s = scratch("o_scratch", (NG, P, S), F32)
    l_s = scratch("l_scratch", (NG * HG, S), F32)
    inv_s = scratch("inv_scratch", (NG * HG, S), F32)
    with ExitStack() as ctx:
        def sem(name):
            return ctx.enter_context(nc.semaphore(name))

        held = sem("held")
        t = {"ident": ctx.enter_context(nc.sbuf_tensor("ident", [P, P], F32))}
        with ExitStack() as early:
            def sb(name, shape, dt=F32):
                return early.enter_context(nc.sbuf_tensor(name, shape, dt))

            t["cos"] = sb("cos", [P, S])
            t["sin"] = sb("sin", [P, S])
            t["bq"] = sb("bq", [P, FC + 1])
            t["bk"] = sb("bk", [P, FC + 1])
            t["bv"] = sb("bv", [P, D])
            w = {k: sb("w_" + k, [P, FC, D if k[0] == "v" else D + P], F32R)
                 for k in ("q_hi", "q_lo", "k_hi", "k_lo", "v_hi", "v_lo")}
            fold_block(nc, sem, t, w, (wdqT, wdkvT, wuq, wqr, wuk, wuv, wkr, bdq, bdkv, buq, bqr, buk, bkr, buv,
                                       cos, sin, ident))
            project_block(nc, sem, held, t, w, x, (*qk, v_s))
        grouped = [a.rearrange("b g p t -> (b g) p t") for a in qk] + [v_s.rearrange("b g p k d -> (b g) p k d")]
        attend_block(nc, sem, held, t, grouped, o_s, l_s.rearrange("(n a) t -> n a t", a=HG))
        mix_block(nc, sem, held, t, x, o_s, l_s, inv_s, wo, wrT, wkT, wvT, bo, mu_r, mu_k, out)


def kernel(**inputs):
    import numpy as np
    import concourse.bacc as bacc
    from concourse.bass_utils import run_bass_kernel_spmd

    def given(name):
        return np.ascontiguousarray(inputs[name])

    def turned(name):
        return np.ascontiguousarray(np.asarray(inputs[name]).T)

    def columns(name):
        return np.ascontiguousarray(np.asarray(inputs[name]).reshape(-1, P).T)

    tiny = np.finfo(np.float32).tiny
    theta = np.power(np.float32(10000.0), np.float32(-2.0) * np.arange(D // 2, dtype=np.float32)) / np.float32(D // 2)
    theta[theta < tiny] = 0.0
    assert not theta[P // 2:].any()
    angle = np.arange(S, dtype=np.float32)[None, :] * theta[:P // 2, None]
    cos = np.repeat(np.cos(angle.astype(np.float64)), 2, axis=0).astype(np.float32)
    sin = np.repeat(np.sin(angle.astype(np.float64)), 2, axis=0).astype(np.float32)
    sin[0::2] *= -1.0

    a, f = "L0_attn_", "L0_ffn_"
    arrays = {
        "x": given(a + "x"), "wdqT": turned(a + "Wd_q_w"), "bdq": columns(a + "Wd_q_b"),
        "wuq": given(a + "Wu_q_w"), "buq": columns(a + "Wu_q_b"), "wqr": given(a + "Wq_r_w"), "bqr": columns(a + "Wq_r_b"),
        "wkr": given(a + "Wk_r_w"), "bkr": columns(a + "Wk_r_b"), "wdkvT": turned(a + "Wd_kv_w"),
        "bdkv": columns(a + "Wd_kv_b"), "wuk": given(a + "Wu_k_w"), "buk": columns(a + "Wu_k_b"),
        "wuv": given(a + "Wu_v_w"), "buv": given(a + "Wu_v_b"), "wo": given(a + "Wo_w"), "bo": given(a + "Wo_b"),
        "wrT": turned(f + "W_r"), "wkT": turned(f + "W_k"), "wvT": turned(f + "W_v"),
        "mu_r": columns(f + "mu_r"), "mu_k": columns(f + "mu_k"),
        "cos": cos, "sin": sin, "ident": np.eye(P, dtype=np.float32),
    }
    nc = bacc.Bacc("TRN2", target_bir_lowering=False, num_devices=1)
    args = [nc.dram_tensor(f"in_{k}", v.shape, mybir.dt.from_np(v.dtype), kind="ExternalInput").ap()
            for k, v in arrays.items()]
    out = nc.dram_tensor("out", (B, S, D), F32, kind="ExternalOutput").ap()
    block_program(nc, *args, out)
    got = run_bass_kernel_spmd(nc, [{f"in_{k}": v for k, v in arrays.items()}], core_ids=[0])
    return got.results[0]["out"]
```

```python
from contextlib import ExitStack

import concourse.bass as bass
from concourse import mybir

F32 = mybir.dt.float32
F32R = mybir.dt.float32r
ALU = mybir.AluOpType
ACT = mybir.ActivationFunctionType
AX = mybir.AxisListType.X

B, S, D, H = 8, 1024, 512, 16
DL = 256
HD = D // H
P = 128
FC = D // P
LC = DL // P
HG = P // HD
NG = B * FC
CH = 512
TPC = CH // P
CPB = S // CH
KT = S // P
EPS = 1e-5
SCALE = float(H + DL + DL) ** -0.5
SWAP = [i ^ 1 for i in range(32)]


def is_first(c):
    return type(c) is int and c == 0


def fold_block(nc, sem, t, w, att, drams, load_x):
    (wdq_d, wdkv_d, wuq_d, wqr_d, wuk_d, wuv_d, wkr_d, bdq_d, bdkv_d, buq_d, bqr_d, buk_d, bkr_d, buv_d,
     cos_d, sin_d, ident_d) = drams
    with ExitStack() as ctx:
        def sb(name, shape, dt=F32):
            return ctx.enter_context(nc.sbuf_tensor(name, shape, dt))

        wdqT = sb("wdqT", [P, LC, D])
        wdkvT = sb("wdkvT", [P, LC, D])
        wuq = sb("wuq", [P, LC, D])
        wqr = sb("wqr", [P, LC, D])
        wuk = sb("wuk", [P, LC, D])
        wuv = sb("wuv", [P, LC, D])
        wkr = sb("wkr", [P, FC, D])
        bdq = sb("bdq", [P, LC])
        bdkv = sb("bdkv", [P, LC])
        buq = sb("buq", [P, FC])
        bqr = sb("bqr", [P, FC])
        buk = sb("buk", [P, FC])
        bkr = sb("bkr", [P, FC])
        buv = sb("buv", [P, D])
        bd_cols = sb("bd_cols", [P, LC, P])
        k_full = sb("k_full", [P, 2, D])
        ps_a = [ctx.enter_context(nc.psum_tensor(f"fold_a{i}", [P, D], F32)) for i in range(2)]
        ps_y = [ctx.enter_context(nc.psum_tensor(f"fold_y{i}", [P, D], F32)) for i in range(2)]
        ps_b = ctx.enter_context(nc.psum_tensor("fold_bias", [P, D], F32))
        ps_v = ctx.enter_context(nc.psum_tensor("fold_vbias", [P, D], F32))

        loaded = [sem("fold_loaded_q"), sem("fold_loaded")]
        product = sem("fold_product")
        hi_done = sem("fold_hi")
        lo_done = sem("fold_lo")
        k_sum = sem("fold_k_sum")
        bcols = sem("fold_bcols")
        bias_ps = sem("fold_bias_ps")
        bias_sb = sem("fold_bias_sb")
        block = ctx.enter_context(nc.Block())
        loads = [(wdqT, wdq_d.rearrange("(j p) n -> p j n", p=P)), (wuq, wuq_d.rearrange("(j p) n -> p j n", p=P)),
                 (wqr, wqr_d.rearrange("(j p) n -> p j n", p=P)), (wdkvT, wdkv_d.rearrange("(j p) n -> p j n", p=P)),
                 (wuk, wuk_d.rearrange("(j p) n -> p j n", p=P)), (wuv, wuv_d.rearrange("(j p) n -> p j n", p=P)),
                 (wkr, wkr_d.rearrange("(j p) n -> p j n", p=P)),
                 (t["cos"], cos_d), (t["sin"], sin_d), (t["ident"], ident_d),
                 (bdq, bdq_d), (bdkv, bdkv_d),
                 (buq, buq_d), (bqr, bqr_d),
                 (buk, buk_d), (bkr, bkr_d),
                 (buv, buv_d.rearrange("(a n) -> a n", a=1).broadcast_to([P, D]))]
        FIRST = 3
        n_loads = [16 * FIRST, 16 * (len(loads) - FIRST)]

        @block.sync
        def _(sp):
            for n, (dst, src) in enumerate(loads):
                sp.dma_start(dst[:], src).then_inc(loaded[0 if n < FIRST else 1], 16)
            load_x(sp)

        @block.tensor
        def _(pe):
            pe.wait_ge(loaded[0], n_loads[0])
            for i in range(3 * FC):
                kind, c = divmod(i, FC)
                if i == FC:
                    pe.wait_ge(loaded[1], n_loads[1])
                if i >= 2:
                    pe.wait_ge(lo_done, i - 1)
                a, y, cs = ps_a[i % 2], ps_y[i % 2], slice(c * P, (c + 1) * P)
                if kind == 0:
                    for j in range(LC):
                        nc.tensor.matmul(a[:, 0:HD], wdqT[:, j, cs], wuq[:, j, 0:HD], start=j == 0, stop=j == LC - 1)
                    for j in range(LC):
                        nc.tensor.matmul(y[:, 0:HD], wdqT[:, j, cs], wqr[:, j, 0:HD], start=j == 0, stop=j == LC - 1)
                    for j in range(LC):
                        nc.tensor.matmul(a[:, HD:D], wdqT[:, j, cs], wuq[:, j, HD:D], start=j == 0, stop=False)
                        last = nc.tensor.matmul(a[:, HD:D], wdqT[:, j, cs], wqr[:, j, HD:D], start=False, stop=j == LC - 1)
                else:
                    up = wuk if kind == 1 else wuv
                    for j in range(LC):
                        last = nc.tensor.matmul(a[:, :], wdkvT[:, j, cs], up[:, j, :], start=j == 0, stop=j == LC - 1)
                last.then_inc(product, 1)
            for n, (up, down) in enumerate(((wuq, bdq), (wqr, bdq), (wuk, bdkv))):
                for g in range(FC):
                    col = n * FC + g
                    for j in range(LC):
                        nc.tensor.matmul(ps_b[:, col:col + 1], up[:, j, g * P:(g + 1) * P], down[:, j:j + 1],
                                         start=j == 0, stop=j == LC - 1)
            pe.wait_ge(bcols, LC)
            for j in range(LC):
                last = nc.tensor.matmul(ps_v[:, :], bd_cols[:, j, :], wuv[:, j, :], start=j == 0, stop=j == LC - 1)
            last.then_inc(bias_ps, 1)

        @block.scalar
        def _(act):
            for i in range(3 * FC):
                kind, c = divmod(i, FC)
                act.wait_ge(product, i + 1)
                if i == FC:
                    act.wait_ge(loaded[1], n_loads[1])
                if kind == 0:
                    nc.scalar.copy(w["q_hi"][:, c, :], ps_a[i % 2][:, :])
                    nc.scalar.copy(w["rot_hi"][:, c, 0:HD], ps_y[i % 2][:, 0:HD]).then_inc(hi_done, 1)
                elif kind == 1:
                    act.wait_ge(k_sum, c + 1)
                    nc.scalar.copy(w["k_hi"][:, c, :], k_full[:, c % 2, :])
                    nc.scalar.copy(w["rot_hi"][:, c, HD:2 * HD], wkr[:, c, 0:HD]).then_inc(hi_done, 1)
                else:
                    nc.scalar.copy(w["v_hi"][:, c, :], ps_a[i % 2][:, :]).then_inc(hi_done, 1)

        @block.vector
        def _(dve):
            nc.vector.memset(att["k"][0][ROWS:ROWS + 1, :, :].bitcast(F32), 1.0)
            nc.vector.memset(att["ones"][:], 1.0).then_inc(att["ones_done"], 1)
            for part in ("rot_hi", "rot_lo"):
                nc.vector.memset(w[part][:, :, 2 * HD:P].bitcast(F32), 0.0)
            nc.vector.memset(bd_cols[:], 1.0).then_inc(bias_sb, 1)
            for i in range(3 * FC):
                kind, c = divmod(i, FC)
                if i == FC:
                    dve.wait_ge(loaded[1], n_loads[1])
                    dve.wait_ge(bias_sb, 1)
                    for j in range(LC):
                        nc.vector.tensor_scalar(bd_cols[:, j, :], bd_cols[:, j, :], bdkv[:, j:j + 1], None,
                                                ALU.mult).then_inc(bcols, 1)
                a, y = ps_a[i % 2], ps_y[i % 2]
                dve.wait_ge(product, i + 1)
                if kind == 0:
                    dve.wait_ge(hi_done, i + 1)
                    nc.vector.tensor_tensor(w["q_lo"][:, c, :], a[:, :], w["q_hi"][:, c, :], ALU.subtract)
                    nc.vector.tensor_tensor(w["rot_lo"][:, c, 0:HD], y[:, 0:HD], w["rot_hi"][:, c, 0:HD],
                                            ALU.subtract).then_inc(lo_done, 1)
                elif kind == 1:
                    kf = k_full[:, c % 2, :]
                    nc.vector.tensor_copy(kf[:, 0:HD], a[:, 0:HD])
                    nc.vector.tensor_tensor(kf[:, HD:D], a[:, HD:D], wkr[:, c, HD:D], ALU.add).then_inc(k_sum, 1)
                    dve.wait_ge(k_sum, c + 1)
                    dve.wait_ge(hi_done, i + 1)
                    nc.vector.tensor_tensor(w["k_lo"][:, c, :], kf, w["k_hi"][:, c, :], ALU.subtract)
                    nc.vector.tensor_tensor(w["rot_lo"][:, c, HD:2 * HD], wkr[:, c, 0:HD], w["rot_hi"][:, c, HD:2 * HD],
                                            ALU.subtract).then_inc(lo_done, 1)
                else:
                    dve.wait_ge(hi_done, i + 1)
                    nc.vector.tensor_tensor(w["v_lo"][:, c, :], a[:, :], w["v_hi"][:, c, :], ALU.subtract).then_inc(lo_done, 1)
            dve.wait_ge(bias_ps, 1)
            rot_q, rot_k = bd_cols[:, 0, 0:FC], bkr
            nc.vector.tensor_tensor(t["bq"][:, :], ps_b[:, 0:FC], buq[:, :], ALU.add)
            nc.vector.tensor_tensor(rot_q, ps_b[:, FC:2 * FC], bqr[:, :], ALU.add)
            nc.vector.tensor_tensor(t["bk"][:, :], ps_b[:, 2 * FC:3 * FC], buk[:, :], ALU.add)
            nc.vector.tensor_tensor(t["bv"][:, :], ps_v[:, :], buv[:, :], ALU.add).then_inc(bias_sb, 1)
            dve.wait_ge(bias_sb, 2)
            for total, rot, row in ((t["bq"], rot_q, 0), (t["bk"], rot_k, HD)):
                nc.vector.tensor_copy(t["br"][row:row + HD, :], rot[0:HD, 0:1])
                for q in range(HD, P, HD):
                    nc.vector.tensor_tensor(total[q:q + HD, 0:1], total[q:q + HD, 0:1], rot[q:q + HD, 0:1], ALU.add)
                nc.vector.tensor_tensor(total[:, 1:FC], total[:, 1:FC], rot[:, 1:FC], ALU.add)


R3 = 3
NQ = S // CH
QT = CH // P
ROWS = 3 * HD
MR = 3
MAXH = 2 * HG * QT
USE = [(0, j) for j in range(MAXH)] + [(1, 0), (1, 1), (0, MAXH)] + [(1, j) for j in range(2, MAXH + 1)]
USES = len(USE)
ROWS_AT = [USE.index((half, MAXH)) for half in range(2)]
LOADS = 3 * NQ + 3


def group_buffers(att, sb, r):
    att["q"].append(sb(f"q_stack{r}", [ROWS + 1, NQ, HG, CH], F32R))
    att["k"].append(sb(f"k_stack{r}", [ROWS + 1, HG, S], F32R))
    att["v"].append(sb(f"v_tiles{r}", [P, KT, P]))


def load_group(sp, att, scratch, n, r):
    qh_d, ql_d, kh_d, kl_d, v_d = scratch
    for part, src in enumerate((qh_d, ql_d, qh_d)):
        for qc in range(NQ):
            sp.dma_start(att["q"][r][part * HD:(part + 1) * HD, qc, :, :].bitcast(F32),
                         src[n, :, qc * CH:(qc + 1) * CH].rearrange("(a p) t -> p a t", p=HD)).then_inc(att["loaded"][r], 16)
    for part, src in enumerate((kh_d, kh_d, kl_d)):
        sp.dma_start(att["k"][r][part * HD:(part + 1) * HD, :, :].bitcast(F32),
                     src[n].rearrange("(a p) t -> p a t", p=HD)).then_inc(att["loaded"][r], 16)
    sp.dma_start(att["v"][r][:], v_d[n]).then_inc(att["v_loaded"][r], 16)


def max_product(nc, pe, att, banks, ident, m, r, loads, u):
    half, j = USE[u]
    if u >= MR or not is_first(m):
        pe.wait_ge(att["m_read"], m * USES + u - MR + 1)
    if j == MAXH:
        pe.wait_ge(att["m_rows"], m * 2 + half + 1)
        nc.tensor.transpose(banks[u % MR][0:HG * QT, 0:P], att["row_max"][:, half, :], ident[:]).then_inc(att["m_scored"], 1)
        return
    if u == 0:
        pe.wait_ge(att["loaded"][r], 16 * LOADS * loads)
    h, q, kc = j // (2 * QT), j // 2 % QT, j % 2
    nc.tensor.matmul(banks[u % MR][:, :], att["q"][r][0:ROWS, half, h, q * P:(q + 1) * P],
                     att["k"][r][0:ROWS, h, kc * CH:(kc + 1) * CH], start=True, stop=True).then_inc(att["m_scored"], 1)


def max_reduce(nc, dve, att, banks, m, u):
    half, j = USE[u]
    part_max, row_max, neg_max = att["part_max"], att["row_max"], att["neg_max"]
    dve.wait_ge(att["m_scored"], m * USES + u + 1)
    if j == MAXH:
        if not is_first(m):
            dve.wait_ge(att["m_stacked"][half], 16 * m)
        nc.vector.tensor_scalar(neg_max[:, half, :], banks[u % MR][0:HG * QT, 0:P], -1.0, None,
                                ALU.mult).then_inc(att["m_read"], 1)
        return
    hq, kc = divmod(j, 2)
    nc.vector.reduce_max(part_max[:, half, kc, hq:hq + 1], banks[u % MR][:, :], AX).then_inc(att["m_read"], 1)
    if j == MAXH - 1:
        dve.wait_ge(att["m_read"], m * USES + u + 1)
        nc.vector.tensor_tensor(row_max[:, half, :], part_max[:, half, 0, :], part_max[:, half, 1, :],
                                ALU.max).then_inc(att["m_rows"], 1)


def stack_max(sp, held, att, n, r, half):
    sp.wait_ge(att["m_read"], n * USES + ROWS_AT[half] + 1)
    sp.sem_inc(held, 1)
    sp.dma_start(att["q"][r][ROWS:ROWS + 1, half, :, :].bitcast(F32).rearrange("o a t -> o (a t)"),
                 att["neg_max"][:, half, :].bitcast(F32)).then_inc(att["m_stacked"][half], 16)


def project_block(nc, sem, held, t, w, x_v, x_in, x_loaded, att, grouped, scratch):
    qh_d, ql_d, kh_d, kl_d, v_d = scratch
    ITEMS = [("q", 1), ("q", 2), ("q", 3), ("k", 1), ("k", 2), ("k", 3), ("q", 0), ("k", 0)] + [("v", s) for s in range(TPC)]
    NI = len(ITEMS)
    STORED = 2 * FC
    PLAIN = STORED - 2
    RING = 4
    TR = 2
    TURNS = {3: (0, 1), 5: (2, 3)}
    with ExitStack() as ctx:
        def sb(name, shape, dt=F32):
            return ctx.enter_context(nc.sbuf_tensor(name, shape, dt))

        xT_hi = [sb(f"xT_hi{i}", [P, FC, CH], F32R) for i in range(2)]
        xT_lo = [sb(f"xT_lo{i}", [P, FC, CH], F32R) for i in range(2)]
        stats = sb("ln_stats", [P, TPC, 6])
        mv = sb("ln_mv", [P, TPC, 2])
        rstd = sb("ln_rstd", [P, TPC])
        minus_half = sb("ln_minus_half", [P, TPC])
        y_rot = sb("y_rot", [2 * HD, CH])
        y_swap = sb("y_swap", [2 * HD, CH])
        y_cos = sb("y_cos", [2 * HD, CH])
        y_sum = sb("y_sum", [P, 2, CH])
        g0 = sb("group0", [P, 2, CH])
        st_hi = sb("st_hi", [P, RING, CH], F32R)
        st_lo = sb("st_lo", [P, RING, CH], F32R)
        st_v = sb("st_v", [P, TPC, D])
        ps_t = [ctx.enter_context(nc.psum_tensor(f"ps_t{i}", [P, CH], F32)) for i in range(TR)]
        ps_m = ps_t + [ctx.enter_context(nc.psum_tensor("ps_m_first", [P, CH], F32))]
        ps_r = ctx.enter_context(nc.psum_tensor("ps_r", [P, CH], F32))
        ps_p = [ctx.enter_context(nc.psum_tensor(f"ps_p{i}", [P, CH], F32)) for i in range(RING)]

        ln_step = sem("ln_step")
        rstd_done = sem("rstd_done")
        normed = sem("normed")
        transposed = sem("transposed")
        xhi_done = sem("xhi_done")
        xlo_done = sem("xlo_done")
        rot_proj = sem("rot_proj")
        proj = sem("proj")
        half_set = sem("half_set")
        rot_zero = sem("rot_zero")
        rot_y = sem("rot_y")
        rot_swap = sem("rot_swap")
        rot_mul = sem("rot_mul")
        rot_sum = sem("rot_sum")
        g0_done = sem("g0_done")
        hi_done = sem("hi_done")
        lo_done = sem("lo_done")
        v_done = sem("v_done")
        stored = [sem(f"stored{i}") for i in range(RING)]
        v_stored = [sem(f"v_stored{i}") for i in range(TPC)]
        block = ctx.enter_context(nc.Block())
        last_i = B - 1

        @block.sync
        def _(sp):
            def body(i, last):
                if last:
                    for s_ in stored:
                        sp.wait_ge(s_, 32 * CPB * STORED // RING)
                    for s_ in v_stored:
                        sp.wait_ge(s_, 16 * CPB)
                    load_group(sp, att, grouped, 0, 0)
                for par in range(CPB):
                    c = i * CPB + par
                    if not last:
                        sp.wait_ge(transposed, c * FC + FC)
                        sp.sem_inc(held, 1)
                        sp.dma_start(x_in[par][:], x_v[i + 1, par]).then_inc(x_loaded[par], 16)
                    cs = slice(par * CH, (par + 1) * CH)
                    for n in range(STORED):
                        sp.wait_ge(lo_done, c * STORED + n + 1)
                        sp.sem_inc(held, 1)
                        g = ITEMS[n][1]
                        is_q = ITEMS[n][0] == "q"
                        dh, dl = (qh_d, ql_d) if is_q else (kh_d, kl_d)
                        sp.dma_start(dh[i, g, :, cs], st_hi[:, n % RING, :].bitcast(F32)).then_inc(stored[n % RING], 16)
                        sp.dma_start(dl[i, g, :, cs], st_lo[:, n % RING, :].bitcast(F32)).then_inc(stored[n % RING], 16)
                    for s in range(TPC):
                        sp.wait_ge(v_done, c * TPC + s + 1)
                        sp.sem_inc(held, 1)
                        sp.dma_start(v_d[i, :, :, par * TPC + s, :].rearrange("g p d -> p g d"),
                                     st_v[:, s, :].rearrange("p (g d) -> p g d", g=FC)).then_inc(v_stored[s], 16)
                        if last and par == CPB - 1 and s == 0:
                            stack_max(sp, held, att, 0, 0, 0)

            body(0, False)
            with sp.Fori(1, last_i) as i:
                body(i, False)
            body(last_i, True)
            stack_max(sp, held, att, 0, 0, 1)
            for half in range(2):
                sp.wait_ge(att["m_stacked"][half], 16)
            for s in stored:
                sp.wait_ge(s, 32 * B * CPB * STORED // RING)
            for s in v_stored:
                sp.wait_ge(s, 16 * B * CPB)

        @block.tensor
        def _(pe):
            def transpose(c, par, f):
                if f == 0:
                    pe.wait_ge(normed, c + 1)
                if f >= TR:
                    pe.wait_ge(xlo_done, c * FC + f - TR + 1)
                elif not is_first(c):
                    pe.wait_ge(xlo_done, (c - 1) * FC + FC - TR + f + 1)
                for s in range(TPC):
                    m = nc.tensor.transpose(ps_t[f % TR][:, s * P:(s + 1) * P], x_in[par][:, s, f * P:(f + 1) * P], t["ident"][:])
                m.then_inc(transposed, 1)

            def features(out, par, k, ws, between):
                hi, lo, wh, wl = xT_hi[par], xT_lo[par], w[k + "_hi"], w[k + "_lo"]
                for f in range(FC):
                    nc.tensor.matmul(out, wh[:, f, ws], hi[:, f, :], start=f == 0, stop=False)
                    nc.tensor.matmul(out, wh[:, f, ws], lo[:, f, :], start=False, stop=False)
                    m = nc.tensor.matmul(out, wl[:, f, ws], hi[:, f, :], start=False, stop=f == FC - 1)
                    if f < FC - 1:
                        between()
                return m

            def rotated(c, par, between):
                if not is_first(c):
                    pe.wait_ge(rot_y, c)
                features(ps_r[:, :], par, "rot", slice(0, P), between).then_inc(rot_proj, 1)

            def item(c, par, n, between):
                kind, g = ITEMS[n]
                if n < RING:
                    if not is_first(c):
                        pe.wait_ge(v_done, (c - 1) * TPC + n + 1)
                elif n < RING + PLAIN:
                    pe.wait_ge(lo_done, c * STORED + n - RING + 1)
                else:
                    pe.wait_ge(g0_done, c * 2 + n - RING - PLAIN + 1)
                out = ps_p[n % RING][:, :]
                if kind == "v":
                    hi, lo, ts_ = xT_hi[par], xT_lo[par], slice(g * P, (g + 1) * P)
                    for f in range(FC):
                        nc.tensor.matmul(out, hi[:, f, ts_], w["v_hi"][:, f, :], start=f == 0, stop=False)
                        nc.tensor.matmul(out, hi[:, f, ts_], w["v_lo"][:, f, :], start=False, stop=False)
                        m = nc.tensor.matmul(out, lo[:, f, ts_], w["v_hi"][:, f, :], start=False, stop=f == FC - 1)
                        if f < FC - 1:
                            between()
                else:
                    m = features(out, par, kind, slice(g * P, (g + 1) * P), between)
                m.then_inc(proj, 1)

            def body(i, last):
                for par in range(CPB):
                    c = i * CPB + par
                    pe.wait_ge(xlo_done, c * FC + FC)
                    todo = list(range(USES - 1)) if last and par == CPB - 1 else []

                    def maxima(count):
                        for _ in range(count if todo else 0):
                            max_product(nc, pe, att, ps_m, t["ident"], 0, 0, 1, todo.pop(0))

                    rotated(c, par, lambda: maxima(1))
                    maxima(2)
                    for n in range(NI):
                        item(c, par, n, lambda: maxima(1))
                        maxima(2)
                        if not (last and par == CPB - 1):
                            for f in TURNS.get(n, ()):
                                transpose(c + 1, 1 - par, f)

            for f in range(FC):
                transpose(0, 0, f)
            body(0, False)
            with pe.Fori(1, last_i) as i:
                body(i, False)
            body(last_i, True)
            max_product(nc, pe, att, ps_m, t["ident"], 0, 0, 1, USES - 1)

        @block.scalar
        def _(act):
            def x_hi(c, par, f):
                act.wait_ge(transposed, c * FC + f + 1)
                if f == 0 and not (type(c) is int and c < CPB):
                    act.wait_ge(proj, (c - CPB) * NI + NI)
                nc.scalar.copy(xT_hi[par][:, f, :], ps_t[f % TR][:, :]).then_inc(xhi_done, 1)

            def rot(c):
                act.wait_ge(rot_proj, c + 1)
                if not is_first(c):
                    act.wait_ge(rot_mul, c)
                nc.scalar.activation(y_rot[:, :], ps_r[0:2 * HD, :], ACT.Identity, bias=t["br"][:, 0:1]).then_inc(rot_y, 1)

            def high(c, n):
                kind, g = ITEMS[n]
                act.wait_ge(proj, c * NI + n + 1)
                if n >= RING or not is_first(c):
                    act.wait_ge(stored[n % RING], 32 * (c * (STORED // RING) + n // RING))
                bias = t["bq"] if kind == "q" else t["bk"]
                nc.scalar.activation(st_hi[:, n % RING, :], ps_p[n % RING][:, :], ACT.Identity,
                                     bias=bias[:, g:g + 1]).then_inc(hi_done, 1)

            def body(i, last):
                for par in range(CPB):
                    c = i * CPB + par
                    rot(c)
                    for n in range(PLAIN):
                        high(c, n)
                        if not (last and par == CPB - 1):
                            for f in TURNS.get(n, ()):
                                x_hi(c + 1, 1 - par, f)
                    for k in range(2):
                        n = PLAIN + k
                        act.wait_ge(g0_done, c * 2 + k + 1)
                        act.wait_ge(stored[n % RING], 32 * (c * (STORED // RING) + n // RING))
                        nc.scalar.copy(st_hi[:, n % RING, :], g0[:, k, :]).then_inc(hi_done, 1)

            for f in range(FC):
                x_hi(0, 0, f)
            body(0, False)
            with act.Fori(1, last_i) as i:
                body(i, False)
            body(last_i, True)

        @block.gpsimd
        def _(pool):
            nc.gpsimd.memset(minus_half[:], -0.5).then_inc(half_set, 1)
            pool.wait_ge(half_set, 1)

            def inv_std(c):
                pool.wait_ge(ln_step, c * 3 + 3)
                nc.gpsimd.tensor_tensor(rstd[:, :], rstd[:, :], minus_half[:, :], ALU.pow).then_inc(rstd_done, 1)

            nc.gpsimd.memset(y_sum[:], 0.0).then_inc(rot_zero, 1)
            pool.wait_ge(rot_zero, 1)

            def body(i, last):
                for par in range(CPB):
                    c = i * CPB + par
                    cs = slice(par * CH, (par + 1) * CH)
                    pool.wait_ge(rot_swap, c + 1)
                    nc.gpsimd.tensor_tensor(y_cos[:, :], y_rot[:, :], t["cos"][:, cs], ALU.mult)
                    nc.gpsimd.tensor_tensor(y_swap[:, :], y_swap[:, :], t["sin"][:, cs], ALU.mult).then_inc(rot_mul, 1)
                    pool.wait_ge(rot_mul, c + 1)
                    if not is_first(c):
                        pool.wait_ge(g0_done, c * 2)
                    for k in range(2):
                        rows = slice(k * HD, (k + 1) * HD)
                        p_ = nc.gpsimd.tensor_tensor(y_sum[0:HD, k, :], y_cos[rows, :], y_swap[rows, :], ALU.add)
                        p_.then_inc(rot_sum, 1)
                        pool.wait_ge(rot_sum, c * 2 + k + 1)
                    if not (last and par == CPB - 1):
                        inv_std(c + 1)

            inv_std(0)
            body(0, False)
            with pool.Fori(1, last_i) as i:
                body(i, False)
            body(last_i, True)

        @block.vector
        def _(dve):
            def norm(c, par, loads):
                dve.wait_ge(x_loaded[par], 16 * loads)
                x = x_in[par]
                for s in range(TPC):
                    v = nc.vector.bn_stats(stats[:, s, :], x[:, s, :])
                v.then_inc(ln_step, 1)
                dve.wait_ge(ln_step, c * 3 + 1)
                dve.sem_inc(held, 1)
                for s in range(TPC):
                    v = nc.vector.bn_aggr(mv[:, s, :], stats[:, s, :])
                v.then_inc(ln_step, 1)
                dve.wait_ge(ln_step, c * 3 + 2)
                nc.vector.tensor_scalar(rstd[:, :], mv[:, :, 1], EPS, None, ALU.add).then_inc(ln_step, 1)
                dve.wait_ge(rstd_done, c + 1)
                for s in range(TPC):
                    v = nc.vector.tensor_scalar(x[:, s, :], x[:, s, :], mv[:, s, 0:1], rstd[:, s:s + 1],
                                                ALU.subtract, ALU.mult)
                v.then_inc(normed, 1)

            def x_lo(c, par, f):
                dve.wait_ge(xhi_done, c * FC + f + 1)
                nc.vector.tensor_tensor(xT_lo[par][:, f, :], ps_t[f % TR][:, :], xT_hi[par][:, f, :],
                                        ALU.subtract).then_inc(xlo_done, 1)

            def low(c, n):
                kind, g = ITEMS[n]
                bias = t["bq"] if kind == "q" else t["bk"]
                dve.wait_ge(hi_done, c * STORED + n + 1)
                nc.vector.scalar_tensor_tensor(st_lo[:, n % RING, :], ps_p[n % RING][:, :], bias[:, g:g + 1],
                                               st_hi[:, n % RING, :], ALU.add, ALU.subtract).then_inc(lo_done, 1)

            def group0_sum(c, k):
                n = PLAIN + k
                bias = t["bq"] if k == 0 else t["bk"]
                dve.wait_ge(proj, c * NI + n + 1)
                dve.wait_ge(rot_sum, c * 2 + k + 1)
                if not is_first(c):
                    dve.wait_ge(lo_done, (c - 1) * STORED + n + 1)
                nc.vector.scalar_tensor_tensor(g0[:, k, :], ps_p[n % RING][:, :], bias[:, 0:1],
                                               y_sum[:, k, :], ALU.add, ALU.add).then_inc(g0_done, 1)

            def group0_low(c, k):
                n = PLAIN + k
                dve.wait_ge(hi_done, c * STORED + n + 1)
                nc.vector.tensor_tensor(st_lo[:, n % RING, :], g0[:, k, :], st_hi[:, n % RING, :],
                                        ALU.subtract).then_inc(lo_done, 1)

            def v_tile(c, s):
                n = STORED + s
                dve.wait_ge(proj, c * NI + n + 1)
                if not is_first(c):
                    dve.wait_ge(v_stored[s], 16 * c)
                nc.vector.tensor_tensor(st_v[:, s, :], ps_p[n % RING][:, :], t["bv"][:, :],
                                        ALU.add).then_inc(v_done, 1)

            def after(c, n):
                if n < PLAIN:
                    low(c, n)
                elif n < STORED:
                    group0_sum(c, n - PLAIN)
                else:
                    if n == STORED:
                        group0_low(c, 0)
                        group0_low(c, 1)
                    v_tile(c, n - STORED)

            def body(i, last):
                for par in range(CPB):
                    c = i * CPB + par
                    more = not (last and par == CPB - 1)
                    dve.wait_ge(rot_y, c + 1)
                    if not is_first(c):
                        dve.wait_ge(rot_sum, c * 2)
                    dve.sem_inc(held, 1)
                    nc.vector.stream_shuffle(y_swap[:, :], y_rot[:, :], SWAP).then_inc(rot_swap, 1)
                    if more:
                        norm(c + 1, 1 - par, i + 1 + par)
                    if last and par == CPB - 1:
                        per = FC + 1
                        for n in range(-1, NI):
                            uses = range((n + 1) * per, (n + 2) * per)
                            for u in uses[:2]:
                                max_reduce(nc, dve, att, ps_m, 0, u)
                            if n >= 1:
                                after(c, n - 1)
                            for u in uses[2:]:
                                max_reduce(nc, dve, att, ps_m, 0, u)
                        after(c, NI - 1)
                        max_reduce(nc, dve, att, ps_m, 0, USES - 1)
                        return
                    for n in range(NI):
                        after(c, n)
                        for f in TURNS.get(n, ()):
                            x_lo(c + 1, 1 - par, f)

            norm(0, 0, 1)
            for f in range(FC):
                x_lo(0, 0, f)
            body(0, False)
            with dve.Fori(1, last_i) as i:
                body(i, False)
            body(last_i, True)


def attend_block(nc, sem, held, t, att, scratch, o_d, l_d):
    UNITS = NQ * KT
    TILES = HG * UNITS
    SR = 3
    PR = 4
    PAIRS = KT // 2
    ADDS = PAIRS + 1
    SUMS = 2
    PAIR_ADDED = [w + 1 if w < 2 else w + 2 for w in range(PAIRS)]
    SUM_AT = {0: 0, 6: 1}
    QUAD_AT = (9, 14, 19, 23)
    with ExitStack() as ctx:
        def sb(name, shape, dt=F32):
            return ctx.enter_context(nc.sbuf_tensor(name, shape, dt))

        for r in range(1, R3):
            group_buffers(att, sb, r)
        qs, ks, vt, ones = att["q"], att["k"], att["v"], att["ones"]
        loaded, v_loaded, m_scored, m_read, m_stacked = (att[k] for k in ("loaded", "v_loaded", "m_scored", "m_read", "m_stacked"))
        probs = sb("probs", [P, PR, HG, CH])
        pairs = sb("pairs", [P, PAIRS, HG, CH])
        o_sb = sb("o_sb", [P, NQ, CH])
        l_sb = sb("l_sb", [P, NQ, CH])
        ps_s = [ctx.enter_context(nc.psum_tensor(f"ps_s{i}", [P, CH], F32)) for i in range(SR)]
        ps_m = [ctx.enter_context(nc.psum_tensor(f"ps_m{i}", [P, CH], F32)) for i in range(MR)]
        ps_o = ctx.enter_context(nc.psum_tensor("ps_o", [P, CH], F32))
        ps_l = ctx.enter_context(nc.psum_tensor("ps_l", [P, CH], F32))

        rows_set = sem("rows_set")
        scored = sem("scored")
        exped = sem("exped")
        pv_done = sem("pv_done")
        pair_done = sem("pair_done")
        quad_done = sem("quad_done")
        sum_done = sem("sum_done")
        o_out = sem("o_out")
        l_out = sem("l_out")
        o_stored = [sem(f"o_stored{q}") for q in range(NQ)]
        l_stored = [sem(f"l_stored{q}") for q in range(NQ)]
        block = ctx.enter_context(nc.Block())

        STEPS = NG // R3
        REST = NG - STEPS * R3

        def rounds(eng, step):
            for r in range(R3):
                step(0, r, r)
            with eng.Fori(1, STEPS) as i:
                for r in range(R3):
                    step(i, r, i * R3 + r)
            for r in range(REST):
                step(STEPS, r, STEPS * R3 + r)

        def is_last(n):
            return type(n) is int and n == NG - 1

        assert R3 * TILES % SR == 0 and USES % MR == 0

        def bank(r, e):
            return (r * TILES + e) % SR

        @block.sync
        def _(sp):
            def store_o(n, qc):
                sp.wait_ge(o_out, n * NQ + qc + 1)
                sp.sem_inc(held, 1)
                sp.dma_start(o_d[n, :, qc * CH:(qc + 1) * CH], o_sb[:, qc, :]).then_inc(o_stored[qc], 16)

            def store_l(n, qc):
                sp.wait_ge(l_out, n * NQ + qc + 1)
                sp.sem_inc(held, 1)
                sp.dma_start(l_d[n, :, qc * CH:(qc + 1) * CH], l_sb[0:P - HD + 1:HD, qc, :]).then_inc(l_stored[qc], 16)

            def step(i, r, n):
                if not (type(n) is int and n + 2 >= NG):
                    if not is_first(n):
                        sp.wait_ge(pv_done, n * UNITS)
                        sp.sem_inc(held, 1)
                    load_group(sp, att, scratch, n + 2, (r + 2) % R3)
                if not is_first(n):
                    store_o(n - 1, 1)
                    store_l(n - 1, 1)
                if not is_last(n):
                    stack_max(sp, held, att, n + 1, (r + 1) % R3, 0)
                store_o(n, 0)
                store_l(n, 0)
                if not is_last(n):
                    stack_max(sp, held, att, n + 1, (r + 1) % R3, 1)

            load_group(sp, att, scratch, 1, 1)
            for r in range(1, R3):
                sp.dma_start(ks[r][ROWS:ROWS + 1, :, :].bitcast(F32),
                             ks[0][ROWS:ROWS + 1, :, :].bitcast(F32)).then_inc(rows_set, 16)
            rounds(sp, step)
            store_o(NG - 1, 1)
            store_l(NG - 1, 1)
            for s in o_stored + l_stored:
                sp.wait_ge(s, 16 * NG)

        SPREAD = [(1, 1, 2, 1, 0) if u % KT == 6 else (1, 1, 1, 1, 0) for u in range(UNITS)]
        SPREAD[UNITS - 1] = (1, 1, 1, 0, 1)
        SPREAD_FIRST = [(0,) * 5 if u < UNITS // 4 else (1, 1, 2, 1, 1) if u % 2 else (1,) * 5 for u in range(UNITS)]
        assert sum(map(sum, SPREAD)) == sum(map(sum, SPREAD_FIRST)) == USES

        @block.tensor
        def _(pe):
            def scores(n, r, u, a):
                qc, kt = divmod(u, KT)
                e = HG * u + a
                if u == 0 and a == 0 and type(n) is int and n == 1:
                    pe.wait_ge(rows_set, 16 * (R3 - 1))
                if kt == 0 and a == 0:
                    pe.wait_ge(m_stacked[qc], 16 * (n + 1))
                if e >= SR or not is_first(n):
                    pe.wait_ge(exped, n * TILES + e - SR + 1)
                nc.tensor.matmul(ps_s[bank(r, e)][:, :], ks[r][:, a, kt * P:(kt + 1) * P],
                                 qs[r][:, qc, a, :], start=True, stop=True).then_inc(scored, 1)

            def pv(n, i, r, u):
                qc, kt = divmod(u, KT)
                if u == 0:
                    pe.wait_ge(v_loaded[r], 16 * (i + 1))
                if kt == 0 and not (is_first(n) and qc == 0):
                    pe.wait_ge(o_out, n * NQ + qc)
                pe.wait_ge(exped, n * TILES + HG * u + HG)
                for a in range(HG):
                    m = nc.tensor.matmul(ps_o[a * HD:(a + 1) * HD, :], vt[r][:, kt, a * HD:(a + 1) * HD],
                                         probs[:, u % PR, a, :], start=kt == 0, stop=kt == KT - 1)
                m.then_inc(pv_done, 1)

            def sums(n, qc, w):
                c = n * NQ + qc
                if w == 0:
                    if not (is_first(n) and qc == 0):
                        pe.wait_ge(l_out, c)
                    pe.wait_ge(pair_done, c * ADDS + 3)
                else:
                    pe.wait_ge(quad_done, c * HG + HG)
                for a in range(HG):
                    m = nc.tensor.matmul(ps_l[a * HD:(a + 1) * HD, :], ones[:, :], pairs[:, 2 * w + 1, a, :],
                                         start=w == 0, stop=w == SUMS - 1)
                m.then_inc(sum_done, 1)

            def step(i, r, n):
                r1 = (r + 1) % R3
                i1 = i + 1 if r1 == 0 else i
                todo = [] if is_last(n) else list(range(USES))
                spread = SPREAD_FIRST if is_first(n) else SPREAD

                def maxima(count):
                    for _ in range(count if todo else 0):
                        max_product(nc, pe, att, ps_m, t["ident"], n + 1, r1, i1 + 1, todo.pop(0))

                for u in range(UNITS):
                    qc, kt = divmod(u, KT)
                    for a in range(HG):
                        if a == HG // 2 and kt in SUM_AT:
                            if qc > 0:
                                sums(n, qc - 1, SUM_AT[kt])
                            elif not is_first(n):
                                sums(n - 1, NQ - 1, SUM_AT[kt])
                        maxima(spread[u][a])
                        scores(n, r, u, a)
                    if u >= 1:
                        pv(n, i, r, u - 1)
                    elif not is_first(n):
                        pv(n - 1, i if r else i - 1, (r - 1) % R3, UNITS - 1)
                    maxima(spread[u][HG])
                if is_last(n):
                    pv(n, i, r, UNITS - 1)
                    for w in range(SUMS):
                        sums(n, NQ - 1, w)

            pe.wait_ge(att["ones_done"], 1)
            rounds(pe, step)

        @block.scalar
        def _(act):
            def take(n, qc, src, dst, ready, count, stored, out):
                act.wait_ge(ready, count)
                if not is_first(n):
                    act.wait_ge(stored[qc], 16 * n)
                nc.scalar.copy(dst[:, qc, :], src[:, :]).then_inc(out, 1)

            def take_o(n, qc):
                take(n, qc, ps_o, o_sb, pv_done, n * UNITS + (qc + 1) * KT, o_stored, o_out)

            def take_l(n, qc):
                take(n, qc, ps_l, l_sb, sum_done, (n * NQ + qc + 1) * SUMS, l_stored, l_out)

            def step(i, r, n):
                for u in range(UNITS):
                    if u == KT + 1:
                        take_o(n, 0)
                    if u == KT + KT - 1:
                        take_l(n, 0)
                    if u == 1 and not is_first(n):
                        take_o(n - 1, 1)
                    if u == KT - 1 and not is_first(n):
                        take_l(n - 1, 1)
                    for a in range(HG):
                        if a == 0 and (u >= PR or not is_first(n)):
                            act.wait_ge(pv_done, n * UNITS + u - PR + 1)
                            if u % 2 == 0:
                                qc, kt = divmod(u - PR, KT)
                                act.wait_ge(pair_done, (n * NQ + qc) * ADDS + PAIR_ADDED[kt // 2])
                        act.wait_ge(scored, n * TILES + HG * u + a + 1)
                        nc.scalar.activation(probs[:, u % PR, a, :], ps_s[bank(r, HG * u + a)][:, :], ACT.Exp,
                                             scale=SCALE).then_inc(exped, 1)
                if is_last(n):
                    take_o(n, 1)
                    take_l(n, 1)

            rounds(act, step)

        @block.gpsimd
        def _(pool):
            def step(i, r, n):
                for qc in range(NQ):
                    c = n * NQ + qc
                    for w in range(PAIRS):
                        if not (is_first(n) and qc == 0):
                            if w == 2:
                                pool.wait_ge(quad_done, c * HG)
                            else:
                                pool.wait_ge(sum_done, (c - 1) * SUMS + w // 2 + 1)
                        pool.wait_ge(exped, n * TILES + HG * (qc * KT + 2 * w + 2))
                        u = qc * KT + 2 * w
                        nc.gpsimd.tensor_tensor(pairs[:, w, :, :], probs[:, u % PR, :, :],
                                                probs[:, (u + 1) % PR, :, :], ALU.add).then_inc(pair_done, 1)
                        if w == 1:
                            pool.wait_ge(pair_done, c * ADDS + 2)
                            nc.gpsimd.tensor_tensor(pairs[:, 1, :, :], pairs[:, 0, :, :], pairs[:, 1, :, :],
                                                    ALU.add).then_inc(pair_done, 1)

            rounds(pool, step)

        @block.vector
        def _(dve):
            def quad(c, a):
                if a == 0:
                    dve.wait_ge(pair_done, c * ADDS + ADDS)
                nc.vector.tensor_tensor(pairs[:, 3, a, :], pairs[:, 2, a, :], pairs[:, 3, a, :], ALU.add).then_inc(quad_done, 1)

            def step(i, r, n):
                for u in range(USES):
                    qc, at = divmod(u, USES // 2)
                    if at in QUAD_AT and not (is_first(n) and qc == 0):
                        quad(n * NQ + qc - 1, QUAD_AT.index(at))
                    if not is_last(n):
                        max_reduce(nc, dve, att, ps_m, n + 1, u)
                if is_last(n):
                    for a in range(HG):
                        quad(NG * NQ - 1, a)

            rounds(dve, step)


def mix_block(nc, sem, held, t, x_d, o_d, l_d, inv_d, wo_d, wr_d, wk_d, wv_d, bo_d, mur_d, muk_d, out_d):
    RELU = 2
    with ExitStack() as ctx:
        def sb(name, shape, dt=F32):
            return ctx.enter_context(nc.sbuf_tensor(name, shape, dt))

        w_hi = {k: sb(f"mix_w_{k}_hi", [P, FC, D], F32R) for k in "okrv"}
        w_lo = {k: sb(f"mix_w_{k}_lo", [P, FC, D], F32R) for k in "okrv"}
        bo = sb("bo", [P, D])
        mu_r = sb("mu_r", [P, FC])
        mu_k = sb("mu_k", [P, FC])
        x_in = sb("mix_x_in", [P, TPC, D])
        xs = [sb(f"xs{i}", [P, TPC, D]) for i in range(2)]
        o_in = sb("o_in", [P, FC, CH])
        o_hi = sb("o_hi", [P, FC, CH], F32R)
        o_lo = sb("o_lo", [P, FC, CH], F32R)
        xT = [sb(f"xT{i}", [P, FC, CH + 1]) for i in range(2)]
        diff = sb("diff", [P, FC, CH])
        mixed = sb("mixed", [P, FC, CH])
        xn = mixed[:].rearrange("p f t -> p (f t)").rearrange("p (s d) -> p s d", s=TPC)
        xk_hi = sb("xk_hi", [P, FC, CH], F32R)
        xk_lo = sb("xk_lo", [P, FC, CH], F32R)
        xr_hi = sb("xr_hi", [P, FC, CH], F32R)
        xr_lo = sb("xr_lo", [P, FC, CH], F32R)
        relu = sb("relu", [P, RELU, CH])
        ka_hi = sb("ka_hi", [P, FC, CH], F32R)
        ka_lo = sb("ka_lo", [P, FC, CH], F32R)
        gate = sb("gate", [P, TPC, D])
        stats = sb("mix_stats", [P, TPC, 6])
        mv = sb("mix_mv", [P, TPC, 2])
        rstd = sb("mix_rstd", [P, TPC])
        minus_half = sb("mix_minus_half", [P, TPC])
        ps_t = [ctx.enter_context(nc.psum_tensor(f"mix_t{i}", [P, CH], F32)) for i in range(FC)]
        ps_p = [ctx.enter_context(nc.psum_tensor(f"mix_p{i}", [P, CH], F32)) for i in range(TPC)]

        w_loaded = {k: sem(f"w_loaded_{k}") for k in "okrv"}
        small_loaded = sem("small_loaded")
        w_split_hi = sem("w_split_hi")
        w_split_lo = sem("w_split_lo")
        l_loaded = sem("l_loaded")
        inv_done = sem("inv_done")
        inv_stored = sem("inv_stored")
        x_loaded = sem("mix_x_loaded")
        o_loaded = sem("mix_o_loaded")
        inv_loaded = sem("inv_loaded")
        o_div = sem("o_div")
        oh_done = sem("oh_done")
        ol_done = sem("ol_done")
        xb_done = sem("xb_done")
        wo_done = sem("wo_done")
        x1_done = sem("x1_done")
        ln_step = sem("mix_ln_step")
        rstd_done = sem("mix_rstd_done")
        normed = sem("mix_normed")
        transposed = sem("mix_transposed")
        xT_done = sem("xT_done")
        half_set = sem("mix_half_set")
        zero_done = sem("zero_done")
        edge_done = sem("edge_done")
        diff_done = sem("diff_done")
        xk_done = sem("xk_done")
        xkh_done = sem("xkh_done")
        xkl_done = sem("xkl_done")
        xr_done = sem("xr_done")
        xrh_done = sem("xrh_done")
        xrl_done = sem("xrl_done")
        k_done = sem("k_done")
        relu_done = sem("relu_done")
        sq_done = sem("sq_done")
        kah_done = sem("kah_done")
        kal_done = sem("kal_done")
        r_done = sem("r_done")
        gate_done = sem("gate_done")
        v_done = sem("mix_v_done")
        gated = sem("gated")
        out_done = sem("out_done")
        out_stored = sem("out_stored")
        block = ctx.enter_context(nc.Block())
        x_v = x_d.rearrange("b (h s p) d -> b h p s d", h=CPB, p=P)
        out_v = out_d.rearrange("b (h s p) d -> b h p s d", h=CPB, p=P)
        o_v = o_d.rearrange("(b g) p t -> b p g t", g=FC)
        ORDER = "okrv"
        staging = {"o": x_in, "k": xs[1], "r": diff, "v": mixed}
        SC = H * S // P
        sums = gate[:].rearrange("p s d -> p (s d)")[:, 0:B * SC].rearrange("p (b c) -> p b c", b=B)
        inv = relu[:].rearrange("p r t -> p (r t)")[:, 0:B * SC].rearrange("p (b c) -> p b c", b=B)

        def by_batch(a):
            return a.rearrange("(b h) t -> b (h t)", b=B).rearrange("b (p c) -> p b c", p=P)

        inv_v = inv_d.rearrange("(b g a) t -> b g a t", g=FC, a=HG)
        last_i = B - 1

        def chunks(eng, body):
            body(0, False)
            with eng.Fori(1, last_i) as i:
                body(i, False)
            body(last_i, True)

        @block.sync
        def _(sp):
            def load_o(b, par, o_too=True):
                cs = slice(par * CH, (par + 1) * CH)
                if o_too:
                    sp.dma_start(o_in[:], o_v[b, :, :, cs]).then_inc(o_loaded, 16)
                for a in range(HG):
                    sp.dma_start(o_lo[a * HD:(a + 1) * HD, :, :].bitcast(F32),
                                 inv_v[b, :, a, cs].rearrange("(o g) t -> o g t", o=1).broadcast_to([HD, FC, CH])
                                 ).then_inc(inv_loaded, 16)

            sp.dma_start(sums, by_batch(l_d)).then_inc(l_loaded, 16)
            sp.dma_start(o_in[:], o_v[0, :, :, 0:CH]).then_inc(o_loaded, 16)
            sp.wait_ge(inv_done, 1)
            sp.dma_start(by_batch(inv_d)[:, 0:1, :], inv[:, 0:1, :]).then_inc(inv_stored, 16)
            for k, src in zip(ORDER, (wo_d, wk_d, wr_d, wv_d)):
                sp.dma_start(staging[k][:], src.rearrange("(c p) n -> p c n", p=P)).then_inc(w_loaded[k], 16)
                if k == "o":
                    sp.wait_ge(inv_stored, 16)
                    load_o(0, 0, o_too=False)
                    sp.dma_start(bo[:], bo_d.rearrange("(a n) -> a n", a=1).broadcast_to([P, D])).then_inc(small_loaded, 16)
                    sp.dma_start(mu_r[:], mur_d).then_inc(small_loaded, 16)
                    sp.dma_start(mu_k[:], muk_d).then_inc(small_loaded, 16)
                    sp.wait_ge(w_split_lo, 1)
                    sp.dma_start(x_in[:], x_v[0, 0]).then_inc(x_loaded, 16)
            sp.wait_ge(wo_done, TPC)
            load_o(0, 1)
            sp.wait_ge(xb_done, TPC)
            sp.dma_start(x_in[:], x_v[0, 1]).then_inc(x_loaded, 16)
            sp.wait_ge(inv_done, 2)
            sp.dma_start(by_batch(inv_d)[:, 1:B, :], inv[:, 1:B, :]).then_inc(inv_stored, 16)
            sp.wait_ge(inv_stored, 32)

            def body(i, last):
                for par in range(CPB):
                    c = i * CPB + par
                    if not last:
                        sp.wait_ge(wo_done, c * TPC + 2 * TPC)
                        sp.sem_inc(held, 1)
                        load_o(i + 1, par)
                        sp.wait_ge(xb_done, c * TPC + 2 * TPC)
                        sp.sem_inc(held, 1)
                        sp.dma_start(x_in[:], x_v[i + 1, par]).then_inc(x_loaded, 16)
                    sp.wait_ge(out_done, c * TPC + TPC)
                    sp.sem_inc(held, 1)
                    sp.dma_start(out_v[i, par], gate[:]).then_inc(out_stored, 16)

            chunks(sp, body)
            sp.wait_ge(out_stored, 16 * B * CPB)

        @block.tensor
        def _(pe):
            def product(out, stat_hi, stat_lo, mov_hi, mov_lo):
                for f in range(FC):
                    nc.tensor.matmul(out, stat_hi(f), mov_hi(f), start=f == 0, stop=False)
                    nc.tensor.matmul(out, stat_hi(f), mov_lo(f), start=False, stop=False)
                    m = nc.tensor.matmul(out, stat_lo(f), mov_hi(f), start=False, stop=f == FC - 1)
                return m

            def by_token(s, hi, lo, k):
                ts_ = slice(s * P, (s + 1) * P)
                return product(ps_p[s][:, :], lambda f: hi[:, f, ts_], lambda f: lo[:, f, ts_],
                               lambda f: w_hi[k][:, f, :], lambda f: w_lo[k][:, f, :])

            def project(c):
                pe.wait_ge(ol_done, c + 1)
                for s in range(TPC):
                    if type(c) is not int or c >= 2:
                        pe.wait_ge(gated, (c - 2) * TPC + s + 1)
                    by_token(s, o_hi, o_lo, "o").then_inc(wo_done, 1)

            def transposes(c):
                pe.wait_ge(normed, c + 1)
                for f in range(FC):
                    if not is_first(c):
                        pe.wait_ge(xT_done, (c - 1) * FC + f + 1)
                    for s in range(TPC):
                        m = nc.tensor.transpose(ps_t[f][:, s * P:(s + 1) * P], xn[:, s, f * P:(f + 1) * P], t["ident"][:])
                    m.then_inc(transposed, 1)

            def body(i, last):
                for par in range(CPB):
                    c = i * CPB + par
                    more = not (last and par == CPB - 1)
                    if more:
                        project(c + 1)
                    pe.wait_ge(xkl_done, c + 1)
                    for g in range(FC):
                        if more:
                            pe.wait_ge(x1_done, (c + 1) * TPC + g + 1)
                        else:
                            pe.wait_ge(gated, (c - 1) * TPC + g + 1)
                        gs = slice(g * P, (g + 1) * P)
                        product(ps_p[g][:, :], lambda f: w_hi["k"][:, f, gs], lambda f: w_lo["k"][:, f, gs],
                                lambda f: xk_hi[:, f, :], lambda f: xk_lo[:, f, :]).then_inc(k_done, 1)
                    pe.wait_ge(xrl_done, c + 1)
                    for s in range(TPC):
                        pe.wait_ge(relu_done, c * TPC + s + 1)
                        by_token(s, xr_hi, xr_lo, "r").then_inc(r_done, 1)
                    if more:
                        transposes(c + 1)
                    pe.wait_ge(kal_done, c * FC + FC)
                    for s in range(TPC):
                        pe.wait_ge(gate_done, c * TPC + s + 1)
                        by_token(s, ka_hi, ka_lo, "v").then_inc(v_done, 1)

            pe.wait_ge(w_split_lo, 1)
            project(0)
            transposes(0)
            pe.wait_ge(w_split_lo, len(ORDER))
            chunks(pe, body)

        @block.scalar
        def _(act):
            def weights_high(k):
                act.wait_ge(w_loaded[k], 16)
                nc.scalar.copy(w_hi[k][:], staging[k][:]).then_inc(w_split_hi, 1)

            def o_high(c):
                act.wait_ge(o_div, c + 1)
                if not is_first(c):
                    act.wait_ge(wo_done, c * TPC)
                nc.scalar.copy(o_hi[:], o_in[:]).then_inc(oh_done, 1)

            def x_T(c, par, batch):
                for f in range(FC):
                    act.wait_ge(transposed, c * FC + f + 1)
                    if f == 0 and (type(c) is not int or c >= 2):
                        act.wait_ge(xr_done, c - 1)
                        if par == 0:
                            act.wait_ge(edge_done, batch)
                    nc.scalar.copy(xT[par][:, f, 1:CH + 1], ps_t[f][:, :]).then_inc(xT_done, 1)

            def highs(c):
                act.wait_ge(xk_done, c + 1)
                if not is_first(c):
                    act.wait_ge(k_done, c * FC)
                nc.scalar.copy(xk_hi[:], mixed[:]).then_inc(xkh_done, 1)
                act.wait_ge(xr_done, c + 1)
                if not is_first(c):
                    act.wait_ge(r_done, c * TPC)
                nc.scalar.copy(xr_hi[:], diff[:]).then_inc(xrh_done, 1)

            def body(i, last):
                for par in range(CPB):
                    c = i * CPB + par
                    more = not (last and par == CPB - 1)

                    def square_hi(g):
                        act.wait_ge(sq_done, c * FC + g + 1)
                        if g == 0 and not is_first(c):
                            act.wait_ge(v_done, c * TPC)
                        nc.scalar.copy(ka_hi[:, g, :], relu[:, g % RELU, :]).then_inc(kah_done, 1)

                    for g in range(FC):
                        act.wait_ge(k_done, c * FC + g + 1)
                        if g >= RELU or not is_first(c):
                            act.wait_ge(kal_done, c * FC + g + 1 - RELU)
                        nc.scalar.activation(relu[:, g % RELU, :], ps_p[g][:, :], ACT.Relu).then_inc(relu_done, 1)
                        if g >= 1:
                            square_hi(g - 1)
                    square_hi(FC - 1)
                    for s in range(TPC):
                        act.wait_ge(r_done, c * TPC + s + 1)
                        if s == 0 and not is_first(c):
                            act.wait_ge(out_stored, 16 * c)
                        nc.scalar.activation(gate[:, s, :], ps_p[s][:, :], ACT.Sigmoid).then_inc(gate_done, 1)
                    if more:
                        x_T(c + 1, 1 - par, i + par)
                        if not (last and par == CPB - 2):
                            o_high(c + 2)
                        highs(c + 1)

            weights_high("o")
            o_high(0)
            for k in ORDER[1:]:
                weights_high(k)
            x_T(0, 0, 0)
            o_high(1)
            highs(0)
            act.wait_ge(inv_stored, 32)
            chunks(act, body)

        @block.gpsimd
        def _(pool):
            nc.gpsimd.memset(xT[0][:, :, 0:1], 0.0).then_inc(zero_done, 1)
            nc.gpsimd.memset(minus_half[:], -0.5).then_inc(half_set, 1)
            pool.wait_ge(half_set, 1)
            pool.wait_ge(small_loaded, 16 * 3)

            def inv_std(c):
                pool.wait_ge(ln_step, c * 3 + 3)
                nc.gpsimd.tensor_tensor(rstd[:, :], rstd[:, :], minus_half[:, :], ALU.pow).then_inc(rstd_done, 1)

            def divide(c):
                pool.wait_ge(o_loaded, 16 * (c + 1))
                pool.wait_ge(inv_loaded, 16 * HG * (c + 1))
                nc.gpsimd.tensor_tensor(o_in[:], o_in[:], o_lo[:].bitcast(F32), ALU.mult).then_inc(o_div, 1)

            def o_low(c):
                pool.wait_ge(oh_done, c + 1)
                nc.gpsimd.tensor_tensor(o_lo[:], o_in[:], o_hi[:], ALU.subtract).then_inc(ol_done, 1)

            def add_bias(c, par, s):
                if s == 0:
                    pool.wait_ge(x_loaded, 16 * (c + 1))
                nc.gpsimd.tensor_tensor(xs[par][:, s, :], x_in[:, s, :], bo[:, :], ALU.add).then_inc(xb_done, 1)

            def edge(c):
                pool.wait_ge(xT_done, c * FC + FC)
                if not is_first(c):
                    pool.wait_ge(xr_done, c)
                pool.sem_inc(held, 1)
                nc.gpsimd.tensor_copy(xT[1][:, :, 0:1], xT[0][:, :, CH:CH + 1]).then_inc(edge_done, 1)

            def body(i, last):
                for par in range(CPB):
                    c = i * CPB + par
                    more = not (last and par == CPB - 1)
                    if more:
                        inv_std(c + 1)
                    for g in range(FC):
                        pool.wait_ge(relu_done, c * FC + g + 1)
                        nc.gpsimd.tensor_tensor(relu[:, g % RELU, :], relu[:, g % RELU, :], relu[:, g % RELU, :],
                                                ALU.mult).then_inc(sq_done, 1)
                    two_more = not last
                    if two_more:
                        divide(c + 2)
                    if more and par == 1:
                        edge(c + 1)
                    if two_more:
                        o_low(c + 2)
                    for s in range(TPC):
                        pool.wait_ge(gated, c * TPC + s + 1)
                        nc.gpsimd.tensor_tensor(gate[:, s, :], gate[:, s, :], xs[par][:, s, :], ALU.add).then_inc(out_done, 1)
                        if two_more:
                            pool.wait_ge(out_done, c * TPC + s + 1)
                            add_bias(c + 2, par, s)

            for s in range(TPC):
                add_bias(0, 0, s)
            inv_std(0)
            edge(0)
            divide(1)
            o_low(1)
            for s in range(TPC):
                add_bias(1, 1, s)
            chunks(pool, body)

        @block.vector
        def _(dve):
            def weights_low(n):
                k = ORDER[n]
                dve.wait_ge(w_split_hi, n + 1)
                nc.vector.tensor_tensor(w_lo[k][:], staging[k][:], w_hi[k][:], ALU.subtract).then_inc(w_split_lo, 1)

            def norm(c, par):
                x = xs[par]
                for s in range(TPC):
                    dve.wait_ge(xb_done, c * TPC + s + 1)
                    dve.wait_ge(wo_done, c * TPC + s + 1)
                    nc.vector.tensor_tensor(x[:, s, :], ps_p[s][:, :], x[:, s, :], ALU.add).then_inc(x1_done, 1)
                for s in range(TPC):
                    dve.wait_ge(x1_done, c * TPC + s + 1)
                    v = nc.vector.bn_stats(stats[:, s, :], x[:, s, :])
                v.then_inc(ln_step, 1)
                dve.wait_ge(ln_step, c * 3 + 1)
                dve.sem_inc(held, 1)
                for s in range(TPC):
                    v = nc.vector.bn_aggr(mv[:, s, :], stats[:, s, :])
                v.then_inc(ln_step, 1)
                dve.wait_ge(ln_step, c * 3 + 2)
                nc.vector.tensor_scalar(rstd[:, :], mv[:, :, 1], EPS, None, ALU.add).then_inc(ln_step, 1)
                dve.wait_ge(rstd_done, c + 1)
                if not is_first(c):
                    dve.wait_ge(transposed, c * FC)
                for s in range(TPC):
                    v = nc.vector.tensor_scalar(xn[:, s, :], x[:, s, :], mv[:, s, 0:1], rstd[:, s:s + 1],
                                                ALU.subtract, ALU.mult)
                v.then_inc(normed, 1)

            def shift(c, par, batch):
                dve.wait_ge(xT_done, c * FC + FC)
                if par == 0:
                    dve.wait_ge(zero_done, 1)
                else:
                    dve.wait_ge(edge_done, batch + 1)
                cur, prev = xT[par][:, :, 1:CH + 1], xT[par][:, :, 0:CH]
                nc.vector.tensor_tensor(diff[:], cur, prev, ALU.subtract).then_inc(diff_done, 1)
                dve.wait_ge(diff_done, c + 1)
                for f in range(FC):
                    v = nc.vector.scalar_tensor_tensor(mixed[:, f, :], diff[:, f, :], mu_k[:, f:f + 1], prev[:, f, :],
                                                       ALU.mult, ALU.add)
                v.then_inc(xk_done, 1)
                for f in range(FC):
                    v = nc.vector.scalar_tensor_tensor(diff[:, f, :], diff[:, f, :], mu_r[:, f:f + 1], prev[:, f, :],
                                                       ALU.mult, ALU.add)
                v.then_inc(xr_done, 1)

            def shift_low(c):
                dve.wait_ge(xkh_done, c + 1)
                nc.vector.tensor_tensor(xk_lo[:], mixed[:], xk_hi[:], ALU.subtract).then_inc(xkl_done, 1)
                dve.wait_ge(xrh_done, c + 1)
                nc.vector.tensor_tensor(xr_lo[:], diff[:], xr_hi[:], ALU.subtract).then_inc(xrl_done, 1)

            def body(i, last):
                for par in range(CPB):
                    c = i * CPB + par
                    more = not (last and par == CPB - 1)

                    def square_lo(g):
                        dve.wait_ge(kah_done, c * FC + g + 1)
                        nc.vector.tensor_tensor(ka_lo[:, g, :], relu[:, g % RELU, :], ka_hi[:, g, :],
                                                ALU.subtract).then_inc(kal_done, 1)

                    if more:
                        norm(c + 1, 1 - par)
                    for g in range(FC):
                        square_lo(g)
                    if more:
                        shift(c + 1, 1 - par, i if par == 0 else i + 1)
                    for s in range(TPC):
                        dve.wait_ge(v_done, c * TPC + s + 1)
                        nc.vector.tensor_tensor(gate[:, s, :], ps_p[s][:, :], gate[:, s, :], ALU.mult).then_inc(gated, 1)
                    if more:
                        shift_low(c + 1)

            dve.wait_ge(l_loaded, 16)
            nc.vector.reciprocal(inv[:, 0:1, :], sums[:, 0:1, :]).then_inc(inv_done, 1)
            weights_low(0)
            dve.wait_ge(o_loaded, 16)
            dve.wait_ge(inv_loaded, 16 * HG)
            nc.vector.tensor_tensor(o_in[:], o_in[:], o_lo[:].bitcast(F32), ALU.mult).then_inc(o_div, 1)
            dve.wait_ge(oh_done, 1)
            nc.vector.tensor_tensor(o_lo[:], o_in[:], o_hi[:], ALU.subtract).then_inc(ol_done, 1)
            dve.wait_ge(small_loaded, 16 * 3)
            dve.sem_inc(held, 1)
            for n in range(1, len(ORDER)):
                weights_low(n)
            norm(0, 0)
            nc.vector.reciprocal(inv[:, 1:B, :], sums[:, 1:B, :]).then_inc(inv_done, 1)
            shift(0, 0, 0)
            shift_low(0)
            chunks(dve, body)


def block_program(nc, x, wdqT, bdq, wuq, buq, wqr, bqr, wkr, bkr, wdkvT, bdkv, wuk, buk, wuv, buv, wo, bo,
                  wrT, wkT, wvT, mu_r, mu_k, cos, sin, ident, out):
    def scratch(name, shape, dt):
        return nc.dram_tensor(name, shape, dt, kind="Internal").ap()

    qk = [scratch(n, (B, FC, P, S), F32) for n in ("q_hi_scratch", "q_lo_scratch", "k_hi_scratch", "k_lo_scratch")]
    v_s = scratch("v_scratch", (B, FC, P, KT, P), F32)
    o_s = scratch("o_scratch", (NG, P, S), F32)
    l_s = scratch("l_scratch", (NG * HG, S), F32)
    inv_s = scratch("inv_scratch", (NG * HG, S), F32)
    with ExitStack() as ctx:
        def sem(name):
            return ctx.enter_context(nc.semaphore(name))

        held = sem("held")
        t = {"ident": ctx.enter_context(nc.sbuf_tensor("ident", [P, P], F32))}
        kept = ExitStack()

        def keep(name, shape, dt=F32):
            return kept.enter_context(nc.sbuf_tensor(name, shape, dt))

        att = {
            "q": [], "k": [], "v": [],
            "ones": keep("ones", [P, HD]),
            "ones_done": sem("ones_done"),
            "part_max": keep("part_max", [P, 2, 2, HG * QT]),
            "row_max": keep("row_max", [P, 2, HG * QT]),
            "neg_max": keep("neg_max", [HG * QT, 2, P], F32R),
            "loaded": [sem(f"stack_loaded{r}") for r in range(R3)],
            "v_loaded": [sem(f"vt_loaded{r}") for r in range(R3)],
            "m_scored": sem("m_scored"),
            "m_read": sem("m_read"),
            "m_rows": sem("m_rows"),
            "m_stacked": [sem(f"m_stacked{h}") for h in range(2)],
        }
        group_buffers(att, keep, 0)
        grouped = [d.rearrange("b g p t -> (b g) p t") for d in qk] + [v_s.rearrange("b g p k d -> (b g) p k d")]
        with ExitStack() as early:
            def sb(name, shape, dt=F32):
                return early.enter_context(nc.sbuf_tensor(name, shape, dt))

            t["cos"] = sb("cos", [2 * HD, S])
            t["sin"] = sb("sin", [2 * HD, S])
            t["bq"] = sb("bq", [P, FC])
            t["bk"] = sb("bk", [P, FC])
            t["br"] = sb("br", [2 * HD, 1])
            t["bv"] = sb("bv", [P, D])
            w = {k: sb("w_" + k, [P, FC, D if len(k) == 4 else P], F32R)
                 for k in ("q_hi", "q_lo", "k_hi", "k_lo", "v_hi", "v_lo", "rot_hi", "rot_lo")}
            x_in = [sb(f"x_in{i}", [P, TPC, D]) for i in range(CPB)]
            x_loaded = [sem(f"x_loaded{i}") for i in range(CPB)]
            x_v = x.rearrange("b (h s p) d -> b h p s d", h=CPB, p=P)

            def load_x(sp):
                for par in range(CPB):
                    sp.dma_start(x_in[par][:], x_v[0, par]).then_inc(x_loaded[par], 16)

            fold_block(nc, sem, t, w, att, (wdqT, wdkvT, wuq, wqr, wuk, wuv, wkr, bdq, bdkv, buq, bqr, buk, bkr, buv,
                                       cos, sin, ident), load_x)
            project_block(nc, sem, held, t, w, x_v, x_in, x_loaded, att, grouped, (*qk, v_s))
        attend_block(nc, sem, held, t, att, grouped, o_s, l_s.rearrange("(n a) t -> n a t", a=HG))
        kept.close()
        mix_block(nc, sem, held, t, x, o_s, l_s, inv_s, wo, wrT, wkT, wvT, bo, mu_r, mu_k, out)


def kernel(**inputs):
    import numpy as np
    import concourse.bacc as bacc
    from concourse.bass_utils import run_bass_kernel_spmd

    def given(name):
        return np.ascontiguousarray(inputs[name])

    def turned(name):
        return np.ascontiguousarray(np.asarray(inputs[name]).T)

    def columns(name):
        return np.ascontiguousarray(np.asarray(inputs[name]).reshape(-1, P).T)

    tiny = np.finfo(np.float32).tiny
    theta = np.power(np.float32(10000.0), np.float32(-2.0) * np.arange(D // 2, dtype=np.float32)) / np.float32(D // 2)
    theta[theta < tiny] = 0.0
    assert not theta[HD // 2:].any()
    angle = np.arange(S, dtype=np.float32)[None, :] * theta[:HD // 2, None]
    cos = np.repeat(np.cos(angle.astype(np.float64)), 2, axis=0).astype(np.float32)
    sin = np.repeat(np.sin(angle.astype(np.float64)), 2, axis=0).astype(np.float32)
    sin[0::2] *= -1.0
    cos, sin = (np.ascontiguousarray(np.tile(a, (2, 1))) for a in (cos, sin))

    a, f = "L0_attn_", "L0_ffn_"
    arrays = {
        "x": given(a + "x"), "wdqT": turned(a + "Wd_q_w"), "bdq": columns(a + "Wd_q_b"),
        "wuq": given(a + "Wu_q_w"), "buq": columns(a + "Wu_q_b"), "wqr": given(a + "Wq_r_w"), "bqr": columns(a + "Wq_r_b"),
        "wkr": given(a + "Wk_r_w"), "bkr": columns(a + "Wk_r_b"), "wdkvT": turned(a + "Wd_kv_w"),
        "bdkv": columns(a + "Wd_kv_b"), "wuk": given(a + "Wu_k_w"), "buk": columns(a + "Wu_k_b"),
        "wuv": given(a + "Wu_v_w"), "buv": given(a + "Wu_v_b"), "wo": given(a + "Wo_w"), "bo": given(a + "Wo_b"),
        "wrT": turned(f + "W_r"), "wkT": turned(f + "W_k"), "wvT": turned(f + "W_v"),
        "mu_r": columns(f + "mu_r"), "mu_k": columns(f + "mu_k"),
        "cos": cos, "sin": sin, "ident": np.eye(P, dtype=np.float32),
    }
    nc = bacc.Bacc("TRN2", target_bir_lowering=False, num_devices=1)
    args = [nc.dram_tensor(f"in_{k}", v.shape, mybir.dt.from_np(v.dtype), kind="ExternalInput").ap()
            for k, v in arrays.items()]
    out = nc.dram_tensor("out", (B, S, D), F32, kind="ExternalOutput").ap()
    block_program(nc, *args, out)
    got = run_bass_kernel_spmd(nc, [{f"in_{k}": v for k, v in arrays.items()}], core_ids=[0])
    return got.results[0]["out"]
```
